# Optimizing a Trainium2 kernel written in Bass

```python
import numpy as np
import jax
import jax.numpy as jnp

def _softmax(x, axis=-1):
    return jax.nn.softmax(x, axis=axis)

def _gelu(x):
    return jax.nn.gelu(x, approximate=True)

def _silu(x):
    return jax.nn.silu(x)

def _sigmoid(x):
    return jax.nn.sigmoid(x)

def _layernorm(x, axis=-1, eps=1e-05):
    m = jnp.mean(x, axis=axis, keepdims=True)
    v = jnp.var(x, axis=axis, keepdims=True)
    return (x - m) / jnp.sqrt(v + eps)

def _scatter_add(tgt, idx, src, axis=0):
    return tgt.at[idx].add(src)

def _segment_sum(src, seg, n):
    return jax.ops.segment_sum(src, seg, n)
kernel_name = 'mk_metaformer_d1_conv_nchw256_r2_a0c168'

def setup_inputs(seed: int=0):
    np.random.seed(seed)
    _w = jnp.asarray

    def _rec_inputs():
        import jax
        import jax.numpy as jnp
        _gk = jax.random.key(seed)
        x = -0.000125 + 0.9999 * jax.random.normal(jax.random.fold_in(_gk, 1), (64, 128, 32, 32), jnp.float32)
        return x
    x = _rec_inputs()

    def _L0_conv_setup():
        import jax, jax.numpy as jnp
        import numpy as np
        from jax import lax
        B, C, H, W, KS = (64, 128, 32, 32, 3)

        def _binact(x):
            p = jnp.where(x < -1.0, -1.0, jnp.where(x < 0.0, x * x + 2.0 * x, jnp.where(x < 1.0, -x * x + 2.0 * x, 1.0)))
            return lax.stop_gradient(jnp.sign(x) - p) + p

        def _binweight(w):
            scale = lax.stop_gradient(jnp.mean(jnp.abs(w), axis=(1, 2, 3), keepdims=True))
            cw = jnp.clip(w, -1.0, 1.0)
            return lax.stop_gradient(jnp.sign(w) * scale - cw) + cw

        def _conv(x, w, stride, groups):
            p = w.shape[-1] // 2
            return lax.conv_general_dilated(x, w, (stride, stride), [(p, p), (p, p)], dimension_numbers=('NCHW', 'OIHW', 'NCHW'), feature_group_count=groups)

        def _bn(x, g, b, m, v, eps=1e-05):
            inv = (g / jnp.sqrt(v + eps))[None, :, None, None]
            return (x - m[None, :, None, None]) * inv + b[None, :, None, None]

        def _cb(b):
            return b[None, :, None, None]
        key = jax.random.key(seed)
        k = jax.random.split(key, 24)
        rn = lambda i, s, sc=1.0: jax.random.normal(k[i], s, jnp.float32) * sc
        return {'x': rn(0, (B, C, H, W)), 'loss': jnp.zeros((), jnp.float32), 'w1': rn(1, (C, C, KS, KS), 0.1), 'w2': rn(2, (C, C, 1, 1), 0.1), 'b11': rn(3, (C,), 0.02), 'b12': rn(4, (C,), 0.02), 'b13': rn(5, (C,), 0.02), 'b21': rn(6, (C,), 0.02), 'b22': rn(7, (C,), 0.02), 'b23': rn(8, (C,), 0.02), 'a1': 0.25 + rn(9, (C,), 0.01), 'a2': 0.25 + rn(10, (C,), 0.01), 'g1m': 1.0 + rn(11, (C,), 0.05), 'be1m': rn(12, (C,), 0.05), 'm1m': rn(13, (C,), 0.05), 'v1m': jax.random.uniform(k[14], (C,), jnp.float32, 0.5, 1.5), 'g2m': 1.0 + rn(15, (C,), 0.05), 'be2m': rn(16, (C,), 0.05), 'm2m': rn(17, (C,), 0.05), 'v2m': jax.random.uniform(k[18], (C,), jnp.float32, 0.5, 1.5), 'ch': 128, 'ksz': 3, 'gr1': 1, 'gr2': 1}
    _L0_conv_all = _L0_conv_setup()
    _L0_conv_in = {k: v for k, v in _L0_conv_all.items() if k in ('loss', 'w1', 'w2', 'b11', 'b12', 'b13', 'b21', 'b22', 'b23', 'a1', 'a2', 'g1m', 'be1m', 'm1m', 'v1m', 'g2m', 'be2m', 'm2m', 'v2m')}
    del _L0_conv_all

    def _L0_ffn_setup():
        import jax, jax.numpy as jnp
        import numpy as np
        B, N, D = (16, 2048, 128)
        NUM_EXPERTS, TOP_K, HEADS = (4, 2, 4)
        N_EDGES = 524288
        LN_EPS = 1e-05

        def _layernorm(x, g, b):
            mu = x.mean(-1, keepdims=True)
            var = ((x - mu) ** 2).mean(-1, keepdims=True)
            return (x - mu) * jax.lax.rsqrt(var + LN_EPS) * g + b

        def _forward(x, edge_index, W_gat, att_src, att_dst, b_gat, ln_gamma, ln_beta, W1, b1, W2, b2):
            Bc, Nc, Dc = x.shape
            M = Bc * Nc
            x_flat = x.reshape(M, Dc)
            h = (x_flat @ W_gat).reshape(M, HEADS, NUM_EXPERTS)
            loops = jnp.arange(M, dtype=edge_index.dtype)
            src = jnp.concatenate([edge_index[0], loops])
            dst = jnp.concatenate([edge_index[1], loops])
            a_src = (h * att_src).sum(-1)
            a_dst = (h * att_dst).sum(-1)
            e = jax.nn.leaky_relu(a_src[src] + a_dst[dst], negative_slope=0.2)
            e_max = jax.ops.segment_max(e, dst, num_segments=M)
            ee = jnp.exp(e - e_max[dst])
            denom = jax.ops.segment_sum(ee, dst, num_segments=M)
            alpha = ee / (denom[dst] + 1e-16)
            msg = h[src] * alpha[:, :, None]
            agg = jax.ops.segment_sum(msg, dst, num_segments=M).reshape(M, HEADS * NUM_EXPERTS) + b_gat
            scores = _layernorm(agg, ln_gamma, ln_beta).reshape(M, HEADS, NUM_EXPERTS).mean(1)
            scores = scores.reshape(Bc, Nc, NUM_EXPERTS)
            topk_s, topk_i = jax.lax.top_k(scores, TOP_K)
            w = jax.nn.softmax(topk_s, axis=-1)
            out = jnp.zeros_like(x)
            for ei in range(NUM_EXPERTS):
                g = jnp.where(topk_i == ei, w, 0.0).sum(-1)
                hh = jax.nn.gelu(x @ W1[ei] + b1[ei], approximate=False)
                out = out + g[..., None] * (hh @ W2[ei] + b2[ei])
            return out
        key = jax.random.key(seed)
        ks = jax.random.split(key, 8)
        s = 0.05
        return {'x': jax.random.normal(ks[0], (B, N, D), jnp.float32), 'W_gat': jax.random.normal(ks[1], (D, HEADS * NUM_EXPERTS), jnp.float32) * s, 'att_src': jax.random.normal(ks[2], (HEADS, NUM_EXPERTS), jnp.float32) * s, 'att_dst': jax.random.normal(ks[3], (HEADS, NUM_EXPERTS), jnp.float32) * s, 'b_gat': jnp.zeros((HEADS * NUM_EXPERTS,), jnp.float32), 'ln_gamma': jnp.ones((HEADS * NUM_EXPERTS,), jnp.float32), 'ln_beta': jnp.zeros((HEADS * NUM_EXPERTS,), jnp.float32), 'W1': jax.random.normal(ks[4], (NUM_EXPERTS, D, 2 * D), jnp.float32) * s, 'b1': jnp.zeros((NUM_EXPERTS, 2 * D), jnp.float32), 'W2': jax.random.normal(ks[5], (NUM_EXPERTS, 2 * D, D), jnp.float32) * s, 'b2': jnp.zeros((NUM_EXPERTS, D), jnp.float32), 'edge_index': jax.random.randint(ks[6], (2, N_EDGES), 0, B * N, jnp.int32)}
    _L0_ffn_all = _L0_ffn_setup()
    _L0_ffn_in = {k: v for k, v in _L0_ffn_all.items() if k in ('W_gat', 'att_src', 'att_dst', 'b_gat', 'ln_gamma', 'ln_beta', 'W1', 'b1', 'W2', 'b2', 'edge_index')}
    del _L0_ffn_all
    return {'x': x, 'L0_conv_loss': _L0_conv_in['loss'], 'L0_conv_w1': _L0_conv_in['w1'], 'L0_conv_w2': _L0_conv_in['w2'], 'L0_conv_b11': _L0_conv_in['b11'], 'L0_conv_b12': _L0_conv_in['b12'], 'L0_conv_b13': _L0_conv_in['b13'], 'L0_conv_b21': _L0_conv_in['b21'], 'L0_conv_b22': _L0_conv_in['b22'], 'L0_conv_b23': _L0_conv_in['b23'], 'L0_conv_a1': _L0_conv_in['a1'], 'L0_conv_a2': _L0_conv_in['a2'], 'L0_conv_g1m': _L0_conv_in['g1m'], 'L0_conv_be1m': _L0_conv_in['be1m'], 'L0_conv_m1m': _L0_conv_in['m1m'], 'L0_conv_v1m': _L0_conv_in['v1m'], 'L0_conv_g2m': _L0_conv_in['g2m'], 'L0_conv_be2m': _L0_conv_in['be2m'], 'L0_conv_m2m': _L0_conv_in['m2m'], 'L0_conv_v2m': _L0_conv_in['v2m'], 'L0_ffn_W_gat': _L0_ffn_in['W_gat'], 'L0_ffn_att_src': _L0_ffn_in['att_src'], 'L0_ffn_att_dst': _L0_ffn_in['att_dst'], 'L0_ffn_b_gat': _L0_ffn_in['b_gat'], 'L0_ffn_ln_gamma': _L0_ffn_in['ln_gamma'], 'L0_ffn_ln_beta': _L0_ffn_in['ln_beta'], 'L0_ffn_W1': _L0_ffn_in['W1'], 'L0_ffn_b1': _L0_ffn_in['b1'], 'L0_ffn_W2': _L0_ffn_in['W2'], 'L0_ffn_b2': _L0_ffn_in['b2'], 'L0_ffn_edge_index': _L0_ffn_in['edge_index']}

def reference(x, L0_conv_loss, L0_conv_w1, L0_conv_w2, L0_conv_b11, L0_conv_b12, L0_conv_b13, L0_conv_b21, L0_conv_b22, L0_conv_b23, L0_conv_a1, L0_conv_a2, L0_conv_g1m, L0_conv_be1m, L0_conv_m1m, L0_conv_v1m, L0_conv_g2m, L0_conv_be2m, L0_conv_m2m, L0_conv_v2m, L0_ffn_W_gat, L0_ffn_att_src, L0_ffn_att_dst, L0_ffn_b_gat, L0_ffn_ln_gamma, L0_ffn_ln_beta, L0_ffn_W1, L0_ffn_b1, L0_ffn_W2, L0_ffn_b2, L0_ffn_edge_index):
    import jax
    import jax.numpy as jnp

    def _L0_conv_ref(x, loss, w1, w2, b11, b12, b13, b21, b22, b23, a1, a2, g1m, be1m, m1m, v1m, g2m, be2m, m2m, v2m, ch, ksz, gr1, gr2):
        import jax, jax.numpy as jnp
        import numpy as np
        from jax import lax
        B, C, H, W, KS = (64, 128, 32, 32, 3)

        def _binact(x):
            p = jnp.where(x < -1.0, -1.0, jnp.where(x < 0.0, x * x + 2.0 * x, jnp.where(x < 1.0, -x * x + 2.0 * x, 1.0)))
            return lax.stop_gradient(jnp.sign(x) - p) + p

        def _binweight(w):
            scale = lax.stop_gradient(jnp.mean(jnp.abs(w), axis=(1, 2, 3), keepdims=True))
            cw = jnp.clip(w, -1.0, 1.0)
            return lax.stop_gradient(jnp.sign(w) * scale - cw) + cw

        def _conv(x, w, stride, groups):
            p = w.shape[-1] // 2
            return lax.conv_general_dilated(x, w, (stride, stride), [(p, p), (p, p)], dimension_numbers=('NCHW', 'OIHW', 'NCHW'), feature_group_count=groups)

        def _bn(x, g, b, m, v, eps=1e-05):
            inv = (g / jnp.sqrt(v + eps))[None, :, None, None]
            return (x - m[None, :, None, None]) * inv + b[None, :, None, None]

        def _cb(b):
            return b[None, :, None, None]
        out1 = _binact(x + _cb(b11))
        out1 = _conv(out1, _binweight(w1), 1, gr1)
        out1 = _bn(out1, g1m, be1m, m1m, v1m)
        out1 = out1 + x
        out1 = out1 + _cb(b12)
        out1 = jnp.where(out1 > 0, out1, _cb(a1) * out1)
        out1 = out1 + _cb(b13)
        out2 = _binact(out1 + _cb(b21))
        out2 = _conv(out2, _binweight(w2), 1, gr2)
        out2 = _bn(out2, g2m, be2m, m2m, v2m)
        out2 = out2 + out1
        out2 = out2 + _cb(b22)
        out2 = jnp.where(out2 > 0, out2, _cb(a2) * out2)
        out2 = out2 + _cb(b23)
        return out2

    def _L0_ffn_ref(x, W_gat, att_src, att_dst, b_gat, ln_gamma, ln_beta, W1, b1, W2, b2, edge_index):
        import jax, jax.numpy as jnp
        import numpy as np
        B, N, D = (16, 2048, 128)
        NUM_EXPERTS, TOP_K, HEADS = (4, 2, 4)
        N_EDGES = 524288
        LN_EPS = 1e-05

        def _layernorm(x, g, b):
            mu = x.mean(-1, keepdims=True)
            var = ((x - mu) ** 2).mean(-1, keepdims=True)
            return (x - mu) * jax.lax.rsqrt(var + LN_EPS) * g + b

        def _forward(x, edge_index, W_gat, att_src, att_dst, b_gat, ln_gamma, ln_beta, W1, b1, W2, b2):
            Bc, Nc, Dc = x.shape
            M = Bc * Nc
            x_flat = x.reshape(M, Dc)
            h = (x_flat @ W_gat).reshape(M, HEADS, NUM_EXPERTS)
            loops = jnp.arange(M, dtype=edge_index.dtype)
            src = jnp.concatenate([edge_index[0], loops])
            dst = jnp.concatenate([edge_index[1], loops])
            a_src = (h * att_src).sum(-1)
            a_dst = (h * att_dst).sum(-1)
            e = jax.nn.leaky_relu(a_src[src] + a_dst[dst], negative_slope=0.2)
            e_max = jax.ops.segment_max(e, dst, num_segments=M)
            ee = jnp.exp(e - e_max[dst])
            denom = jax.ops.segment_sum(ee, dst, num_segments=M)
            alpha = ee / (denom[dst] + 1e-16)
            msg = h[src] * alpha[:, :, None]
            agg = jax.ops.segment_sum(msg, dst, num_segments=M).reshape(M, HEADS * NUM_EXPERTS) + b_gat
            scores = _layernorm(agg, ln_gamma, ln_beta).reshape(M, HEADS, NUM_EXPERTS).mean(1)
            scores = scores.reshape(Bc, Nc, NUM_EXPERTS)
            topk_s, topk_i = jax.lax.top_k(scores, TOP_K)
            w = jax.nn.softmax(topk_s, axis=-1)
            out = jnp.zeros_like(x)
            for ei in range(NUM_EXPERTS):
                g = jnp.where(topk_i == ei, w, 0.0).sum(-1)
                hh = jax.nn.gelu(x @ W1[ei] + b1[ei], approximate=False)
                out = out + g[..., None] * (hh @ W2[ei] + b2[ei])
            return out
        return _forward(x, edge_index, W_gat, att_src, att_dst, b_gat, ln_gamma, ln_beta, W1, b1, W2, b2)

    def _gn(v, G=32, eps=1e-05):
        B_, C_, H_, W_ = v.shape
        g = v.reshape(B_, G, C_ // G, H_, W_)
        m = jnp.mean(g, axis=(2, 3, 4), keepdims=True)
        s = jnp.var(g, axis=(2, 3, 4), keepdims=True)
        return ((g - m) / jnp.sqrt(s + eps)).reshape(v.shape)

    def _ln_c(v, eps=1e-06):
        m = jnp.mean(v, axis=1, keepdims=True)
        s = jnp.var(v, axis=1, keepdims=True)
        return (v - m) / jnp.sqrt(s + eps)

    def _ln_t(v, eps=1e-05):
        m = jnp.mean(v, axis=-1, keepdims=True)
        s = jnp.var(v, axis=-1, keepdims=True)
        return (v - m) / jnp.sqrt(s + eps)

    def _to_tokens(v):
        B_, C_, H_, W_ = v.shape
        return v.reshape(B_, C_, H_ * W_).transpose(0, 2, 1)

    def _from_tokens(t, like):
        B_, C_, H_, W_ = like.shape
        return t.transpose(0, 2, 1).reshape(B_, C_, H_, W_)
    x = x + _L0_conv_ref(_ln_c(x), L0_conv_loss, L0_conv_w1, L0_conv_w2, L0_conv_b11, L0_conv_b12, L0_conv_b13, L0_conv_b21, L0_conv_b22, L0_conv_b23, L0_conv_a1, L0_conv_a2, L0_conv_g1m, L0_conv_be1m, L0_conv_m1m, L0_conv_v1m, L0_conv_g2m, L0_conv_be2m, L0_conv_m2m, L0_conv_v2m, 128, 3, 1, 1)
    t = _to_tokens(x)
    t = t + _L0_ffn_ref(_ln_t(t), L0_ffn_W_gat, L0_ffn_att_src, L0_ffn_att_dst, L0_ffn_b_gat, L0_ffn_ln_gamma, L0_ffn_ln_beta, L0_ffn_W1, L0_ffn_b1, L0_ffn_W2, L0_ffn_b2, L0_ffn_edge_index)
    x = _from_tokens(t, x)
    return x

_drawn_inputs = setup_inputs


def setup_inputs(seed=0):
    import zlib

    import numpy as np

    out = dict(_drawn_inputs(seed))
    spreads = {'L0_ffn_b_gat': (0.0, 0.517),
     'L0_ffn_ln_gamma': (1.0, 0.6),
     'L0_ffn_ln_beta': (0.0, 2.0),
     'L0_ffn_b1': (0.0, 1.802),
     'L0_ffn_b2': (0.0, 0.973)}
    factors = {'L0_conv_b22': 6.459,
     'L0_conv_b23': 22.571,
     'L0_conv_a1': 5.883,
     'L0_conv_a2': 8.0,
     'L0_conv_g2m': 3.526,
     'L0_conv_be2m': 3.146,
     'L0_conv_m2m': 3.052,
     'L0_ffn_att_src': 100.19,
     'L0_ffn_att_dst': 200.0}
    for name, (base, spread) in spreads.items():
        noise = np.random.default_rng([zlib.crc32(name.encode()), seed]).standard_normal(out[name].shape)
        drawn = base * np.exp(spread * noise) if base else spread * noise
        out[name] = jnp.asarray(drawn.astype(out[name].dtype))
    for name, factor in factors.items():
        out[name] = (out[name] * factor).astype(out[name].dtype)
    return out
```

```python
from contextlib import ExitStack, contextmanager

import concourse.bass as bass
from concourse import mybir

F32 = mybir.dt.float32
I32 = mybir.dt.int32
BF16 = mybir.dt.bfloat16
ALU = mybir.AluOpType
ACT = mybir.ActivationFunctionType
AX = mybir.AxisListType

P = 128
EDGES = 524288
HALF = 32768
HEADS, EXPERTS = 4, 4

EDGE_COLS = EDGES // P
PART_BITS, COL_BITS = 7, 12
TURN_CHUNKS = 4
HEAD_COLS = HALF // P
LEAST = 128
SHIFT = HALF // 2 - LEAST
FLIP = 2 * SHIFT

ENTRIES = EDGES + HALF
RUN = ENTRIES // P
TAIL = RUN
CHUNKS = 64
COLS = RUN // CHUNKS
ROW = 24
BIG = 1e30
HIS = HALF // P
COUNT_TILES = EDGE_COLS // CHUNKS
RING = 8

HID = 2
PARTS = 3
G = PARTS * PARTS * EXPERTS
TOK = 512
BLKS = TOK // P
TOKEN_TILES = HALF // TOK


def need(eng, sem, count):
    if isinstance(count, int) and count <= 0:
        return
    eng.wait_ge(sem, count)

def rounds(eng, first, last, tail, unroll, body):
    turns = (last - first - tail) // unroll
    for k in range(first):
        body(k, k, 0)
    with eng.Fori(0, turns) as turn:
        for at in range(first, first + unroll):
            body(turn * unroll + at, at, turn)
    for k in range(first + turns * unroll, last):
        body(k, k, 0)

@contextmanager
def semaphores(nc, prefix, names):
    with ExitStack() as stack:
        signals = {n: stack.enter_context(nc.semaphore(f"{prefix}_{n}")) for n in names.split()}
        yield signals
        with nc.Block() as block:
            @block.gpsimd
            def _(pool):
                for s in signals.values():
                    pool.sem_clear(s)

def mixer(nc, io, tables):
    x, w1, w2 = io["x"], io["w1"], io["w2"]
    IMAGES, C, H, W = x.shape
    PIX = H * W
    BLK = PIX // P
    HALVES = PIX // 512
    TAPS = 9
    ROW = tables["ROW"]
    PADW = W + 2
    x_d = x.rearrange("b c h w -> b c (h w)")
    xmid_d, norm_d, rows_d, agg = tables["xmid"], tables["norm"], tables["rows"], tables["agg"]
    with ExitStack() as ctx:
        def sb(name, shape, dt=F32): return ctx.enter_context(nc.sbuf_tensor(name, shape, dt))
        def ps(name, shape, dt=F32): return ctx.enter_context(nc.psum_tensor(name, shape, dt))
        def sem(name): return ctx.enter_context(nc.semaphore(name))
        NAMES = ["b11","b12","b13","b21","b22","b23","a1","a2","g1m","be1m","m1m","v1m","g2m","be2m","m2m","v2m"]
        par = sb("par", [P, len(NAMES)])
        col = {n: par[:, i:i+1] for i, n in enumerate(NAMES)}
        der = sb("der", [P, 16])
        eps = sb("eps", [P, 4])
        w1f = sb("w1f", [P, C*TAPS]); w2f = sb("w2f", [P, C])
        w1s = sb("w1s", [P, TAPS, C], BF16); w2s = sb("w2s", [P, C], BF16)
        w1T = sb("w1T", [P, TAPS, C], BF16); w2T = sb("w2T", [P, C], BF16)
        wabs = sb("wabs", [P, C*TAPS])
        identb = sb("identb", [P, P], BF16); ident = sb("ident", [P, P])
        wg = sb("wg", [P, ROW]); att = sb("att", [P, 32]); wtmp = sb("wtmp", [P, 32])
        NX = 4
        xin = sb("xin", [P, NX, PIX])
        stats = sb("stats", [P, BLK, 6]); mv1 = sb("mv1", [P, BLK, 2]); mv2 = sb("mv2", [P, BLK, 2]); stats2 = sb("stats2", [P, BLK, 6])
        sd1 = sb("sd1", [P, BLK]); rs1 = sb("rs1", [P, BLK]); nb1 = sb("nb1", [P, BLK])
        sd2 = sb("sd2", [P, BLK]); rs2 = sb("rs2", [P, BLK]); nb2 = sb("nb2", [P, BLK])
        xn = sb("xn", [P, 2, PIX]); xt1 = sb("xt1", [P, PIX]); xt2 = sb("xt2", [P, PIX])
        sg1 = sb("sg1", [P, 2, PADW, PADW], BF16); sg2 = sb("sg2", [P, PIX], BF16)
        z1 = sb("z1", [P, PIX]); lin1 = sb("lin1", [P, PIX]); pos1 = sb("pos1", [P, PIX]); out1 = sb("out1", [P, PIX])
        z2 = sb("z2", [P, PIX]); lin2 = sb("lin2", [P, PIX]); pos2 = sb("pos2", [P, PIX]); out2 = sb("out2", [P, PIX])
        xm = sb("xm", [P, 2, PIX]); tn = sb("tn", [P, 2, PIX]); rw = sb("rw", [P, 2, BLK, ROW])
        ln1_ps = ps("ln1_ps", [P, 2, PIX]); conv_ps = ps("conv_ps", [P, PIX]); ln2_ps = ps("ln2_ps", [P, PIX])
        S = ctx.enter_context(semaphores(nc, "m", "par w params const ident dp sdv wsg wT x0 x1 x2 x3 xT1 st1 bn1 sd1 rc1 rs1 xt1 xn1 xn sg1 conv z1 lin1 pos1 out1 sg2 "
             "conv2 z2 lin2 pos2 out2 xm xT2 st2 bn2 sd2 rc2 rs2 xt2 xnT2 tn rows rw stx0 stx1 stt0 stt1 str0 str1 hold"))
        block = ctx.enter_context(nc.Block())
        LAST = IMAGES + 2
        def front(k): return not isinstance(k, int) or k < IMAGES
        def middle(k): return not isinstance(k, int) or 1 <= k <= IMAGES
        def back(k): return not isinstance(k, int) or k >= 2

        @block.sync
        def _(sp):
            for i, n in enumerate(NAMES):
                sp.dma_start(col[n], io[n].rearrange("(p a) -> p a", a=1)).then_inc(S["par"], 16)
            sp.dma_start(w1f[:, :], w1.rearrange("o i a b -> o (i a b)")).then_inc(S["w"], 16)
            sp.dma_start(w2f[:, :], w2.rearrange("o i a b -> o (i a b)")).then_inc(S["w"], 16)
            sp.dma_start(wg[:, 0:16], io["W_gat"]).then_inc(S["w"], 16)
            sp.dma_start(att[:, 0:16], io["att_src"].rearrange("(a h) e -> a (h e)", a=1).broadcast_to([P, 16])).then_inc(S["w"], 16)
            sp.dma_start(att[:, 16:32], io["att_dst"].rearrange("(a h) e -> a (h e)", a=1).broadcast_to([P, 16])).then_inc(S["w"], 16)
            for k in range(2):
                sp.dma_start(xin[:, k, :], x_d[k, :, :]).then_inc(S["x%d" % k], 16)

            def body(k, at, turn):
                if not isinstance(k, int) or k + 2 < IMAGES:
                    need(sp, S["xm"], k - 1)
                    u = (at + 2) % NX
                    sp.dma_start(xin[:, u, :], x_d[k + 2, :, :]).then_inc(S["x%d" % u], 16)
                if middle(k):
                    q = (at - 1) % 2
                    need(sp, S["xm"], k)
                    sp.dma_start(xmid_d[k - 1, :, :], xm[:, q, :]).then_inc(S["stx%d" % q], 16)
                if back(k):
                    q = at % 2
                    need(sp, S["tn"], k - 1)
                    sp.dma_start(norm_d[k - 2, :, :], tn[:, q, :]).then_inc(S["stt%d" % q], 16)
                    need(sp, S["rw"], k - 1)
                    sp.dma_start(rows_d[k - 2], rw[:, q, :, :]).then_inc(S["str%d" % q], 16)
            rounds(sp, 6, LAST, 4, 4, body)
            for n in ("stx", "stt", "str"):
                for q in range(2):
                    sp.wait_ge(S[n + str(q)], 16 * IMAGES // 2)

        @block.gpsimd
        def _(pool):
            pool.memset(identb[:, :], 0.0)
            pool.memset(ident[:, :], 0.0)
            pool.memset(sg1[:, :, :, :], 0.0)
            pool.memset(eps[:, 0:1], 1e-6)
            pool.memset(eps[:, 1:2], 1e-5).then_inc(S["const"], 1)
            pool.wait_ge(S["const"], 1)
            for m in (identb, ident):
                last = pool.affine_select(out=m[:, :], in_=m[:, :], compare_op=ALU.not_equal, fill=1.0, base=0,
                                          pattern=[[-1, P]], channel_multiplier=1)
            last.then_inc(S["ident"], 1)

            def body(k, at, turn):
                if middle(k):
                    q = (at - 1) % 2
                    need(pool, S["out2"], k)
                    need(pool, S["xT2"], k - 2)
                    need(pool, S["stx%d" % q], 16 * ((at - 1) // 2) + 32 * turn)
                    pool.tensor_tensor(xm[:, q, :], out2[:, :], xin[:, (at - 1) % NX, :], ALU.add).then_inc(S["xm"], 1)
            rounds(pool, 6, LAST, 4, 4, body)

        @block.tensor
        def _(pe):
            pe.wait_ge(S["ident"], 1)
            pe.wait_ge(S["wsg"], 2)
            wps = conv_ps[:, :].bitcast(BF16)
            for t in range(TAPS + 1):
                src = w1s[:, t, :] if t < TAPS else w2s[:, :]
                last = pe.transpose(wps[:, t*P:(t+1)*P], src, identb[:, :])
            last.then_inc(S["wT"], 1)
            pe.wait_ge(S["wT"], 3)

            def body(k, at, turn):
                if front(k):
                    u = at % NX
                    pe.wait_ge(S["x%d" % u], 16 * (at // NX + 1) + 16 * turn)
                    need(pe, S["z1"], k - 1)
                    need(pe, S["xn"], k - 1)
                    for j in range(BLK):
                        last = pe.transpose(ln1_ps[:, at % 2, j*P:(j+1)*P], xin[:, u, j*P:(j+1)*P], ident[:, :])
                    last.then_inc(S["xT1"], 1)
                if middle(k):
                    need(pe, S["sg1"], k)
                    need(pe, S["z2"], k - 1)
                    rows_of = H // HALVES
                    for hf in range(HALVES):
                        for t in range(TAPS):
                            dy, dx = t // 3, t % 3
                            last = pe.matmul(conv_ps[:, hf*512:(hf+1)*512], w1T[:, t, :],
                                             sg1[:, (at - 1) % 2, hf*rows_of+dy:hf*rows_of+dy+rows_of, dx:dx+W],
                                             start=(t == 0), stop=(t == TAPS - 1))
                    last.then_inc(S["conv"], 1)
                if back(k):
                    need(pe, S["xm"], k - 1)
                    need(pe, S["rw"], k - 2)
                    for j in range(BLK):
                        last = pe.transpose(ln2_ps[:, j*P:(j+1)*P], xm[:, at % 2, j*P:(j+1)*P], ident[:, :])
                    last.then_inc(S["xT2"], 1)
                if front(k):
                    need(pe, S["xt1"], k + 1)
                    for j in range(BLK):
                        last = pe.transpose(ln1_ps[:, at % 2, j*P:(j+1)*P], xt1[:, j*P:(j+1)*P], ident[:, :])
                    last.then_inc(S["xn1"], 1)
                if middle(k):
                    need(pe, S["sg2"], k)
                    need(pe, S["z1"], k)
                    for hf in range(HALVES):
                        last = pe.matmul(conv_ps[:, hf*512:(hf+1)*512], w2T[:, :], sg2[:, hf*512:(hf+1)*512], start=True, stop=True)
                    last.then_inc(S["conv2"], 1)
                if back(k):
                    need(pe, S["xt2"], k - 1)
                    for j in range(BLK):
                        last = pe.transpose(ln2_ps[:, j*P:(j+1)*P], xt2[:, j*P:(j+1)*P], ident[:, :])
                    last.then_inc(S["xnT2"], 1)
                    need(pe, S["tn"], k - 1)
                    for j in range(BLK):
                        last = pe.matmul(ln2_ps[:, j*ROW:(j+1)*ROW], tn[:, at % 2, j*P:(j+1)*P], wg[:, :], start=True, stop=True)
                    last.then_inc(S["rows"], 1)
            rounds(pe, 6, LAST, 4, 4, body)

        @block.vector
        def _(v):
            n = [0]
            def go(i):
                n[0] += 1
                i.then_inc(S["dp"], 1)
                v.wait_ge(S["dp"], n[0])
            v.wait_ge(S["par"], 16 * len(NAMES))
            v.wait_ge(S["w"], 80)
            go(v.scalar_tensor_tensor(out=wabs[:, :], in0=w1f[:, :], scalar=-1.0, in1=w1f[:, :], op0=ALU.mult, op1=ALU.max))
            go(v.reduce_sum(der[:, 0:1], wabs[:, :], axis=AX.X))
            go(v.scalar_tensor_tensor(out=wabs[:, 0:C], in0=w2f[:, :], scalar=-1.0, in1=w2f[:, :], op0=ALU.mult, op1=ALU.max))
            go(v.reduce_sum(der[:, 1:2], wabs[:, 0:C], axis=AX.X))
            v.wait_ge(S["sdv"], 2)
            go(v.reciprocal(der[:, 4:6], der[:, 2:4]))
            for s, (g, m, be, b2, a, b3) in enumerate((("g1m","m1m","be1m","b12","a1","b13"), ("g2m","m2m","be2m","b22","a2","b23"))):
                inv, kk, cc, ll, oma = (der[:, o+s:o+s+1] for o in (4, 6, 8, 10, 12))
                go(v.tensor_tensor(inv, inv, col[g], ALU.mult))
                go(v.tensor_scalar(kk, der[:, s:s+1], 1.0 / (C * (TAPS if s == 0 else 1)), inv, ALU.mult, ALU.mult))
                go(v.tensor_tensor(cc, col[m], inv, ALU.mult))
                go(v.tensor_tensor(cc, col[be], cc, ALU.subtract))
                go(v.tensor_tensor(cc, cc, col[b2], ALU.add))
                go(v.scalar_tensor_tensor(out=ll, in0=cc, scalar=col[a], in1=col[b3], op0=ALU.mult, op1=ALU.add))
                go(v.tensor_scalar(oma, col[a], -1.0, 1.0, ALU.mult, ALU.add))
            for s in range(2):
                go(v.tensor_tensor(wtmp[:, 0:16], wg[:, 0:16], att[:, 16*s:16*s+16], ALU.mult))
                go(v.reduce_sum(wg[:, 16+4*s:20+4*s], wtmp[:, 0:16].rearrange("p (h e) -> p h e", e=4), axis=AX.X))
            v.wait_ge(S["wT"], 1)
            wps = conv_ps[:, :].bitcast(BF16)
            v.tensor_copy(w1T[:, :, :], wps[:, 0:TAPS*P].rearrange("p (t o) -> p t o", o=P)).then_inc(S["wT"], 1)
            v.tensor_copy(w2T[:, :], wps[:, TAPS*P:(TAPS+1)*P]).then_inc(S["wT"], 1)
            v.memset(der[:, 15:16], 0.0).then_inc(S["params"], 1)

            def moments(src, st, mv, s_st, s_bn, s_sd, s_rs, j):
                need(v, s_bn, j)
                for b in range(BLK):
                    last = v.bn_stats(st[:, b, :], src[:, b*P:(b+1)*P])
                last.then_inc(s_st, 1)
                need(v, s_st, j + 1)
                need(v, s_sd, j)
                need(v, s_rs, j)
                v.sem_inc(S["hold"], 1)
                for b in range(BLK):
                    last = v.bn_aggr(mv[:, b, :], st[:, b, :])
                last.then_inc(s_bn, 1)

            def scale_shift(sd, rs, nb, mv, s_sd, s_rc, s_rs, s_xt, j):
                need(v, s_sd, j + 1)
                need(v, s_xt, j)
                v.reciprocal(rs[:, :], sd[:, :]).then_inc(s_rc, 1)
                need(v, s_rc, j + 1)
                v.scalar_tensor_tensor(out=nb[:, :], in0=mv[:, :, 0], scalar=-1.0, in1=rs[:, :], op0=ALU.mult, op1=ALU.mult).then_inc(s_rs, 1)

            def body(k, at, turn):
                if front(k):
                    need(v, S["xT1"], k + 1)
                    moments(ln1_ps[:, at % 2, :], stats, mv1, S["st1"], S["bn1"], S["sd1"], S["rs1"], k)
                    scale_shift(sd1, rs1, nb1, mv1, S["sd1"], S["rc1"], S["rs1"], S["xt1"], k)
                if middle(k):
                    need(v, S["conv"], k)
                    need(v, S["lin1"], k - 1)
                    need(v, S["pos1"], k - 1)
                    need(v, S["xn"], k)
                    v.scalar_tensor_tensor(out=z1[:, :], in0=conv_ps[:, :], scalar=der[:, 6:7], in1=xn[:, (at - 1) % 2, :],
                                           op0=ALU.mult, op1=ALU.add).then_inc(S["z1"], 1)
                if back(k):
                    need(v, S["xT2"], k - 1)
                    moments(ln2_ps[:, :], stats2, mv2, S["st2"], S["bn2"], S["sd2"], S["rs2"], k - 2)
                if middle(k):
                    need(v, S["lin1"], k)
                    need(v, S["pos1"], k)
                    need(v, S["sg2"], k - 1)
                    need(v, S["z2"], k - 1)
                    v.scalar_tensor_tensor(out=out1[:, :], in0=pos1[:, :], scalar=der[:, 12:13], in1=lin1[:, :],
                                           op0=ALU.mult, op1=ALU.add).then_inc(S["out1"], 1)
                if back(k):
                    scale_shift(sd2, rs2, nb2, mv2, S["sd2"], S["rc2"], S["rs2"], S["xt2"], k - 2)
                if middle(k):
                    need(v, S["conv2"], k)
                    need(v, S["out1"], k)
                    need(v, S["lin2"], k - 1)
                    need(v, S["pos2"], k - 1)
                    v.scalar_tensor_tensor(out=z2[:, :], in0=conv_ps[:, :], scalar=der[:, 7:8], in1=out1[:, :],
                                           op0=ALU.mult, op1=ALU.add).then_inc(S["z2"], 1)
                if back(k):
                    q = at % 2
                    need(v, S["xnT2"], k - 1)
                    need(v, S["stt%d" % q], 16 * ((at - 2) // 2) + 32 * turn)
                    v.tensor_copy(tn[:, q, :], ln2_ps[:, :]).then_inc(S["tn"], 1)
                if middle(k):
                    need(v, S["lin2"], k)
                    need(v, S["pos2"], k)
                    need(v, S["xm"], k - 1)
                    v.scalar_tensor_tensor(out=out2[:, :], in0=pos2[:, :], scalar=der[:, 13:14], in1=lin2[:, :],
                                           op0=ALU.mult, op1=ALU.add).then_inc(S["out2"], 1)
            rounds(v, 6, LAST, 4, 4, body)

        @block.scalar
        def _(act):
            act.wait_ge(S["const"], 1)
            act.wait_ge(S["par"], 16 * len(NAMES))
            act.wait_ge(S["w"], 80)
            act.activation(der[:, 2:3], col["v1m"], ACT.Sqrt, bias=eps[:, 1:2]).then_inc(S["sdv"], 1)
            act.activation(der[:, 3:4], col["v2m"], ACT.Sqrt, bias=eps[:, 1:2]).then_inc(S["sdv"], 1)
            act.activation(w1s[:, :, :], w1f[:, :].rearrange("o (i t) -> o t i", t=TAPS), ACT.Sign).then_inc(S["wsg"], 1)
            act.activation(w2s[:, :], w2f[:, :], ACT.Sign).then_inc(S["wsg"], 1)
            act.wait_ge(S["params"], 1)

            def deviation(sd, mv, e, s_bn, s_rc, s_sd, j):
                need(act, s_bn, j + 1)
                need(act, s_rc, j)
                act.activation(sd[:, :], mv[:, :, 1], ACT.Sqrt, bias=eps[:, e:e+1]).then_inc(s_sd, 1)

            def normal(xt, src, rs, nb, s_rs, s_turned, s_xt, j):
                need(act, s_rs, j + 1)
                need(act, s_turned, j)
                for b in range(BLK):
                    last = act.activation(xt[:, b*P:(b+1)*P], src[:, b*P:(b+1)*P], ACT.Identity, bias=nb[:, b:b+1], scale=rs[:, b:b+1])
                last.then_inc(s_xt, 1)

            def body(k, at, turn):
                if front(k):
                    deviation(sd1, mv1, 0, S["bn1"], S["rc1"], S["sd1"], k)
                    normal(xt1, ln1_ps[:, at % 2, :], rs1, nb1, S["rs1"], S["xn1"], S["xt1"], k)
                if middle(k):
                    need(act, S["z1"], k)
                    need(act, S["out1"], k - 1)
                    act.activation(lin1[:, :], z1[:, :], ACT.Identity, bias=der[:, 10:11], scale=col["a1"]).then_inc(S["lin1"], 1)
                    act.activation(pos1[:, :], z1[:, :], ACT.Relu, bias=der[:, 8:9]).then_inc(S["pos1"], 1)
                if back(k):
                    deviation(sd2, mv2, 1, S["bn2"], S["rc2"], S["sd2"], k - 2)
                    normal(xt2, ln2_ps[:, :], rs2, nb2, S["rs2"], S["xnT2"], S["xt2"], k - 2)
                if front(k):
                    need(act, S["xn1"], k + 1)
                    need(act, S["conv"], k - 1)
                    act.activation(sg1[:, at % 2, 1:H+1, 1:W+1], ln1_ps[:, at % 2, :].rearrange("p (h w) -> p h w", w=W),
                                   ACT.Sign, bias=col["b11"]).then_inc(S["sg1"], 1)
                    need(act, S["z1"], k - 1)
                    act.activation(xn[:, at % 2, :], ln1_ps[:, at % 2, :], ACT.Identity).then_inc(S["xn"], 1)
                if middle(k):
                    need(act, S["out1"], k)
                    need(act, S["conv2"], k - 1)
                    act.activation(sg2[:, :], out1[:, :], ACT.Sign, bias=col["b21"]).then_inc(S["sg2"], 1)
                    need(act, S["z2"], k)
                    need(act, S["out2"], k - 1)
                    act.activation(lin2[:, :], z2[:, :], ACT.Identity, bias=der[:, 11:12], scale=col["a2"]).then_inc(S["lin2"], 1)
                    act.activation(pos2[:, :], z2[:, :], ACT.Relu, bias=der[:, 9:10]).then_inc(S["pos2"], 1)
                if back(k):
                    q = at % 2
                    need(act, S["rows"], k - 1)
                    need(act, S["str%d" % q], 16 * ((at - 2) // 2) + 32 * turn)
                    act.activation(agg[:, bass.ds((k - 2) * BLK, BLK), :], ln2_ps[:, 0:BLK*ROW].rearrange("p (b r) -> p b r", r=ROW)[:, :, 0:16], ACT.Identity)
                    act.activation(rw[:, q, :, :], ln2_ps[:, 0:BLK*ROW].rearrange("p (b r) -> p b r", r=ROW), ACT.Identity).then_inc(S["rw"], 1)
            rounds(act, 6, LAST, 4, 4, body)

def sorter(nc, edges_d, keys_d, half, flag):
    with ExitStack() as ctx:
        def sb(name, shape, dt=F32): return ctx.enter_context(nc.sbuf_tensor(f"s{half}_{name}", shape, dt))
        def sem(name): return ctx.enter_context(nc.semaphore(f"s{half}_{name}"))
        ping = sb("ping", [P, EDGE_COLS]); pong = sb("pong", [P, EDGE_COLS]); upper = sb("upper", [P, EDGE_COLS])
        src = sb("src", [P, EDGE_COLS], I32); dst = sb("dst", [P, EDGE_COLS], I32); word = sb("word", [P, EDGE_COLS], I32)
        hi_half = sb("hi_half", [P, EDGE_COLS // 2])
        lane = sb("lane", [P, 8], I32); sign = sb("sign", [P, 8]); turn_sign = sb("turn_sign", [P, 8])
        ident = sb("ident", [P, P]); pad = sb("pad", [P, TAIL // P]); top = sb("top", [P, 1]); topf = sb("topf", [1, 1])
        u_a = sb("u_a", [P, HEAD_COLS]); u_b = sb("u_b", [P, HEAD_COLS])
        turned_ps = ctx.enter_context(nc.psum_tensor(f"s{half}_turned", [P, EDGE_COLS], F32))
        loaded, const, ident_ok, done, to_turn, turned, copied, tables, iota_free, stored, u_back, flagged = (
            ctx.enter_context(semaphores(nc, f"s{half}", "loaded const ident done to_turn turned copied tables iota_free stored u_back flagged")).values())
        block = ctx.enter_context(nc.Block())
        edge_rows = [edges_d[r:r+1, :].rearrange("a (p f) -> (a p) f", p=P) for r in range(2)]
        low_rows = keys_d[1:1 + EDGES].rearrange("(p f) -> p f", p=P)
        high_flat = keys_d[1 + EDGES:1 + EDGES + HALF]
        CROSS = 2 * PART_BITS + 2

        final_low, final_high = [ping], [u_b]

        @block.sync
        def _(sp):
            sp.dma_start(src[:, :], edge_rows[0]).then_inc(loaded, 16)
            sp.dma_start(dst[:, :], edge_rows[1]).then_inc(loaded, 16)
            sp.wait_ge(const, 1)
            sp.dma_start(keys_d[0:1].rearrange("(a b) -> a b", a=1), pad[0:1, 0:1]).then_inc(stored, 16)
            sp.dma_start(keys_d[1 + EDGES + HALF:1 + EDGES + HALF + TAIL].rearrange("(a b) -> a b", a=P), pad[:, :]).then_inc(stored, 16)
            sp.wait_ge(iota_free, 1)
            sp.dma_start(high_flat.rearrange("(p f) -> p f", f=EDGE_COLS), upper[P - HALF // EDGE_COLS:P, :]).then_inc(stored, 16)
            sp.wait_ge(stored, 48)
            sp.dma_start(u_a[:, :], high_flat.rearrange("(p f) -> p f", p=P)).then_inc(u_back, 16)
            sp.wait_ge(iota_free, 2)
            sp.dma_start(low_rows, final_low[0][:, :]).then_inc(stored, 16)
            sp.wait_ge(iota_free, 3)
            sp.dma_start(high_flat.rearrange("(p f) -> p f", p=P), final_high[0][:, :]).then_inc(stored, 16)
            sp.wait_ge(stored, 80)

        @block.gpsimd
        def _(pool):
            pool.memset(ident[:, :], 0.0)
            pool.memset(pad[:, :], 1e4).then_inc(const, 1)
            pool.iota(lane[:, 0:1], [[0, 1]], base=0, channel_multiplier=1).then_inc(tables, 1)
            pool.wait_ge(const, 1)
            pool.affine_select(out=ident[:, :], in_=ident[:, :], compare_op=ALU.not_equal, fill=1.0, base=0,
                               pattern=[[-1, P]], channel_multiplier=1).then_inc(ident_ok, 1)
            pool.wait_ge(tables, 2)
            pool.iota(dst[:, :], [[-1, EDGE_COLS]], base=EDGES - 1, channel_multiplier=-EDGE_COLS).then_inc(tables, 1)

        crossing_source = []

        def halves(ap, span, mirrored=False):
            v = ap.rearrange("p (g two h) -> p g two h", two=2, h=span)
            return v[:, :, 0, :], (v[:, :, 1, ::-1] if mirrored else v[:, :, 1, :])

        def chunk_of(ap, x, span, c):
            lo, hi = halves(ap, span)
            if x % 2 == 0:
                n = lo.shape[1] // TURN_CHUNKS
                return lo[:, c*n:(c+1)*n, :], hi[:, c*n:(c+1)*n, :]
            n = span // TURN_CHUNKS
            return lo[:, :, c*n:(c+1)*n], hi[:, :, c*n:(c+1)*n]

        spans = []
        for k in [*range(1, PART_BITS + 1), PART_BITS]:
            spans += [1 << (k - 1), 1 << (COL_BITS - 1)]

        def copy_of(x, c):
            n = EDGE_COLS // 2 // TURN_CHUNKS
            _, hi = chunk_of(turned_ps[:, :], x, spans[x], c)
            return hi_half[:, c*n:(c+1)*n].rearrange("p (g h) -> p g h", h=hi.shape[2])
        def u_copy(x):
            return hi_half[:, 0:HEAD_COLS//2].rearrange("p (g h) -> p g h", h=(64, 128)[x])
        u_source = (u_a, u_b)
        @block.vector
        def _(v):
            count = [0]
            def go(i):
                count[0] += 1
                i.then_inc(done, 1)
            def settle():
                v.wait_ge(done, count[0])
            edge_clamp, edge_op = ([float(HALF - SHIFT - 1)], ALU.min) if half == 0 else ([-float(SHIFT)], ALU.max)
            def words(word_f, limit_first):
                base = HALF * half + SHIFT
                settle()
                if half == 0:
                    go(v.tensor_scalar(upper_scratch, dst[:, :], base + (HALF - SHIFT) - 0.5, 16.0, ALU.subtract, ALU.mult))
                else:
                    go(v.tensor_scalar(upper_scratch, dst[:, :], base - SHIFT - 0.5, -16.0, ALU.subtract, ALU.mult))
                go(v.tensor_tensor(src[:, :], src[:, :], dst[:, :], ALU.bitwise_xor)); settle()
                go(v.tensor_scalar(word[:, :], dst[:, :], float(base), *edge_clamp, ALU.subtract, edge_op)); settle()
                go(v.tensor_scalar(dst[:, :], word[:, :], float(LEAST), -1.0, ALU.is_lt, ALU.mult)); settle()
                go(v.scalar_tensor_tensor(out=word[:, :], in0=dst[:, :], scalar=-float(FLIP), in1=word[:, :], op0=ALU.mult, op1=ALU.add)); settle()
                go(v.tensor_scalar(word[:, :], word[:, :], 16, None, ALU.logical_shift_left)); settle()
                go(v.tensor_tensor(word[:, :], word[:, :], src[:, :], ALU.bitwise_or)); settle()
                go(v.tensor_tensor(word[:, :], word[:, :], dst[:, :], ALU.bitwise_xor)); settle()
                go(v.tensor_tensor(word_f, word[:, :].bitcast(F32), upper_scratch, ALU.max)); settle()
            v.wait_ge(loaded, 32)
            if flag is not None:
                go(v.tensor_reduce(top[:, :], dst[:, :], AX.X, ALU.max))
            upper_scratch = upper[:, :]
            words(ping[:, :], True)
            v.wait_ge(tables, 1)
            for k in range(8):
                go(v.tensor_scalar(lane[:, k:k+1], lane[:, 0:1], k, 1, ALU.logical_shift_right, ALU.bitwise_and)) if k else None
            settle()
            go(v.tensor_scalar(lane[:, 0:1], lane[:, 0:1], 1, None, ALU.bitwise_and)); settle()
            go(v.tensor_scalar(sign[:, :], lane[:, :], -2.0, 1.0, ALU.mult, ALU.add)); settle()
            go(v.tensor_copy(turn_sign[:, 0:1], sign[:, 0:1]))
            go(v.tensor_tensor(turn_sign[:, 1:8], sign[:, 0:7], sign[:, 1:8], ALU.mult)); settle()
            a, b = ping, pong
            go(v.tensor_scalar(b[:, :], a[:, :], turn_sign[:, 0:1], None, ALU.mult)); settle()
            v.sem_inc(tables, 1)
            a, b = b, a

            def step(a, b, span, mirrored=False, n=None):
                lo, hi = halves(a[:, :], span, mirrored)
                olo, ohi = halves(b[:, :], span, mirrored)
                go(v.tensor_tensor(olo, lo, hi, ALU.min))
                go(v.tensor_tensor(ohi, lo, hi, ALU.max))
                settle()
                return b, a

            def cross(a, b):
                x = len(crossing_source)
                crossing_source.append(a)
                v.sem_inc(to_turn, 1)
                for c in range(TURN_CHUNKS):
                    lo, _ = chunk_of(turned_ps[:, :], x, spans[x], c)
                    olo, ohi = chunk_of(b[:, :], x, spans[x], c)
                    hi = copy_of(x, c)
                    v.wait_ge(copied, TURN_CHUNKS * x + c + 1)
                    go(v.tensor_tensor(olo, lo, hi, ALU.min))
                    go(v.tensor_tensor(ohi, lo, hi, ALU.max))
                settle()
                return b, a

            for level in range(1, COL_BITS + 1):
                for s in range(level, 0, -1):
                    a, b = step(a, b, 1 << (s - 1), mirrored=(s == level))
            for k in range(1, PART_BITS + 1):
                go(v.tensor_scalar(b[:, :], a[:, :], turn_sign[:, k:k+1] if k < PART_BITS else sign[:, PART_BITS-1:PART_BITS], None, ALU.mult)); settle()
                a, b = b, a
                a, b = cross(a, b)
                for s in range(k - 1, 0, -1):
                    a, b = step(a, b, 1 << (s - 1))
                a, b = cross(a, b)
                for s in range(COL_BITS - 1, 0, -1):
                    a, b = step(a, b, 1 << (s - 1))
            v.wait_ge(tables, 3)
            if half:
                go(v.tensor_scalar(b[:, :], dst[:, :], HALF - 0.5, 16.0, ALU.subtract, ALU.mult))
                go(v.tensor_scalar(src[:, :], dst[:, :], float(HALF), 2.0 * HALF - 1, ALU.add, ALU.min)); settle()
                go(v.tensor_copy(dst[:, :], src[:, :])); settle()
                words(upper[:, :], False)
                go(v.tensor_tensor(upper[:, :], upper[:, :], b[:, :], ALU.max)); settle()
            else:
                go(v.tensor_copy(src[:, :], dst[:, :])); settle()
                words(upper[:, :], False)
            go(v.tensor_tensor(b[:, :], a[:, :], upper[:, :], ALU.min))
            go(v.tensor_tensor(upper[:, :], a[:, :], upper[:, :], ALU.max)); settle()
            v.sem_inc(iota_free, 1)
            a, b = b, a
            a, b = cross(a, b)
            for s in range(PART_BITS - 1, 0, -1):
                a, b = step(a, b, 1 << (s - 1))
            a, b = cross(a, b)
            for s in range(COL_BITS - 1, 0, -1):
                a, b = step(a, b, 1 << (s - 1))
            assert a is final_low[0], "low"
            v.sem_inc(iota_free, 1)
            v.wait_ge(u_back, 16)
            ua, ub = u_a, u_b
            for x, (top_bit) in enumerate((PART_BITS, COL_BITS - 4)):
                v.sem_inc(to_turn, 1)
                v.wait_ge(copied, TURN_CHUNKS * CROSS + x + 1)
                lo, _ = halves(turned_ps[:, 0:HEAD_COLS], 1 << (top_bit - 1))
                olo, ohi = halves(ub[:, :], 1 << (top_bit - 1))
                hi = u_copy(x)
                go(v.tensor_tensor(olo, lo, hi, ALU.min))
                go(v.tensor_tensor(ohi, lo, hi, ALU.max)); settle()
                ua, ub = ub, ua
                for s in range(top_bit - 1, 0, -1):
                    ua, ub = step(ua, ub, 1 << (s - 1))
                if x == 0:
                    assert ua is u_source[1], "u"
            assert ua is final_high[0], "high"
            v.sem_inc(iota_free, 1)
            if flag is not None:
                v.sem_inc(flagged, 1)
                v.wait_ge(flagged, 2)
                go(v.tensor_reduce(topf[:, :], turned_ps[0:1, 0:P], AX.X, ALU.max)); settle()
                go(v.tensor_scalar(flag, topf[:, :], float(HALF), None, ALU.is_ge)); settle()

        @block.scalar
        def _(act):
            for x in range(CROSS):
                for c in range(TURN_CHUNKS):
                    act.wait_ge(turned, TURN_CHUNKS * x + c + 1)
                    _, hi = chunk_of(turned_ps[:, :], x, spans[x], c)
                    act.activation(copy_of(x, c), hi, ACT.Copy).then_inc(copied, 1)
            for x in range(2):
                act.wait_ge(turned, TURN_CHUNKS * CROSS + x + 1)
                _, hi = halves(turned_ps[:, 0:HEAD_COLS], (64, 128)[x])
                act.activation(u_copy(x), hi, ACT.Copy).then_inc(copied, 1)
        @block.tensor
        def _(pe):
            pe.wait_ge(ident_ok, 1)
            blocks = EDGE_COLS // P
            per = blocks // TURN_CHUNKS
            for x in range(CROSS):
                pe.wait_ge(to_turn, x + 1)
                source = crossing_source[x]
                for c in range(TURN_CHUNKS):
                    if x % 2 == 0:
                        which = range(c * per, (c + 1) * per)
                    else:
                        a = range(c * per // 2, (c + 1) * per // 2)
                        which = [*a, *(g + blocks // 2 for g in a)]
                    for g in which:
                        last = pe.transpose(turned_ps[:, g*P:(g+1)*P], source[:, g*P:(g+1)*P], ident[:, :])
                    last.then_inc(turned, 1)
            for x in range(2):
                pe.wait_ge(to_turn, CROSS + x + 1)
                source = (u_a, u_b)[x]
                for g in range(HEAD_COLS // P):
                    last = pe.transpose(turned_ps[:, g*P:(g+1)*P], source[:, g*P:(g+1)*P], ident[:, :])
                last.then_inc(turned, 1)
            if flag is not None:
                pe.wait_ge(flagged, 1)
                pe.transpose(turned_ps[0:1, 0:P], top[:, :], ident[:, :]).then_inc(flagged, 1)


def attention(nc, edges_d, keys_d, rows_d, res_d, agg, half, gathers, make_experts=None):
    with ExitStack() as ctx, ExitStack() as during:
        def keep(name, shape, dt=F32): return ctx.enter_context(nc.sbuf_tensor(f"e{half}_{name}", shape, dt))
        def sb(name, shape, dt=F32): return during.enter_context(nc.sbuf_tensor(f"e{half}_{name}", shape, dt))
        def sem(name): return during.enter_context(nc.semaphore(f"e{half}_{name}"))
        prev_seg, first_seg, last_seg = (keep(n, [P, 1]) for n in ("prev_seg", "first_seg", "last_seg"))
        iota_f, zlast, counts = keep("iota_f", [P, HIS]), keep("zlast", [P, ROW]), keep("counts", [P, HIS])
        x = make_experts(during) if make_experts else None
        key = sb("key", [P, 2, COLS + 1], I32)
        sgn = sb("sgn", [P, COLS + 1], I32); mag = sb("mag", [P, COLS + 1], I32); low = sb("low", [P, COLS + 1], I32)
        seg = sb("seg", [P, COLS + 1], I32); dfull = sb("dfull", [P, COLS + 1], I32)
        index = sb("index", [P, 2, COLS], I32); first = sb("first", [P, 1], I32)
        start = sb("start", [P, 2, COLS]); cont = sb("cont", [P, 2, COLS]); cut = sb("cut", [P, 2, COLS])
        got = sb("got", [P, 2, COLS, ROW]); head0 = sb("head0", [P, ROW])
        adv = sb("adv", [P, HEADS, COLS]); ad = sb("ad", [P, 2, HEADS, COLS]); e = sb("e", [P, HEADS, COLS])
        mx = sb("mx", [P, 2, HEADS, COLS + 1]); dif = sb("dif", [P, 2, HEADS, COLS]); rp = sb("rp", [P, 2, HEADS, COLS])
        wgt = sb("wgt", [P, HEADS, EXPERTS, COLS]); out = sb("out", [P, 2, COLS, ROW])
        tgt = sb("tgt", [P, 2, COUNT_TILES], I32); tlo_i = sb("tlo_i", [P, COUNT_TILES], I32); thi_i = sb("thi_i", [P, COUNT_TILES], I32)
        tlo = sb("tlo", [P, COUNT_TILES]); thi = sb("thi", [P, COUNT_TILES])
        iota_i = sb("iota_i", [P, HIS], I32); iota_b = sb("iota_b", [P, HIS], BF16)
        is_lo = sb("is_lo", [P, 2, RING, P], BF16); is_hi = sb("is_hi", [P, 2, RING, HIS], BF16)
        count_ps = during.enter_context(nc.psum_tensor(f"e{half}_count_ps", [P, 512], F32))
        S = dict(during.enter_context(semaphores(nc, f"e{half}", "key0 key1 dec idx init proc dif exp out st0 st1 tgt0 tgt1 cnt_d hot hit edge iot free")))
        S.update({n: gathers(f"e{half}_{n}") for n in ("gat0", "gat1", "gat2", "gat3", "head")})
        DEC, PROC, CNT = 12, 37, 4

        LAST = CHUNKS + 1
        def decodes(k): return not isinstance(k, int) or k < CHUNKS
        def attends(k): return not isinstance(k, int) or k >= 1

        key_rows = lambda k: keys_d[bass.ds(k * COLS, P * RUN)].rearrange("(q f) -> q f", f=RUN)[:, 0:COLS + 1]
        tgt_rows = lambda k: edges_d[1:2, bass.ds(k * (P * COUNT_TILES), P * COUNT_TILES)].rearrange("a (p f) -> (a p) f", p=P)
        res_rows = res_d.rearrange("(q f) r -> q (f r)", f=RUN)

        with nc.Block() as block:
            @block.sync
            def _(sp):
                if x: x.start_sync(sp)
                for u in range(2):
                    sp.dma_start(key[:, u, :].bitcast(F32), key_rows(u)).then_inc(S["key%d" % u], 16)
                    sp.dma_start(tgt[:, u, :], tgt_rows(u)).then_inc(S["tgt%d" % u], 16)
                def body(k, at, turn):
                    if attends(k):
                        q = (at - 1) % 2
                        need(sp, S["out"], k)
                        sp.dma_start(res_rows[:, bass.ds((k - 1) * (COLS * ROW), COLS * ROW)],
                                     out[:, q, :, :].rearrange("p f r -> p (f r)")).then_inc(S["st%d" % q], 16)
                    if not isinstance(k, int) or k + 2 < CHUNKS:
                        u = at % 2
                        need(sp, S["dec"], DEC * (k + 1))
                        sp.dma_start(key[:, u, :].bitcast(F32), key_rows(k + 2)).then_inc(S["key%d" % u], 16)
                        need(sp, S["cnt_d"], CNT * (k + 1))
                        sp.dma_start(tgt[:, u, :], tgt_rows(k + 2)).then_inc(S["tgt%d" % u], 16)
                    if x: x.sync(sp, k, at, turn, 4)
                rounds(sp, 6, LAST, 3, 4, body)
                for q in range(2):
                    sp.wait_ge(S["st%d" % q], 16 * CHUNKS // 2)
                if x: x.end_sync(sp)

            @block.gpsimd
            def _(pool):
                pool.iota(iota_i[:, :], [[1, HIS]], base=0, channel_multiplier=0).then_inc(S["iot"], 1)
                if x: x.start_gpsimd(pool)
                pool.wait_ge(S["edge"], 1)
                pool.indirect_dma_start(head0[:, :], None, rows_d, bass.IndirectOffsetOnAxis(ap=first[:, :], axis=0)).then_inc(S["head"], 16)
                def body(k, at, turn):
                    if decodes(k):
                        need(pool, S["idx"], k + 1)
                        need(pool, S["out"], k - 1)
                        pool.sem_inc(S["free"], 1)
                        for c in range(COLS):
                            pool.indirect_dma_start(got[:, at % 2, c, :], None, rows_d,
                                bass.IndirectOffsetOnAxis(ap=index[:, at % 2, c:c+1], axis=0)).then_inc(S["gat%d" % (at % 4)], 16)
                rounds(pool, 6, LAST, 3, 4, body)

            @block.tensor
            def _(pe):
                if x: x.start_tensor(pe)
                def body(k, at, turn):
                    if decodes(k):
                        for g in range(COUNT_TILES // RING):
                            need(pe, S["hot"], k * (COUNT_TILES // RING) + g + 1)
                            for t in range(RING):
                                last = pe.matmul(count_ps[:, 0:HIS], is_lo[:, g % 2, t, :], is_hi[:, g % 2, t, :],
                                                 start=(isinstance(k, int) and k == 0 and g == 0 and t == 0),
                                                 stop=(isinstance(k, int) and k == CHUNKS - 1 and g == COUNT_TILES // RING - 1 and t == RING - 1))
                            last.then_inc(S["hit"], 1)
                    if x: x.tensor(pe, k, at, turn, 4)
                rounds(pe, 6, LAST, 3, 4, body)

            @block.scalar
            def _(act):
                if x: act.wait_ge(x.S["w"], x.WEIGHTS)
                def body(k, at, turn):
                    if attends(k):
                        need(act, S["dif"], k)
                        act.activation(rp[:, :, :, :], dif[:, :, :, :], ACT.Exp).then_inc(S["exp"], 1)
                    if x: x.scalar(act, k, at, turn, 4)
                rounds(act, 6, LAST, 3, 4, body)

            @block.vector
            def _(v):
                if x: x.start_vector(v)
                v.wait_ge(S["iot"], 1)
                v.tensor_copy(iota_f[:, :], iota_i[:, :]).then_inc(S["iot"], 1)
                v.tensor_copy(iota_b[:, :], iota_i[:, :]).then_inc(S["iot"], 1)

                def body(k, at, turn):
                    if decodes(k):
                        u = at % 2
                        i = [0]
                        def go(ins):
                            i[0] += 1
                            ins.then_inc(S["dec"], 1)
                            v.wait_ge(S["dec"], DEC * k + i[0])
                        v.wait_ge(S["key%d" % u], 16 * (at // 2 + 1) + 32 * turn)
                        kk = key[:, u, :]
                        go(v.tensor_scalar(sgn[:, :], kk, 31, None, ALU.arith_shift_right))
                        go(v.tensor_tensor(mag[:, :], kk, sgn[:, :], ALU.bitwise_xor))
                        go(v.tensor_scalar(low[:, :], mag[:, :], 16, None, ALU.logical_shift_right))
                        go(v.scalar_tensor_tensor(out=seg[:, :], in0=sgn[:, :], scalar=float(FLIP), in1=low[:, :], op0=ALU.mult, op1=ALU.add))
                        go(v.tensor_scalar(dfull[:, :], seg[:, :], float(SHIFT + HALF * half), None, ALU.add))
                        go(v.tensor_tensor(mag[:, :], mag[:, :], dfull[:, :], ALU.bitwise_xor))
                        if not isinstance(k, int) or k >= 2:
                            v.wait_ge(S["gat%d" % ((at - 2) % 4)], 16 * COLS * ((at - 2) // 4 + 1) + 16 * COLS * turn)
                        go(v.tensor_scalar(index[:, u, :], mag[:, 1:COLS+1], 65535, None, ALU.bitwise_and))
                        v.sem_inc(S["idx"], 1)
                        go(v.tensor_tensor(start[:, u, :], seg[:, 1:COLS+1], seg[:, 0:COLS], ALU.not_equal))
                        go(v.tensor_scalar(cont[:, u, :], start[:, u, :], -1.0, 1.0, ALU.mult, ALU.add))
                        go(v.tensor_scalar(cut[:, u, :], start[:, u, :], -BIG, None, ALU.mult))
                        if isinstance(k, int) and k == 0:
                            go(v.tensor_copy(prev_seg[:, :], seg[:, 0:1]))
                            go(v.tensor_copy(first_seg[:, :], seg[:, 1:2]))
                            v.tensor_scalar(first[:, :], dfull[:, 1:2], 65535, None, ALU.bitwise_and).then_inc(S["edge"], 1)
                        else:
                            go(v.tensor_copy(last_seg[:, :], seg[:, COLS:COLS+1]))
                            go(v.tensor_copy(last_seg[:, :], seg[:, COLS:COLS+1]))
                        assert i[0] == DEC
                        v.wait_ge(S["tgt%d" % u], 16 * (at // 2 + 1) + 32 * turn)
                        need(v, S["hit"], k * (COUNT_TILES // RING))
                        c = S["cnt_d"]
                        v.tensor_scalar(tlo_i[:, :], tgt[:, u, :], P - 1, None, ALU.bitwise_and).then_inc(c, 1)
                        v.tensor_scalar(thi_i[:, :], tgt[:, u, :], 7, None, ALU.logical_shift_right).then_inc(c, 1)
                        v.wait_ge(c, CNT * k + 2)
                        v.tensor_copy(tlo[:, :], tlo_i[:, :]).then_inc(c, 1)
                        v.tensor_scalar(thi[:, :], thi_i[:, :], float(HIS * half), None, ALU.subtract).then_inc(c, 1)
                        v.wait_ge(c, CNT * k + 4)
                        v.wait_ge(S["iot"], 3)
                        for g in range(COUNT_TILES // RING):
                            if (isinstance(k, int) and k > 0) or not isinstance(k, int) or g >= 2:
                                v.wait_ge(S["hit"], k * (COUNT_TILES // RING) + g - 1)
                            for t in range(RING):
                                n = g * RING + t
                                v.tensor_scalar(is_lo[:, g % 2, t, :], iota_b[:, 0:P], tlo[:, n:n+1], None, ALU.is_equal)
                                last = v.tensor_scalar(is_hi[:, g % 2, t, :], iota_b[:, :], thi[:, n:n+1], None, ALU.is_equal)
                            last.then_inc(S["hot"], 1)
                    if attends(k):
                        q = (at - 1) % 2
                        j = k - 1
                        i = [0]
                        def go(ins):
                            i[0] += 1
                            ins.then_inc(S["proc"], 1)
                        def settle():
                            v.wait_ge(S["proc"], PROC * j + i[0])
                        if isinstance(k, int) and k == 1:
                            v.wait_ge(S["head"], 16)
                            v.tensor_copy(ad[:, 1, :, COLS-1], head0[:, 20:24]).then_inc(S["init"], 1)
                            v.memset(mx[:, 1, :, COLS], -BIG).then_inc(S["init"], 1)
                            v.memset(out[:, 1, :, :], 0.0).then_inc(S["init"], 1)
                            v.wait_ge(S["init"], 3)
                        v.wait_ge(S["gat%d" % ((at - 1) % 4)], 16 * COLS * ((at - 1) // 4 + 1) + 16 * COLS * turn)
                        if not isinstance(k, int) or k >= 3:
                            v.wait_ge(S["st%d" % q], 16 * ((at - 1) // 2) + 32 * turn)
                        g = got[:, q, :, :]
                        by_head = lambda ap: ap.unsqueeze(1).broadcast_to([P, HEADS, COLS])
                        go(v.tensor_tensor(adv[:, :, :], g[:, :, 20:24].rearrange("p c h -> p h c"), by_head(start[:, q, :]), ALU.mult)); settle()
                        for h in range(HEADS):
                            go(v.tensor_tensor_scan(ad[:, q, h, :], cont[:, q, :], adv[:, h, :], ad[:, 1 - q, h, COLS-1:COLS], ALU.mult, ALU.add))
                        settle()
                        go(v.tensor_tensor(e[:, :, :], ad[:, q, :, :], g[:, :, 16:20].rearrange("p c h -> p h c"), ALU.add)); settle()
                        go(v.scalar_tensor_tensor(out=e[:, :, :], in0=e[:, :, :], scalar=0.2, in1=e[:, :, :], op0=ALU.mult, op1=ALU.max))
                        go(v.tensor_copy(mx[:, q, :, 0], mx[:, 1 - q, :, COLS])); settle()
                        for h in range(HEADS):
                            go(v.tensor_tensor_scan(mx[:, q, h, 1:COLS+1], cut[:, q, :], e[:, h, :], mx[:, 1 - q, h, COLS:COLS+1], ALU.add, ALU.max))
                        settle()
                        go(v.tensor_tensor(dif[:, 0, :, :], mx[:, q, :, 0:COLS], by_head(cut[:, q, :]), ALU.add)); settle()
                        go(v.tensor_tensor(dif[:, 0, :, :], dif[:, 0, :, :], mx[:, q, :, 1:COLS+1], ALU.subtract))
                        go(v.tensor_tensor(dif[:, 1, :, :], e[:, :, :], mx[:, q, :, 1:COLS+1], ALU.subtract)); settle()
                        v.sem_inc(S["dif"], 1)
                        go(v.tensor_copy(out[:, q, :, 20:24].rearrange("p c h -> p h c"), mx[:, q, :, 1:COLS+1]))
                        v.wait_ge(S["exp"], k)
                        go(v.tensor_tensor(wgt[:, :, :, :], g[:, :, 0:16].rearrange("p c (h x) -> p h x c", x=EXPERTS),
                                           rp[:, 1, :, :].unsqueeze(2).broadcast_to([P, HEADS, EXPERTS, COLS]), ALU.mult)); settle()
                        for h in range(HEADS):
                            for w in range(EXPERTS + 1):
                                ch = h * EXPERTS + w if w < EXPERTS else HEADS * EXPERTS + h
                                data = wgt[:, h, w, :] if w < EXPERTS else rp[:, 1, h, :]
                                go(v.tensor_tensor_scan(out[:, q, :, ch], rp[:, 0, h, :], data, out[:, 1 - q, COLS-1, ch:ch+1], ALU.mult, ALU.add))
                        settle()
                        v.sem_inc(S["out"], 1)
                        assert i[0] == PROC, i[0]
                    if x: x.vector(v, k, at, turn, 4)
                rounds(v, 6, LAST, 3, 4, body)
                v.wait_ge(S["hit"], CHUNKS * COUNT_TILES // RING)
                v.tensor_scalar(counts[:, :], count_ps[:, 0:HIS], 1.0, None, ALU.add).then_inc(S["iot"], 1)
                v.tensor_copy(zlast[:, :], out[:, (CHUNKS - 1) % 2, COLS-1, :]).then_inc(S["iot"], 1)
                v.wait_ge(S["iot"], 5)

        during.close()
        gather_tokens(nc, ctx, res_d, agg, half, gathers, zlast, counts, prev_seg, first_seg, last_seg, iota_f)

def gather_tokens(nc, ctx, res_d, agg, half, gathers, zlast, counts, prev_seg, first_seg, last_seg, iota_f):
    def sb(name, shape, dt=F32): return ctx.enter_context(nc.sbuf_tensor(f"e{half}_{name}", shape, dt))
    def ps(name, shape, dt=F32): return ctx.enter_context(nc.psum_tensor(f"e{half}_{name}", shape, dt))
    def sem(name): return ctx.enter_context(nc.semaphore(f"g{half}_{name}"))
    CH = HEADS * (EXPERTS + 1)
    ident = sb("g_ident", [P, P]); ones = sb("g_ones", [P, P]); upto = sb("g_upto", [P, P])
    total = sb("g_total", [P, HIS]); before = sb("g_before", [P, HIS]); pos = sb("g_pos", [P, HIS]); pos_i = sb("g_pos_i", [P, HIS], I32)
    tok = sb("g_tok", [P, 1]); tok_i = sb("g_tok_i", [P, 1], I32); lo_i = sb("g_lo_i", [P, 1], I32); hi_i = sb("g_hi_i", [P, 1], I32)
    lo_f = sb("g_lo_f", [P, 1]); hi_f = sb("g_hi_f", [P, 1])
    one_lo = sb("g_one_lo", [P, P]); one_lo_t = sb("g_one_lo_t", [P, P]); one_hi = sb("g_one_hi", [P, HIS]); picked = sb("g_picked", [P, HIS])
    end = sb("g_end", [P, 1]); lane_end = sb("g_lane_end", [P, 1]); lane_i = sb("g_lane_i", [P, 1], I32)
    t1 = sb("g_t1", [P, 1]); t2 = sb("g_t2", [P, 1]); skip = sb("g_skip", [P, 1]); at_i = sb("g_at_i", [P, 1], I32); to_i = sb("g_to_i", [P, 1], I32)
    z = sb("g_z", [P, 3, CH]); zt = sb("g_zt", [CH, 3, P]); mm = sb("g_mm", [CH, P + 1]); ss = sb("g_ss", [CH, P + 1])
    dd = sb("g_dd", [CH, 2, P]); ee = sb("g_ee", [CH, 2, P]); ww = sb("g_ww", [CH, P])
    cin = sb("g_cin", [P, 2, CH]); row = sb("g_row", [P, ROW]); rm = sb("g_rm", [P, CH]); nm = sb("g_nm", [P, CH])
    d2 = sb("g_d2", [P, 2, CH]); e2 = sb("g_e2", [P, 2, CH]); new = sb("g_new", [P, ROW])
    PER = 8
    tidx = sb("g_tidx", [P, 2, PER], I32); trow = sb("g_trow", [P, 2, PER, ROW]); tsum = sb("g_tsum", [P, 2, PER, HEADS]); trec = sb("g_trec", [P, 2, PER, HEADS])
    a_ps = ps("g_a_ps", [P, 512]); b_ps = ps("g_b_ps", [P, 512]); c_ps = ps("g_c_ps", [P, 512])
    S = dict(ctx.enter_context(semaphores(nc, f"g{half}", "const c2 dv pe act got idx agg dn free")))
    S.update({n: gathers(f"g{half}_{n}") for n in ("put", "tg0", "tg1")})
    TURNS = HIS // PER
    with nc.Block() as block:
        dv, pe_s = S["dv"], S["pe"]
        @block.gpsimd
        def _(pool):
            pool.memset(ident[:, :], 0.0)
            pool.memset(ones[:, :], 1.0)
            pool.memset(upto[:, :], 1.0).then_inc(S["const"], 1)
            pool.wait_ge(S["const"], 1)
            pool.iota(lane_i[:, :], [[0, 1]], base=RUN - 1, channel_multiplier=RUN)
            pool.affine_select(out=ident[:, :], in_=ident[:, :], compare_op=ALU.not_equal, fill=1.0, base=0, pattern=[[-1, P]], channel_multiplier=1)
            pool.affine_select(out=upto[:, :], in_=upto[:, :], compare_op=ALU.is_ge, fill=0.0, base=0, pattern=[[1, P]], channel_multiplier=-1).then_inc(S["const"], 1)
            pool.wait_ge(S["got"], 1)
            pool.indirect_dma_start(row[:, :], None, res_d, bass.IndirectOffsetOnAxis(ap=at_i[:, :], axis=0)).then_inc(S["put"], 16)
            pool.wait_ge(S["got"], 2)
            pool.indirect_dma_start(res_d, bass.IndirectOffsetOnAxis(ap=to_i[:, :], axis=0), new[:, :], None,
                                    bounds_check=ENTRIES - 1, oob_is_err=False).then_inc(S["put"], 16)
            pool.wait_ge(S["put"], 32)
            def body(k, at, turn):
                if not isinstance(k, int) or k < TURNS:
                    need(pool, S["idx"], k + 1)
                    need(pool, S["agg"], k - 1)
                    pool.sem_inc(S["free"], 1)
                    for c in range(PER):
                        pool.indirect_dma_start(trow[:, at % 2, c, :], None, res_d,
                            bass.IndirectOffsetOnAxis(ap=tidx[:, at % 2, c:c+1], axis=0)).then_inc(S["tg%d" % (at % 2)], 16)
            rounds(pool, 2, TURNS + 1, 1, 2, body)

        @block.tensor
        def _(pe):
            pe.wait_ge(S["const"], 2)
            pe.matmul(a_ps[:, 0:HIS], ones[:, :], counts[:, :], start=True, stop=True)
            pe.matmul(a_ps[:, HIS:2*HIS], upto[:, :], counts[:, :], start=True, stop=True).then_inc(pe_s, 1)
            pe.wait_ge(S["c2"], 1)
            pe.transpose(b_ps[:, 0:P], one_lo[:, :], ident[:, :]).then_inc(pe_s, 1)
            pe.wait_ge(S["c2"], 2)
            pe.matmul(b_ps[:, P:P+HIS], one_lo_t[:, :], pos[:, :], start=True, stop=True).then_inc(pe_s, 1)
            pe.wait_ge(S["c2"], 3)
            for i in range(3):
                last = pe.transpose(c_ps[0:CH, i*P:(i+1)*P], z[:, i, :], ident[:, :])
            last.then_inc(pe_s, 1)
            pe.wait_ge(S["c2"], 4)
            pe.transpose(c_ps[:, 384:384+CH], mm[:, 0:P], ident[0:CH, 0:CH])
            pe.transpose(c_ps[:, 448:448+CH], ss[:, 0:P], ident[0:CH, 0:CH]).then_inc(pe_s, 1)

        @block.scalar
        def _(act):
            act.wait_ge(S["act"], 1)
            act.activation(ee[:, :, :], dd[:, :, :], ACT.Exp).then_inc(S["act"], 1)
            act.wait_ge(S["act"], 3)
            act.activation(e2[:, :, :], d2[:, :, :], ACT.Exp).then_inc(S["act"], 1)

        @block.vector
        def _(v):
            n = [0]
            def go(i):
                n[0] += 1
                i.then_inc(dv, 1)
                v.wait_ge(dv, n[0])
            v.wait_ge(S["const"], 2)
            v.wait_ge(pe_s, 1)
            go(v.tensor_copy(total[:, :], a_ps[:, 0:HIS]))
            go(v.memset(one_hi[:, :], 1.0))
            go(v.tensor_tensor_scan(before[:, :], one_hi[:, :], total[:, :], 0.0, ALU.mult, ALU.add))
            go(v.tensor_tensor(before[:, :], before[:, :], total[:, :], ALU.subtract))
            go(v.scalar_tensor_tensor(out=pos[:, :], in0=a_ps[:, HIS:2*HIS], scalar=-1.0, in1=before[:, :], op0=ALU.add, op1=ALU.add))
            go(v.tensor_copy(pos_i[:, :], pos[:, :]))
            go(v.tensor_scalar(tok[:, :], first_seg[:, :], float(SHIFT), None, ALU.add))
            go(v.tensor_copy(tok_i[:, :], tok[:, :]))
            go(v.tensor_scalar(lo_i[:, :], tok_i[:, :], P - 1, None, ALU.bitwise_and))
            go(v.tensor_scalar(hi_i[:, :], tok_i[:, :], 7, None, ALU.logical_shift_right))
            go(v.tensor_copy(lo_f[:, :], lo_i[:, :]))
            go(v.tensor_copy(hi_f[:, :], hi_i[:, :]))
            go(v.tensor_scalar(one_lo[:, :], iota_f[:, 0:P], lo_f[:, :], None, ALU.is_equal))
            go(v.tensor_scalar(one_hi[:, :], iota_f[:, :], hi_f[:, :], None, ALU.is_equal))
            v.sem_inc(S["c2"], 1)
            v.wait_ge(pe_s, 2)
            go(v.tensor_copy(one_lo_t[:, :], b_ps[:, 0:P]))
            v.sem_inc(S["c2"], 1)
            v.wait_ge(pe_s, 3)
            go(v.tensor_tensor(picked[:, :], b_ps[:, P:P+HIS], one_hi[:, :], ALU.mult))
            go(v.reduce_sum(end[:, :], picked[:, :], axis=AX.X))
            go(v.tensor_copy(lane_end[:, :], lane_i[:, :]))
            go(v.tensor_tensor(skip[:, :], first_seg[:, :], prev_seg[:, :], ALU.not_equal))
            go(v.tensor_tensor(t1[:, :], end[:, :], lane_end[:, :], ALU.is_gt))
            go(v.tensor_tensor(skip[:, :], skip[:, :], t1[:, :], ALU.add))
            go(v.tensor_scalar(t2[:, :], tok[:, :], float(HALF), None, ALU.is_ge))
            go(v.tensor_tensor(skip[:, :], skip[:, :], t2[:, :], ALU.add))
            go(v.tensor_copy(at_i[:, :], end[:, :]))
            v.sem_inc(S["got"], 1)
            go(v.scalar_tensor_tensor(out=t1[:, :], in0=skip[:, :], scalar=float(ENTRIES), in1=end[:, :], op0=ALU.mult, op1=ALU.add))
            go(v.tensor_copy(to_i[:, :], t1[:, :]))
            five = lambda ap: ap.unsqueeze(2).broadcast_to([P, HEADS, EXPERTS])
            go(v.tensor_copy(z[:, 0, 0:16].rearrange("p (h x) -> p h x", x=EXPERTS), five(zlast[:, 20:24])))
            go(v.tensor_copy(z[:, 0, 16:20], zlast[:, 20:24]))
            go(v.tensor_copy(z[:, 1, :], zlast[:, 0:20]))
            go(v.tensor_tensor(t2[:, :], last_seg[:, :], prev_seg[:, :], ALU.not_equal))
            go(v.tensor_scalar(z[:, 2, :], z[:, 0, :], 0.0, t2[:, :], ALU.mult, ALU.add))
            go(v.tensor_scalar(z[:, 2, :], z[:, 2, :], -BIG, None, ALU.mult))
            v.sem_inc(S["c2"], 1)
            v.wait_ge(pe_s, 4)
            go(v.tensor_copy(zt[:, :, :], c_ps[0:CH, 0:3*P].rearrange("c (i p) -> c i p", p=P)))
            go(v.memset(mm[:, 0:1], -BIG))
            go(v.memset(ss[:, 0:1], 0.0))
            go(v.tensor_tensor_scan(mm[:, 1:P+1], zt[:, 2, :], zt[:, 0, :], mm[:, 0:1], ALU.add, ALU.max))
            go(v.tensor_tensor(dd[:, 0, :], mm[:, 0:P], zt[:, 2, :], ALU.add))
            go(v.tensor_tensor(dd[:, 0, :], dd[:, 0, :], mm[:, 1:P+1], ALU.subtract))
            go(v.tensor_tensor(dd[:, 1, :], zt[:, 0, :], mm[:, 1:P+1], ALU.subtract))
            v.sem_inc(S["act"], 1)
            v.wait_ge(S["act"], 2)
            go(v.tensor_tensor(ww[:, :], ee[:, 1, :], zt[:, 1, :], ALU.mult))
            go(v.tensor_tensor_scan(ss[:, 1:P+1], ee[:, 0, :], ww[:, :], ss[:, 0:1], ALU.mult, ALU.add))
            v.sem_inc(S["c2"], 1)
            v.wait_ge(pe_s, 5)
            go(v.tensor_copy(cin[:, 0, :], c_ps[:, 384:384+CH]))
            go(v.tensor_copy(cin[:, 1, :], c_ps[:, 448:448+CH]))
            v.wait_ge(S["put"], 16)
            go(v.tensor_copy(rm[:, 0:16].rearrange("p (h x) -> p h x", x=EXPERTS), five(row[:, 20:24])))
            go(v.tensor_copy(rm[:, 16:20], row[:, 20:24]))
            go(v.tensor_tensor(nm[:, :], rm[:, :], cin[:, 0, :], ALU.max))
            go(v.tensor_tensor(d2[:, 0, :], rm[:, :], nm[:, :], ALU.subtract))
            go(v.tensor_tensor(d2[:, 1, :], cin[:, 0, :], nm[:, :], ALU.subtract))
            v.sem_inc(S["act"], 1)
            v.wait_ge(S["act"], 4)
            go(v.tensor_tensor(new[:, 0:20], row[:, 0:20], e2[:, 0, :], ALU.mult))
            go(v.tensor_tensor(cin[:, 1, :], cin[:, 1, :], e2[:, 1, :], ALU.mult))
            go(v.tensor_tensor(new[:, 0:20], new[:, 0:20], cin[:, 1, :], ALU.add))
            go(v.tensor_copy(new[:, 20:24], nm[:, 16:20]))
            v.sem_inc(S["got"], 1)

            def indices(k, at, turn):
                if not isinstance(k, int) or k >= 2:
                    v.wait_ge(S["tg%d" % (at % 2)], 16 * PER * (at // 2) + 16 * PER * turn)
                v.tensor_copy(tidx[:, at % 2, :], pos_i[:, bass.ds(k * PER, PER)]).then_inc(S["idx"], 1)
            def body(k, at, turn):
                if not isinstance(k, int) or k < TURNS:
                    indices(k, at, turn)
                if not isinstance(k, int) or k >= 1:
                    j, q = k - 1, (at - 1) % 2
                    v.wait_ge(S["tg%d" % q], 16 * PER * ((at - 1) // 2 + 1) + 16 * PER * turn)
                    need(v, S["agg"], j)
                    v.tensor_scalar(tsum[:, q, :, :], trow[:, q, :, 16:20], 1e-16, None, ALU.add).then_inc(S["dn"], 1)
                    v.wait_ge(S["dn"], 2 * j + 1)
                    v.reciprocal(trec[:, q, :, :], tsum[:, q, :, :]).then_inc(S["dn"], 1)
                    v.wait_ge(S["dn"], 2 * j + 2)
                    v.tensor_tensor(agg[:, bass.ds(half * HIS + j * PER, PER), :].rearrange("p b (h x) -> p b h x", x=EXPERTS), trow[:, q, :, 0:16].rearrange("p b (h x) -> p b h x", x=EXPERTS),
                                    trec[:, q, :, :].unsqueeze(3).broadcast_to([P, PER, HEADS, EXPERTS]), ALU.mult).then_inc(S["agg"], 1)
            rounds(v, 2, TURNS + 1, 1, 2, body)

def gates(nc, agg, io, parts, name):
    with ExitStack() as ctx:
        def sb(n, shape, dt=F32): return ctx.enter_context(nc.sbuf_tensor(f"{name}_{n}", shape, dt))
        def sem(n): return ctx.enter_context(nc.semaphore(f"{name}_{n}"))
        D = HEADS * EXPERTS
        con = sb("con", [P, 3, D]); eps = sb("eps", [P, 1])
        cen = sb("cen", [P, HIS, D]); sq = sb("sq", [P, HIS, D])
        mu = sb("mu", [P, HIS]); var = sb("var", [P, HIS]); sd = sb("sd", [P, HIS]); rs = sb("rs", [P, HIS])
        sc = sb("sc", [P, HIS, EXPERTS]); won = sb("won", [P, HIS, EXPERTS]); cmp_ = sb("cmp", [P, HIS, EXPERTS]); top = sb("top", [P, HIS])
        ex = sb("ex", [P, HIS, EXPERTS]); g = sb("g", [P, HIS, EXPERTS])
        ld, dv, act_s, cst = ctx.enter_context(semaphores(nc, name, "ld dv act cst")).values()
        over = lambda ap, d: ap.unsqueeze(2).broadcast_to([P, HIS, d])
        row = lambda i: con[:, i, :].unsqueeze(1).broadcast_to([P, HIS, D])
        with nc.Block() as block:
            @block.sync
            def _(sp):
                for i, n in enumerate(("b_gat", "ln_gamma", "ln_beta")):
                    sp.dma_start(con[:, i, :], io[n].rearrange("(a d) -> a d", a=1).broadcast_to([P, D])).then_inc(ld, 16)
            @block.gpsimd
            def _(pool):
                pool.memset(eps[:, :], 1e-5).then_inc(cst, 1)
            @block.scalar
            def _(act):
                act.wait_ge(cst, 1)
                act.wait_ge(act_s, 1)
                act.activation(sd[:, :], var[:, :], ACT.Sqrt, bias=eps[:, :], scale=1.0 / D).then_inc(act_s, 1)
                act.wait_ge(act_s, 3)
                act.activation(ex[:, :, :], ex[:, :, :], ACT.Exp).then_inc(act_s, 1)
            @block.vector
            def _(v):
                n = [0]
                def go(i):
                    n[0] += 1
                    i.then_inc(dv, 1)
                    v.wait_ge(dv, n[0])
                v.wait_ge(ld, 48)
                go(v.tensor_tensor(cen[:, :, :], agg, row(0), ALU.add))
                go(v.reduce_sum(mu[:, :], cen[:, :, :], axis=AX.X))
                go(v.tensor_scalar(mu[:, :], mu[:, :], 1.0 / D, None, ALU.mult))
                go(v.tensor_tensor(cen[:, :, :], cen[:, :, :], over(mu[:, :], D), ALU.subtract))
                go(v.tensor_tensor(sq[:, :, :], cen[:, :, :], cen[:, :, :], ALU.mult))
                go(v.reduce_sum(var[:, :], sq[:, :, :], axis=AX.X))
                v.sem_inc(act_s, 1)
                v.wait_ge(act_s, 2)
                go(v.reciprocal(rs[:, :], sd[:, :]))
                go(v.tensor_tensor(cen[:, :, :], cen[:, :, :], over(rs[:, :], D), ALU.mult))
                go(v.tensor_tensor(cen[:, :, :], cen[:, :, :], row(1), ALU.mult))
                go(v.tensor_tensor(cen[:, :, :], cen[:, :, :], row(2), ALU.add))
                go(v.reduce_sum(sc[:, :, :], cen[:, :, :].rearrange("p b (h e) -> p b e h", e=EXPERTS), axis=AX.X))
                go(v.tensor_scalar(sc[:, :, :], sc[:, :, :], 1.0 / HEADS, None, ALU.mult))
                go(v.memset(won[:, :, :], 0.0))
                for d in range(1, EXPERTS):
                    lo, hi = slice(0, EXPERTS - d), slice(d, EXPERTS)
                    for mine, other, op in ((lo, hi, ALU.is_ge), (hi, lo, ALU.is_gt)):
                        go(v.tensor_tensor(cmp_[:, :, mine], sc[:, :, mine], sc[:, :, other], op))
                        go(v.tensor_tensor(won[:, :, mine], won[:, :, mine], cmp_[:, :, mine], ALU.add))
                go(v.tensor_scalar(won[:, :, :], won[:, :, :], 2.0, None, ALU.is_ge))
                go(v.tensor_reduce(top[:, :], sc[:, :, :], AX.X, ALU.max))
                go(v.tensor_tensor(ex[:, :, :], sc[:, :, :], over(top[:, :], EXPERTS), ALU.subtract))
                v.sem_inc(act_s, 1)
                v.wait_ge(act_s, 4)
                go(v.tensor_tensor(ex[:, :, :], ex[:, :, :], won[:, :, :], ALU.mult))
                go(v.reduce_sum(mu[:, :], ex[:, :, :], axis=AX.X))
                go(v.reciprocal(rs[:, :], mu[:, :]))
                go(v.tensor_tensor(g[:, :, :], ex[:, :, :], over(rs[:, :], EXPERTS), ALU.mult))
                split = parts.rearrange("p b (i j e) -> p b i j e", j=PARTS, e=EXPERTS)
                for j in range(PARTS):
                    go(v.tensor_copy(split[:, :, 0, j, :], g[:, :, :]))
                    if j < PARTS - 1:
                        go(v.tensor_tensor(g[:, :, :], g[:, :, :], split[:, :, 0, j, :], ALU.subtract))
                for i in range(1, PARTS):
                    go(v.tensor_copy(split[:, :, i, :, :], split[:, :, 0, :, :]))

class Experts:
    AHEAD = 3
    PREPARED = 25
    WEIGHTS = 16 * (3 + PARTS * PARTS)
    def __init__(self, nc, ctx, io, norm_d, mid_d, out_d, parts, half, name):
        self.nc, self.io, self.half, self.norm_d, self.mid_d, self.out_d, self.parts = nc, io, half, norm_d, mid_d, out_d, parts
        def sb(n, shape, dt=F32): return ctx.enter_context(nc.sbuf_tensor(f"{name}_{n}", shape, dt))
        def ps(n, shape, dt=F32): return ctx.enter_context(nc.psum_tensor(f"{name}_{n}", shape, dt))
        self.S = ctx.enter_context(semaphores(nc, name, "w prep lane ident ld0 ld1 ld2 ld3 gst gtp gt w1 gel sel mul w2 fin go st0 st1 st2 st3"))
        self.w1 = sb("w1", [P, EXPERTS, HID * P]); self.w2 = sb("w2", [P, EXPERTS, HID, P]); self.b1 = sb("b1", [P, EXPERTS, HID])
        self.b2f = sb("b2f", [G, P]); self.b2t = sb("b2t", [G, P]); self.b2p = sb("b2p", [G, PARTS, P], BF16); self.b2 = sb("b2", [G, P], BF16)
        self.lane_i = sb("lane_i", [G, 1], I32); self.lane = sb("lane", [G, 2], I32); self.mask = sb("mask", [G, 8]); self.lf = sb("lf", [G, 2])
        self.choose = sb("choose", [G, EXPERTS, P], BF16); self.onesb = sb("onesb", [G, P], BF16)
        self.ident = sb("ident", [P, P], BF16)
        self.tn = sb("tn", [P, 4, TOK]); self.xm = sb("xm", [P, 4, TOK]); self.o = sb("o", [P, 4, TOK])
        self.gst = sb("gst", [P, 2, BLKS, G], BF16); self.gT = sb("gT", [G, 2, TOK], BF16)
        self.hh = sb("hh", [P, 2, TOK]); self.hs = sb("hs", [P, 2, TOK])
        self.hid_ps = ps("hid_ps", [P, 2, TOK]); self.gate_ps = ps("gate_ps", [P, 2, TOK]); self.out_ps = ps("out_ps", [P, 2, TOK])
        self.gT_ps = ps("gT_ps", [P, 2 * TOK], BF16)
    def tile(self, d, at, turn, unroll, ahead=0):
        n = at + ahead
        img = self.half * (TOKEN_TILES // 2) + n // 2 + turn * (unroll // 2)
        return d[img, :, (n % 2) * TOK:(n % 2 + 1) * TOK]
    def start_sync(self, sp):
        S, io = self.S, self.io
        sp.dma_start(self.w1[:, :, :], io["W1"].rearrange("e c h -> c e h")).then_inc(S["w"], 16)
        sp.dma_start(self.w2[:, :, :, :], io["W2"].rearrange("e (f h) c -> h e f c", h=P)).then_inc(S["w"], 16)
        with self.nc.allow_non_contiguous_dma("the hidden biases, once, one to a partition"):
            sp.dma_start(self.b1[:, :, :], io["b1"].rearrange("e (f h) -> h e f", h=P)).then_inc(S["w"], 16)
        for r in range(PARTS * PARTS):
            sp.dma_start(self.b2f[r*EXPERTS:(r+1)*EXPERTS, :], io["b2"]).then_inc(S["w"], 16)
        for k in range(self.AHEAD):
            self.load(sp, k, 0, 4, 0)
    def load(self, sp, at, turn, unroll, ahead):
        u = (at + ahead) % 4
        sp.dma_start(self.tn[:, u, :], self.tile(self.norm_d, at, turn, unroll, ahead)).then_inc(self.S["ld%d" % u], 16)
        sp.dma_start(self.xm[:, u, :], self.tile(self.mid_d, at, turn, unroll, ahead)).then_inc(self.S["ld%d" % u], 16)
    def start_gpsimd(self, pool):
        S = self.S
        pool.iota(self.lane_i[:, :], [[0, 1]], base=0, channel_multiplier=1)
        pool.memset(self.onesb[:, :], 1.0)
        pool.memset(self.ident[:, :], 0.0).then_inc(S["lane"], 1)
        pool.wait_ge(S["lane"], 1)
        pool.affine_select(out=self.ident[:, :], in_=self.ident[:, :], compare_op=ALU.not_equal, fill=1.0, base=0, pattern=[[-1, P]], channel_multiplier=1).then_inc(S["ident"], 1)
    def start_vector(self, v):
        S = self.S
        n = [0]
        def go(i):
            n[0] += 1
            i.then_inc(S["prep"], 1)
            v.wait_ge(S["prep"], n[0])
        v.wait_ge(S["lane"], 1)
        v.wait_ge(S["w"], self.WEIGHTS)
        GE = PARTS * EXPERTS
        go(v.tensor_copy(self.lf[:, 0:1], self.lane_i[:, :]))
        go(v.tensor_scalar(self.lane[:, 0:1], self.lane_i[:, :], EXPERTS - 1, None, ALU.bitwise_and))
        go(v.tensor_copy(self.lf[:, 1:2], self.lane[:, 0:1]))
        m = self.mask
        go(v.tensor_scalar(m[:, 0:1], self.lf[:, 0:1], float(GE), None, ALU.is_lt))
        go(v.tensor_scalar(m[:, 2:3], self.lf[:, 0:1], float(2 * GE), None, ALU.is_ge))
        go(v.tensor_scalar(m[:, 1:2], m[:, 0:1], -1.0, 1.0, ALU.mult, ALU.add))
        go(v.tensor_tensor(m[:, 1:2], m[:, 1:2], m[:, 2:3], ALU.subtract))
        for e in range(EXPERTS):
            go(v.tensor_scalar(m[:, 4+e:5+e], self.lf[:, 1:2], float(e), m[:, 0:1], ALU.is_equal, ALU.mult))
            go(v.tensor_scalar(self.choose[:, e, :], self.onesb[:, :], m[:, 4+e:5+e], None, ALU.mult))
        for i in range(PARTS):
            go(v.tensor_copy(self.b2p[:, i, :], self.b2f[:, :]))
            go(v.tensor_tensor(self.b2f[:, :], self.b2f[:, :], self.b2p[:, i, :], ALU.subtract))
        go(v.tensor_scalar(self.b2t[:, :], self.b2p[:, 0, :], m[:, 0:1], None, ALU.mult))
        for i in (1, 2):
            go(v.scalar_tensor_tensor(out=self.b2t[:, :], in0=self.b2p[:, i, :], scalar=m[:, i:i+1], in1=self.b2t[:, :], op0=ALU.mult, op1=ALU.add))
        go(v.tensor_copy(self.b2[:, :], self.b2t[:, :]))
        assert n[0] == self.PREPARED
        self.stage(v, 0, 0)
        self.turned(v, 0, 0)
    def stage(self, v, k, at):
        need(v, self.S["gtp"], k - 1)
        v.tensor_copy(self.gst[:, at % 2, :, :], self.parts[:, bass.ds(k * BLKS, BLKS), :]).then_inc(self.S["gst"], 1)
    def turned(self, v, k, at):
        v.wait_ge(self.S["gtp"], k + 1)
        need(v, self.S["w2"], 8 * (k - 1))
        v.tensor_copy(self.gT[:, at % 2, :], self.gT_ps[0:G, 0:TOK]).then_inc(self.S["gt"], 1)
    def turn_gates(self, pe, k, at):
        need(pe, self.S["gst"], k + 1)
        need(pe, self.S["gt"], k)
        if not isinstance(k, int):
            pe.sem_inc(self.S["go"], 1)
        for b in range(BLKS):
            last = pe.transpose(self.gT_ps[0:G, b*P:(b+1)*P], self.gst[:, at % 2, b, :], self.ident[:, :])
        last.then_inc(self.S["gtp"], 1)
    def first_product(self, pe, k, at, s):
        S = self.S
        need(pe, S["gel"], 8 * k + s - 1)
        e, f = s // HID, s % HID
        pe.matmul(self.hid_ps[:, s % 2, :], self.w1[:, e, f*P:(f+1)*P], self.tn[:, at % 4, :], start=True, stop=True).then_inc(S["w1"], 1)
    def choose_gate(self, pe, k, at, e):
        S = self.S
        need(pe, S["gt"], k + 1)
        need(pe, S["mul"], 8 * k + 2 * e - 2)
        pe.matmul(self.gate_ps[:, e % 2, :], self.choose[:, e, :], self.gT[:, at % 2, :], start=True, stop=True).then_inc(S["sel"], 1)
    def start_tensor(self, pe):
        S = self.S
        pe.wait_ge(S["ident"], 1)
        pe.wait_ge(S["w"], self.WEIGHTS)
        self.turn_gates(pe, 0, 0)
        pe.wait_ge(S["ld0"], 32)
        for s in range(2):
            self.first_product(pe, 0, 0, s)
        pe.wait_ge(S["prep"], self.PREPARED)
        self.choose_gate(pe, 0, 0, 0)
    def sync(self, sp, k, at, turn, unroll):
        S = self.S
        if not isinstance(k, int) or k >= 1:
            q = (at - 1) % 4
            need(sp, S["fin"], k)
            sp.dma_start(self.tile(self.out_d, at, turn, unroll, -1), self.o[:, q, :]).then_inc(S["st%d" % q], 16)
            if not isinstance(k, int) or k + 2 < TOKEN_TILES:
                if not isinstance(k, int) or k >= 1:
                    self.load(sp, at, turn, unroll, 2)
    def end_sync(self, sp):
        for q in range(4):
            sp.wait_ge(self.S["st%d" % q], 16 * TOKEN_TILES // 4)
    def tensor(self, pe, k, at, turn, unroll):
        S = self.S
        if isinstance(k, int) and k >= TOKEN_TILES:
            return
        more = not isinstance(k, int) or k + 1 < TOKEN_TILES
        need(pe, S["fin"], k - 1)
        pe.matmul(self.out_ps[:, at % 2, :], self.b2[:, :], self.gT[:, at % 2, :], start=True, stop=False)
        for s in range(8):
            e, f = s // HID, s % HID
            need(pe, S["mul"], 8 * k + s + 1)
            pe.matmul(self.out_ps[:, at % 2, :], self.w2[:, e, f, :], self.hs[:, s % 2, :], start=False, stop=(s == 7)).then_inc(S["w2"], 1)
            if s + 2 < 8:
                self.first_product(pe, k, at, s + 2)
            elif more:
                if s == 6:
                    pe.wait_ge(S["ld%d" % ((at + 1) % 4)], 32 * ((at + 1) // 4 + 1) + 32 * (unroll // 4) * turn)
                self.first_product(pe, k + 1, at + 1, s - 6)
            if s % 2 == 0 and s < 6:
                self.choose_gate(pe, k, at, s // 2 + 1)
            if s == 3 and more:
                self.turn_gates(pe, k + 1, at + 1)
            if s == 7 and more:
                self.choose_gate(pe, k + 1, at + 1, 0)
    def scalar(self, act, k, at, turn, unroll):
        S = self.S
        if isinstance(k, int) and k >= TOKEN_TILES:
            return
        for s in range(8):
            need(act, S["w1"], 8 * k + s + 1)
            need(act, S["mul"], 8 * k + s - 1)
            act.activation(self.hh[:, s % 2, :], self.hid_ps[:, s % 2, :], ACT.Gelu, bias=self.b1[:, s // HID, s % HID:s % HID + 1]).then_inc(S["gel"], 1)
    def vector(self, v, k, at, turn, unroll):
        S = self.S
        tile = not isinstance(k, int) or k < TOKEN_TILES
        more = not isinstance(k, int) or k + 1 < TOKEN_TILES
        for s in range(8):
            if tile:
                need(v, S["gel"], 8 * k + s + 1)
                need(v, S["sel"], 4 * k + s // HID + 1)
                need(v, S["w2"], 8 * k + s - 1)
                v.tensor_tensor(self.hs[:, s % 2, :], self.hh[:, s % 2, :], self.gate_ps[:, (s // HID) % 2, :], ALU.mult).then_inc(S["mul"], 1)
            if s == 1 and (not isinstance(k, int) or k >= 1):
                q = (at - 1) % 4
                need(v, S["w2"], 8 * k)
                need(v, S["ld%d" % q], 32 * ((at - 1) // 4 + 1) + 32 * (unroll // 4) * turn)
                need(v, S["st%d" % q], 16 * ((at - 1) // 4) + 16 * (unroll // 4) * turn)
                v.tensor_tensor(self.o[:, q, :], self.xm[:, q, :], self.out_ps[:, (at - 1) % 2, :], ALU.add).then_inc(S["fin"], 1)
            if s == 2 and more:
                self.stage(v, k + 1, at + 1)
            if s == 5 and more:
                self.turned(v, k + 1, at + 1)

def experts_alone(nc, io, norm_d, mid_d, out_d, parts, half, name):
    with ExitStack() as ctx:
        x = Experts(nc, ctx, io, norm_d, mid_d, out_d, parts, half, name)
        with nc.Block() as block:
            @block.vector
            def _(v):
                x.start_vector(v)
                rounds(v, 6, TOKEN_TILES + 1, 3, 4, lambda k, at, turn: x.vector(v, k, at, turn, 4))
            @block.sync
            def _(sp):
                x.start_sync(sp)
                rounds(sp, 6, TOKEN_TILES + 1, 3, 4, lambda k, at, turn: x.sync(sp, k, at, turn, 4))
                x.end_sync(sp)
            @block.gpsimd
            def _(pool):
                x.start_gpsimd(pool)
            @block.tensor
            def _(pe):
                x.start_tensor(pe)
                rounds(pe, 6, TOKEN_TILES + 1, 3, 4, lambda k, at, turn: x.tensor(pe, k, at, turn, 4))
            @block.scalar
            def _(act):
                act.wait_ge(x.S["w"], x.WEIGHTS)
                rounds(act, 6, TOKEN_TILES + 1, 3, 4, lambda k, at, turn: x.scalar(act, k, at, turn, 4))
def program(nc, io, out):
    IMAGES, C, H, W = io["x"].shape
    M = IMAGES * H * W
    keys = [nc.dram_tensor(f"keys{h}", [1 + ENTRIES + TAIL], F32, kind="Internal").ap() for h in range(2)]
    rows = nc.dram_tensor("rows", [M, ROW], F32, kind="Internal").ap()
    res = [nc.dram_tensor(f"sums{h}", [ENTRIES, ROW], F32, kind="Internal").ap() for h in range(2)]
    mid = nc.dram_tensor("mid", [IMAGES, C, H * W], F32, kind="Internal").ap()
    norm = nc.dram_tensor("norm", [IMAGES, C, H * W], F32, kind="Internal").ap()
    out_d = out.rearrange("b c h w -> b c (h w)")
    edges = io["edge_index"]
    with ExitStack() as ctx:
        agg = ctx.enter_context(nc.sbuf_tensor("agg", [P, M // P, 16], F32))
        gathers = lambda name: ctx.enter_context(nc.semaphore(name))
        flag = ctx.enter_context(nc.sbuf_tensor("flag", [1, 1], I32))
        sorter(nc, edges, keys[0], 0, flag[:, :])
        mixer(nc, io, dict(xmid=mid, norm=norm, rows=rows.rearrange("(b j p) r -> b p j r", j=H*W//P, p=P), agg=agg[:, :, :], ROW=ROW))
        high = nc.values_load(flag[0:1, 0:1], min_val=0, max_val=1)
        with nc.If(high):
            sorter(nc, edges, keys[1], 1, None)
            attention(nc, edges, keys[1], rows, res[1], agg[:, :, :], 1, gathers)
        with ExitStack() as c1:
            parts = c1.enter_context(nc.sbuf_tensor("parts1", [P, HIS, G], BF16))
            gates(nc, agg[:, HIS:2*HIS, :], io, parts[:, :, :], "gates1")
            attention(nc, edges, keys[0], rows, res[0], agg[:, :, :], 0, gathers,
                      lambda c: Experts(nc, c, io, norm, mid, out_d, parts[:, :, :], 1, "ex1"))
        with ExitStack() as c1:
            parts = c1.enter_context(nc.sbuf_tensor("parts0", [P, HIS, G], BF16))
            gates(nc, agg[:, 0:HIS, :], io, parts[:, :, :], "gates0")
            experts_alone(nc, io, norm, mid, out_d, parts[:, :, :], 0, "ex0")


_INS = ['x', 'L0_conv_w1', 'L0_conv_w2', 'L0_conv_b11', 'L0_conv_b12', 'L0_conv_b13', 'L0_conv_b21', 'L0_conv_b22', 'L0_conv_b23',
        'L0_conv_a1', 'L0_conv_a2', 'L0_conv_g1m', 'L0_conv_be1m', 'L0_conv_m1m', 'L0_conv_v1m', 'L0_conv_g2m', 'L0_conv_be2m',
        'L0_conv_m2m', 'L0_conv_v2m', 'L0_ffn_W_gat', 'L0_ffn_att_src', 'L0_ffn_att_dst', 'L0_ffn_b_gat', 'L0_ffn_ln_gamma',
        'L0_ffn_ln_beta', 'L0_ffn_W1', 'L0_ffn_b1', 'L0_ffn_W2', 'L0_ffn_b2', 'L0_ffn_edge_index']


def kernel(**inputs):
    import numpy as _np
    import concourse.bacc as _bacc
    from concourse import mybir as _mybir
    from concourse.bass_utils import run_bass_kernel_spmd as _run

    nc = _bacc.Bacc("TRN2", target_bir_lowering=False, num_devices=1)
    arrays, io = {}, {}
    for name in _INS:
        a = _np.ascontiguousarray(inputs[name])
        arrays[f"in_{name}_dram"] = a
        short = name.replace("L0_conv_", "").replace("L0_ffn_", "")
        io[short] = nc.dram_tensor(f"in_{name}_dram", a.shape, _mybir.dt.from_np(a.dtype), kind="ExternalInput").ap()
    shape = inputs["x"].shape
    out = nc.dram_tensor("out_0_dram", shape, _mybir.dt.float32, kind="ExternalOutput").ap()
    program(nc, io, out)
    r = _run(nc, [arrays], core_ids=[0])
    return r.results[0]["out_0_dram"]
```

```python
from contextlib import ExitStack, contextmanager

import concourse.bass as bass
from concourse import mybir

F32 = mybir.dt.float32
I32 = mybir.dt.int32
BF16 = mybir.dt.bfloat16
ALU = mybir.AluOpType
ACT = mybir.ActivationFunctionType
AX = mybir.AxisListType

P = 128
EDGES = 524288
HALF = 32768
HEADS, EXPERTS = 4, 4

EDGE_COLS = EDGES // P
PART_BITS, COL_BITS = 7, 12
TURN_CHUNKS = 4
HEAD_COLS = HALF // P
LEAST = 128
SHIFT = HALF // 2 - LEAST
FLIP = 2 * SHIFT

ENTRIES = EDGES + HALF
RUN = ENTRIES // P
TAIL = RUN
CHUNKS = 64
COLS = RUN // CHUNKS
ROW = 24
BIG = 1e30
HIS = HALF // P
COUNT_TILES = EDGE_COLS // CHUNKS
RING = 8

HID = 2
PARTS = 3
G = PARTS * PARTS * EXPERTS
TOK = 512
BLKS = TOK // P
TOKEN_TILES = HALF // TOK



def need(eng, sem, count):
    if isinstance(count, int) and count <= 0:
        return
    eng.wait_ge(sem, count)

def rounds(eng, first, last, tail, unroll, body):
    turns = (last - first - tail) // unroll
    for k in range(first):
        body(k, k, 0)
    with eng.Fori(0, turns) as turn:
        for at in range(first, first + unroll):
            body(turn * unroll + at, at, turn)
    for k in range(first + turns * unroll, last):
        body(k, k, 0)

@contextmanager
def semaphores(nc, prefix, names):
    with ExitStack() as stack:
        signals = {n: stack.enter_context(nc.semaphore(f"{prefix}_{n}")) for n in names.split()}
        yield signals
        with nc.Block() as block:
            @block.gpsimd
            def _(pool):
                for s in signals.values():
                    pool.sem_clear(s)

def mixer(nc, io, tables):
    x, w1, w2 = io["x"], io["w1"], io["w2"]
    IMAGES, C, H, W = x.shape
    PIX = H * W
    BLK = PIX // P
    HALVES = PIX // 512
    TAPS = 9
    PADW = W + 2
    LEAD, WIDE = 2, 6
    LAST = IMAGES + 5
    FIRST, TAIL_ROUNDS = 8, 7
    x_d = x.rearrange("b c h w -> b c (h w)")
    xmid_d, norm_d, rows_d, agg = tables["xmid"], tables["norm"], tables["rows"], tables["agg"]
    with ExitStack() as ctx:
        def sb(name, shape, dt=F32): return ctx.enter_context(nc.sbuf_tensor(f"m_{name}", shape, dt))
        def ps(name, shape, dt=F32): return ctx.enter_context(nc.psum_tensor(f"m_{name}", shape, dt))
        NAMES = ["b11", "b12", "b13", "b21", "b22", "b23", "a1", "a2", "g1m", "be1m", "m1m", "v1m", "g2m", "be2m", "m2m", "v2m"]
        par = sb("par", [P, len(NAMES)])
        col = {n: par[:, i:i+1] for i, n in enumerate(NAMES)}
        der = sb("der", [P, 16])
        weight_sum, deviation_v, gain, scale, shift, one_less_slope = (der[:, 2*i:2*i+2] for i in range(6))
        sign_shift2, relu_shift2, last_shift, excess_slope1 = (der[:, i:i+1] for i in (12, 13, 14, 15))
        eps = sb("eps", [P, 2])
        w1f = sb("w1f", [P, C*TAPS]); w2f = sb("w2f", [P, C])
        w1s = sb("w1s", [P, TAPS, C], BF16); w2s = sb("w2s", [P, C], BF16)
        w1T = sb("w1T", [P, TAPS, C], BF16); w2T = sb("w2T", [P, C], BF16)
        wabs = sb("wabs", [P, C*TAPS])
        identb = sb("identb", [P, P], BF16); ident = sb("ident", [P, P])
        wg = sb("wg", [P, ROW]); att = sb("att", [P, 32]); wtmp = sb("wtmp", [P, 32])
        xin = sb("xin", [P, WIDE, PIX])
        stats1 = sb("stats1", [P, BLK, 6]); mv1 = sb("mv1", [P, BLK, 2]); stats2 = sb("stats2", [P, BLK, 6]); mv2 = sb("mv2", [P, BLK, 2])
        sd1 = sb("sd1", [P, BLK]); rs1 = sb("rs1", [P, BLK]); nb1 = sb("nb1", [P, BLK])
        sd2 = sb("sd2", [P, BLK]); rs2 = sb("rs2", [P, BLK]); nb2 = sb("nb2", [P, BLK])
        xn = sb("xn", [P, 2, PIX]); xt1 = sb("xt1", [P, PIX]); xt2 = sb("xt2", [P, PIX])
        sg1 = sb("sg1", [P, 2, PADW, PADW], BF16); sg2 = sb("sg2", [P, PIX], BF16)
        z1 = sb("z1", [P, PIX]); neg1 = sb("neg1", [P, PIX]); out1 = sb("out1", [P, 2, PIX])
        z2 = sb("z2", [P, PIX]); neg2 = sb("neg2", [P, PIX]); out2 = sb("out2", [P, PIX])
        xm = sb("xm", [P, 2, PIX]); tn = sb("tn", [P, 2, PIX]); rw = sb("rw", [P, 2, BLK, ROW])
        ln1_ps = ps("ln1_ps", [P, 2, PIX]); conv_ps = ps("conv_ps", [P, PIX]); ln2_ps = ps("ln2_ps", [P, PIX])
        S = ctx.enter_context(semaphores(nc, "m", "par w params const ident dp sdv wsg wT x0 x1 x2 x3 x4 x5 xT1 st1 bn1 sd1 rc1 rs1 xt1 xnT1 xn sg1 conv z1 neg1 out1 sg2 "
             "conv2 z2 neg2 out2 xm xT2 st2 bn2 sd2 rc2 rs2 xt2 xnT2 tn rows rw stx0 stx1 stt0 stt1 str0 str1 xs hold still"))
        block = ctx.enter_context(nc.Block())
        def there(k, lag):
            return not isinstance(k, int) or 0 <= k - lag < IMAGES
        def after(eng, sem, images):
            need(eng, sem, min(images, IMAGES) if isinstance(images, int) else images)
        def stored(at, turn, lag):
            return 16 * ((at - lag) // 2) + 16 * (WIDE // 2) * turn

        @block.sync
        def _(sp):
            for i, n in enumerate(NAMES):
                sp.dma_start(col[n], io[n].rearrange("(p a) -> p a", a=1)).then_inc(S["par"], 16)
            sp.dma_start(w1f[:, :], w1.rearrange("o i a b -> o (i a b)")).then_inc(S["w"], 16)
            sp.dma_start(w2f[:, :], w2.rearrange("o i a b -> o (i a b)")).then_inc(S["w"], 16)
            sp.dma_start(wg[:, 0:16], io["W_gat"]).then_inc(S["w"], 16)
            sp.dma_start(att[:, 0:16], io["att_src"].rearrange("(a h) e -> a (h e)", a=1).broadcast_to([P, 16])).then_inc(S["w"], 16)
            sp.dma_start(att[:, 16:32], io["att_dst"].rearrange("(a h) e -> a (h e)", a=1).broadcast_to([P, 16])).then_inc(S["w"], 16)
            for k in range(LEAD):
                sp.dma_start(xin[:, k, :], x_d[k, :, :]).then_inc(S["x%d" % k], 16)

            def body(k, at, turn):
                if not isinstance(k, int) or k + LEAD < IMAGES:
                    after(sp, S["xm"], k - 3)
                    u = (at + LEAD) % WIDE
                    sp.dma_start(xin[:, u, :], x_d[k + LEAD, :, :]).then_inc(S["x%d" % u], 16)
                if there(k, 5):
                    q = (at - 5) % 2
                    after(sp, S["tn"], k - 4)
                    sp.dma_start(norm_d[k - 5, :, :], tn[:, q, :]).then_inc(S["stt%d" % q], 16)
                    after(sp, S["rw"], k - 4)
                    sp.dma_start(rows_d[k - 5], rw[:, q, :, :]).then_inc(S["str%d" % q], 16)
                if there(k, 3):
                    q = (at - 3) % 2
                    after(sp, S["xm"], k - 2)
                    sp.dma_start(xmid_d[k - 3, :, :], xm[:, q, :]).then_inc(S["stx%d" % q], 16)
            rounds(sp, FIRST, LAST, TAIL_ROUNDS, WIDE, body)
            for n in ("stx", "stt", "str"):
                for q in range(2):
                    sp.wait_ge(S[n + str(q)], 16 * IMAGES // 2)

        @block.gpsimd
        def _(pool):
            pool.memset(identb[:, :], 0.0)
            pool.memset(ident[:, :], 0.0)
            pool.memset(sg1[:, :, :, :], 0.0)
            pool.memset(eps[:, 0:1], 1e-6)
            pool.memset(eps[:, 1:2], 1e-5).then_inc(S["const"], 1)
            pool.wait_ge(S["const"], 1)
            for m in (identb, ident):
                last = pool.affine_select(out=m[:, :], in_=m[:, :], compare_op=ALU.not_equal, fill=1.0, base=0,
                                          pattern=[[-1, P]], channel_multiplier=1)
            last.then_inc(S["ident"], 1)
            pool.wait_ge(S["params"], 1)

            def body(k, at, turn):
                if there(k, 2):
                    after(pool, S["neg1"], k - 1)
                    after(pool, S["sg2"], k - 3)
                    after(pool, S["z2"], k - 3)
                    pool.tensor_tensor(out1[:, at % 2, :], neg1[:, :], z1[:, :], ALU.add).then_inc(S["out1"], 1)
                if there(k, 3):
                    q, u = (at - 3) % 2, (at - 3) % WIDE
                    after(pool, S["xT1"], k - 2)
                    pool.sem_inc(S["still"], 1)
                    pool.tensor_scalar(xin[:, u, :], xin[:, u, :], last_shift, None, ALU.add).then_inc(S["xs"], 1)
                    after(pool, S["xs"], k - 2)
                    after(pool, S["out2"], k - 2)
                    after(pool, S["xT2"], k - 4)
                    need(pool, S["stx%d" % q], stored(at, turn, 3))
                    pool.tensor_tensor(xm[:, q, :], out2[:, :], xin[:, u, :], ALU.add).then_inc(S["xm"], 1)
            rounds(pool, FIRST, LAST, TAIL_ROUNDS, WIDE, body)

        @block.tensor
        def _(pe):
            pe.wait_ge(S["ident"], 1)
            pe.wait_ge(S["wsg"], 2)
            wps = conv_ps[:, :].bitcast(BF16)
            for t in range(TAPS + 1):
                src = w1s[:, t, :] if t < TAPS else w2s[:, :]
                last = pe.transpose(wps[:, t*P:(t+1)*P], src, identb[:, :])
            last.then_inc(S["wT"], 1)
            pe.wait_ge(S["wT"], 3)
            pe.wait_ge(S["params"], 1)

            def turned(out, src, signal):
                for j in range(BLK):
                    last = pe.transpose(out[:, j*P:(j+1)*P], src[:, j*P:(j+1)*P], ident[:, :])
                last.then_inc(signal, 1)
            def body(k, at, turn):
                if there(k, 2):
                    after(pe, S["sg1"], k - 1)
                    after(pe, S["z1"], k - 2)
                    after(pe, S["z2"], k - 3)
                    rows_of = H // HALVES
                    for hf in range(HALVES):
                        for t in range(TAPS):
                            dy, dx = t // 3, t % 3
                            last = pe.matmul(conv_ps[:, hf*512:(hf+1)*512], w1T[:, t, :],
                                             sg1[:, at % 2, hf*rows_of+dy:hf*rows_of+dy+rows_of, dx:dx+W],
                                             start=(t == 0), stop=(t == TAPS - 1))
                    last.then_inc(S["conv"], 1)
                if there(k, 1):
                    after(pe, S["xt1"], k)
                    turned(ln1_ps[:, (at - 1) % 2, :], xt1[:, :], S["xnT1"])
                if there(k, 5):
                    after(pe, S["xt2"], k - 4)
                    turned(ln2_ps[:, :], xt2[:, :], S["xnT2"])
                if there(k, 0):
                    pe.wait_ge(S["x%d" % (at % WIDE)], 16 * (at // WIDE + 1) + 16 * turn)
                    after(pe, S["xn"], k - 1)
                    turned(ln1_ps[:, at % 2, :], xin[:, at % WIDE, :], S["xT1"])
                if there(k, 3):
                    after(pe, S["sg2"], k - 2)
                    after(pe, S["z1"], k - 1)
                    after(pe, S["z2"], k - 3)
                    for hf in range(HALVES):
                        last = pe.matmul(conv_ps[:, hf*512:(hf+1)*512], w2T[:, :], sg2[:, hf*512:(hf+1)*512], start=True, stop=True)
                    last.then_inc(S["conv2"], 1)
                if there(k, 5):
                    after(pe, S["tn"], k - 4)
                    for j in range(BLK):
                        last = pe.matmul(ln2_ps[:, j*ROW:(j+1)*ROW], tn[:, (at - 5) % 2, j*P:(j+1)*P], wg[:, :], start=True, stop=True)
                    last.then_inc(S["rows"], 1)
                if there(k, 4):
                    after(pe, S["xm"], k - 3)
                    after(pe, S["rw"], k - 4)
                    turned(ln2_ps[:, :], xm[:, at % 2, :], S["xT2"])
            rounds(pe, FIRST, LAST, TAIL_ROUNDS, WIDE, body)

        @block.vector
        def _(v):
            n = [0]
            def go(i):
                n[0] += 1
                i.then_inc(S["dp"], 1)
                v.wait_ge(S["dp"], n[0])
            v.wait_ge(S["par"], 16 * len(NAMES))
            v.wait_ge(S["w"], 80)
            go(v.scalar_tensor_tensor(out=wabs[:, :], in0=w1f[:, :], scalar=-1.0, in1=w1f[:, :], op0=ALU.mult, op1=ALU.max))
            go(v.reduce_sum(weight_sum[:, 0:1], wabs[:, :], axis=AX.X))
            go(v.scalar_tensor_tensor(out=wabs[:, 0:C], in0=w2f[:, :], scalar=-1.0, in1=w2f[:, :], op0=ALU.mult, op1=ALU.max))
            go(v.reduce_sum(weight_sum[:, 1:2], wabs[:, 0:C], axis=AX.X))
            v.wait_ge(S["sdv"], 2)
            go(v.reciprocal(gain, deviation_v))
            for s, (g, m, be, b2, a) in enumerate((("g1m", "m1m", "be1m", "b12", "a1"), ("g2m", "m2m", "be2m", "b22", "a2"))):
                inv, sc, sh, less = (t[:, s:s+1] for t in (gain, scale, shift, one_less_slope))
                go(v.tensor_tensor(inv, inv, col[g], ALU.mult))
                go(v.tensor_scalar(sc, weight_sum[:, s:s+1], 1.0 / (C * (TAPS if s == 0 else 1)), inv, ALU.mult, ALU.mult))
                go(v.tensor_tensor(sh, col[m], inv, ALU.mult))
                go(v.tensor_tensor(sh, col[be], sh, ALU.subtract))
                go(v.tensor_tensor(sh, sh, col[b2], ALU.add))
                go(v.tensor_scalar(less, col[a], -1.0, 1.0, ALU.mult, ALU.add))
            go(v.tensor_scalar(excess_slope1, one_less_slope[:, 0:1], -1.0, None, ALU.mult))
            go(v.tensor_tensor(sign_shift2, col["b13"], col["b21"], ALU.add))
            go(v.tensor_tensor(last_shift, col["b13"], shift[:, 1:2], ALU.add))
            go(v.tensor_scalar(relu_shift2, last_shift, -1.0, None, ALU.mult))
            go(v.tensor_tensor(last_shift, last_shift, col["b23"], ALU.add))
            for s in range(2):
                go(v.tensor_tensor(wtmp[:, 0:16], wg[:, 0:16], att[:, 16*s:16*s+16], ALU.mult))
                go(v.reduce_sum(wg[:, 16+4*s:20+4*s], wtmp[:, 0:16].rearrange("p (h e) -> p h e", e=4), axis=AX.X))
            v.wait_ge(S["wT"], 1)
            wps = conv_ps[:, :].bitcast(BF16)
            v.tensor_copy(w1T[:, :, :], wps[:, 0:TAPS*P].rearrange("p (t o) -> p t o", o=P)).then_inc(S["wT"], 1)
            v.tensor_copy(w2T[:, :], wps[:, TAPS*P:(TAPS+1)*P]).then_inc(S["wT"], 1)
            v.wait_ge(S["wT"], 3)
            v.sem_inc(S["params"], 1)

            def moments(src, st, mv, s_st, s_bn, s_sd, s_rs, j):
                after(v, s_bn, j)
                for b in range(BLK):
                    last = v.bn_stats(st[:, b, :], src[:, b*P:(b+1)*P])
                last.then_inc(s_st, 1)
                after(v, s_st, j + 1)
                after(v, s_sd, j)
                after(v, s_rs, j)
                v.sem_inc(S["hold"], 1)
                for b in range(BLK):
                    last = v.bn_aggr(mv[:, b, :], st[:, b, :])
                last.then_inc(s_bn, 1)

            def scale_shift(sd, rs, nb, mv, s_sd, s_rc, s_rs, s_xt, j):
                after(v, s_sd, j + 1)
                after(v, s_xt, j)
                v.reciprocal(rs[:, :], sd[:, :]).then_inc(s_rc, 1)
                after(v, s_rc, j + 1)
                v.scalar_tensor_tensor(out=nb[:, :], in0=mv[:, :, 0], scalar=-1.0, in1=rs[:, :], op0=ALU.mult, op1=ALU.mult).then_inc(s_rs, 1)

            def body(k, at, turn):
                if there(k, 2):
                    after(v, S["conv"], k - 1)
                    after(v, S["xn"], k - 1)
                    after(v, S["out1"], k - 2)
                    v.scalar_tensor_tensor(out=z1[:, :], in0=conv_ps[:, :], scalar=scale[:, 0:1], in1=xn[:, at % 2, :],
                                           op0=ALU.mult, op1=ALU.add).then_inc(S["z1"], 1)
                    after(v, S["z1"], k - 1)
                    v.tensor_scalar(neg1[:, :], z1[:, :], 0.0, excess_slope1, ALU.min, ALU.mult).then_inc(S["neg1"], 1)
                if there(k, 5):
                    q = (at - 5) % 2
                    after(v, S["xnT2"], k - 4)
                    need(v, S["stt%d" % q], stored(at, turn, 5))
                    v.tensor_copy(tn[:, q, :], ln2_ps[:, :]).then_inc(S["tn"], 1)
                if there(k, 0):
                    after(v, S["xT1"], k + 1)
                    moments(ln1_ps[:, at % 2, :], stats1, mv1, S["st1"], S["bn1"], S["sd1"], S["rs1"], k)
                if there(k, 3):
                    after(v, S["conv2"], k - 2)
                    after(v, S["out2"], k - 3)
                    v.scalar_tensor_tensor(out=z2[:, :], in0=conv_ps[:, :], scalar=scale[:, 1:2], in1=out1[:, (at - 3) % 2, :],
                                           op0=ALU.mult, op1=ALU.add).then_inc(S["z2"], 1)
                if there(k, 0):
                    scale_shift(sd1, rs1, nb1, mv1, S["sd1"], S["rc1"], S["rs1"], S["xt1"], k)
                if there(k, 4):
                    after(v, S["xT2"], k - 3)
                    moments(ln2_ps[:, :], stats2, mv2, S["st2"], S["bn2"], S["sd2"], S["rs2"], k - 4)
                if there(k, 4):
                    scale_shift(sd2, rs2, nb2, mv2, S["sd2"], S["rc2"], S["rs2"], S["xt2"], k - 4)
                if there(k, 3):
                    after(v, S["neg2"], k - 2)
                    after(v, S["xm"], k - 3)
                    v.scalar_tensor_tensor(out=out2[:, :], in0=neg2[:, :], scalar=one_less_slope[:, 1:2], in1=z2[:, :],
                                           op0=ALU.mult, op1=ALU.add).then_inc(S["out2"], 1)
            rounds(v, FIRST, LAST, TAIL_ROUNDS, WIDE, body)

        @block.scalar
        def _(act):
            act.wait_ge(S["const"], 1)
            act.wait_ge(S["par"], 16 * len(NAMES))
            act.wait_ge(S["w"], 80)
            act.activation(deviation_v[:, 0:1], col["v1m"], ACT.Sqrt, bias=eps[:, 1:2]).then_inc(S["sdv"], 1)
            act.activation(deviation_v[:, 1:2], col["v2m"], ACT.Sqrt, bias=eps[:, 1:2]).then_inc(S["sdv"], 1)
            act.activation(w1s[:, :, :], w1f[:, :].rearrange("o (i t) -> o t i", t=TAPS), ACT.Sign).then_inc(S["wsg"], 1)
            act.activation(w2s[:, :], w2f[:, :], ACT.Sign).then_inc(S["wsg"], 1)
            act.wait_ge(S["params"], 1)

            def normal(xt, src, sd, mv, rs, nb, e, s_rc, s_bn, s_sd, s_rs, s_turned, s_xt, j):
                after(act, s_bn, j + 1)
                after(act, s_rc, j)
                act.activation(sd[:, :], mv[:, :, 1], ACT.Sqrt, bias=eps[:, e:e+1]).then_inc(s_sd, 1)
                yield
                after(act, s_rs, j + 1)
                after(act, s_turned, j)
                for b in range(BLK):
                    last = act.activation(xt[:, b*P:(b+1)*P], src[:, b*P:(b+1)*P], ACT.Identity, bias=nb[:, b:b+1], scale=rs[:, b:b+1])
                last.then_inc(s_xt, 1)

            def body(k, at, turn):
                if there(k, 3):
                    after(act, S["out1"], k - 2)
                    after(act, S["conv2"], k - 3)
                    act.activation(sg2[:, :], out1[:, (at - 3) % 2, :], ACT.Sign, bias=sign_shift2).then_inc(S["sg2"], 1)
                if there(k, 1):
                    p = (at - 1) % 2
                    after(act, S["xnT1"], k)
                    after(act, S["conv"], k - 2)
                    act.activation(sg1[:, p, 1:H+1, 1:W+1], ln1_ps[:, p, :].rearrange("p (h w) -> p h w", w=W),
                                   ACT.Sign, bias=col["b11"]).then_inc(S["sg1"], 1)
                if there(k, 1):
                    after(act, S["z1"], k - 2)
                    act.activation(xn[:, p, :], ln1_ps[:, p, :], ACT.Identity, bias=shift[:, 0:1]).then_inc(S["xn"], 1)
                if there(k, 5):
                    q = (at - 5) % 2
                    after(act, S["rows"], k - 4)
                    need(act, S["str%d" % q], stored(at, turn, 5))
                    act.activation(agg[:, bass.ds((k - 5) * BLK, BLK), :], ln2_ps[:, 0:BLK*ROW].rearrange("p (b r) -> p b r", r=ROW)[:, :, 0:16], ACT.Identity)
                    act.activation(rw[:, q, :, :], ln2_ps[:, 0:BLK*ROW].rearrange("p (b r) -> p b r", r=ROW), ACT.Identity).then_inc(S["rw"], 1)
                if there(k, 0):
                    one = normal(xt1, ln1_ps[:, at % 2, :], sd1, mv1, rs1, nb1, 0, S["rc1"], S["bn1"], S["sd1"], S["rs1"], S["xnT1"], S["xt1"], k)
                    next(one)
                if there(k, 3):
                    after(act, S["z2"], k - 2)
                    after(act, S["out2"], k - 3)
                    act.activation(neg2[:, :], z2[:, :], ACT.Relu, bias=relu_shift2, scale=-1.0).then_inc(S["neg2"], 1)
                if there(k, 0):
                    next(one, None)
                if there(k, 4):
                    two = normal(xt2, ln2_ps[:, :], sd2, mv2, rs2, nb2, 1, S["rc2"], S["bn2"], S["sd2"], S["rs2"], S["xnT2"], S["xt2"], k - 4)
                    next(two)
                    next(two, None)
            rounds(act, FIRST, LAST, TAIL_ROUNDS, WIDE, body)

def sorter(nc, edges_d, keys_d, half, flag):
    with ExitStack() as ctx:
        def sb(name, shape, dt=F32): return ctx.enter_context(nc.sbuf_tensor(f"s{half}_{name}", shape, dt))
        def sem(name): return ctx.enter_context(nc.semaphore(f"s{half}_{name}"))
        ping = sb("ping", [P, EDGE_COLS]); pong = sb("pong", [P, EDGE_COLS]); upper = sb("upper", [P, EDGE_COLS])
        src = sb("src", [P, EDGE_COLS], I32); dst = sb("dst", [P, EDGE_COLS], I32); word = sb("word", [P, EDGE_COLS], I32)
        hi_half = sb("hi_half", [P, EDGE_COLS // 2])
        lane = sb("lane", [P, 8], I32); sign = sb("sign", [P, 8]); turn_sign = sb("turn_sign", [P, 8])
        ident = sb("ident", [P, P]); pad = sb("pad", [P, TAIL // P]); top = sb("top", [P, 1]); topf = sb("topf", [1, 1])
        u_a = sb("u_a", [P, HEAD_COLS]); u_b = sb("u_b", [P, HEAD_COLS])
        turned_ps = ctx.enter_context(nc.psum_tensor(f"s{half}_turned", [P, EDGE_COLS], F32))
        loaded, const, ident_ok, done, to_turn, turned, copied, tables, iota_free, stored, u_back, flagged = (
            ctx.enter_context(semaphores(nc, f"s{half}", "loaded const ident done to_turn turned copied tables iota_free stored u_back flagged")).values())
        block = ctx.enter_context(nc.Block())
        edge_rows = [edges_d[r:r+1, :].rearrange("a (p f) -> (a p) f", p=P) for r in range(2)]
        low_rows = keys_d[1:1 + EDGES].rearrange("(p f) -> p f", p=P)
        high_flat = keys_d[1 + EDGES:1 + EDGES + HALF]
        CROSS = 2 * PART_BITS + 2

        final_low, final_high = [ping], [u_b]

        @block.sync
        def _(sp):
            sp.dma_start(src[:, :], edge_rows[0]).then_inc(loaded, 16)
            sp.dma_start(dst[:, :], edge_rows[1]).then_inc(loaded, 16)
            sp.wait_ge(const, 1)
            sp.dma_start(keys_d[0:1].rearrange("(a b) -> a b", a=1), pad[0:1, 0:1]).then_inc(stored, 16)
            sp.dma_start(keys_d[1 + EDGES + HALF:1 + EDGES + HALF + TAIL].rearrange("(a b) -> a b", a=P), pad[:, :]).then_inc(stored, 16)
            sp.wait_ge(iota_free, 1)
            sp.dma_start(high_flat.rearrange("(p f) -> p f", f=EDGE_COLS), upper[P - HALF // EDGE_COLS:P, :]).then_inc(stored, 16)
            sp.wait_ge(stored, 48)
            sp.dma_start(u_a[:, :], high_flat.rearrange("(p f) -> p f", p=P)).then_inc(u_back, 16)
            sp.wait_ge(iota_free, 2)
            sp.dma_start(low_rows, final_low[0][:, :]).then_inc(stored, 16)
            sp.wait_ge(iota_free, 3)
            sp.dma_start(high_flat.rearrange("(p f) -> p f", p=P), final_high[0][:, :]).then_inc(stored, 16)
            sp.wait_ge(stored, 80)

        @block.gpsimd
        def _(pool):
            pool.memset(ident[:, :], 0.0)
            pool.memset(pad[:, :], 1e4).then_inc(const, 1)
            pool.iota(lane[:, 0:1], [[0, 1]], base=0, channel_multiplier=1).then_inc(tables, 1)
            pool.wait_ge(const, 1)
            pool.affine_select(out=ident[:, :], in_=ident[:, :], compare_op=ALU.not_equal, fill=1.0, base=0,
                               pattern=[[-1, P]], channel_multiplier=1).then_inc(ident_ok, 1)
            pool.wait_ge(tables, 2)
            pool.iota(dst[:, :], [[-1, EDGE_COLS]], base=EDGES - 1, channel_multiplier=-EDGE_COLS).then_inc(tables, 1)

        crossing_source = []

        def halves(ap, span, mirrored=False):
            v = ap.rearrange("p (g two h) -> p g two h", two=2, h=span)
            return v[:, :, 0, :], (v[:, :, 1, ::-1] if mirrored else v[:, :, 1, :])

        def chunk_of(ap, x, span, c):
            lo, hi = halves(ap, span)
            if x % 2 == 0:
                n = lo.shape[1] // TURN_CHUNKS
                return lo[:, c*n:(c+1)*n, :], hi[:, c*n:(c+1)*n, :]
            n = span // TURN_CHUNKS
            return lo[:, :, c*n:(c+1)*n], hi[:, :, c*n:(c+1)*n]

        spans = []
        for k in [*range(1, PART_BITS + 1), PART_BITS]:
            spans += [1 << (k - 1), 1 << (COL_BITS - 1)]

        def copy_of(x, c):
            n = EDGE_COLS // 2 // TURN_CHUNKS
            _, hi = chunk_of(turned_ps[:, :], x, spans[x], c)
            return hi_half[:, c*n:(c+1)*n].rearrange("p (g h) -> p g h", h=hi.shape[2])
        def u_copy(x):
            return hi_half[:, 0:HEAD_COLS//2].rearrange("p (g h) -> p g h", h=(64, 128)[x])
        u_source = (u_a, u_b)
        @block.vector
        def _(v):
            count = [0]
            def go(i):
                count[0] += 1
                i.then_inc(done, 1)
            def settle():
                v.wait_ge(done, count[0])
            edge_clamp, edge_op = ([float(HALF - SHIFT - 1)], ALU.min) if half == 0 else ([-float(SHIFT)], ALU.max)
            def words(word_f, limit_first):
                base = HALF * half + SHIFT
                settle()
                if half == 0:
                    go(v.tensor_scalar(upper_scratch, dst[:, :], base + (HALF - SHIFT) - 0.5, 16.0, ALU.subtract, ALU.mult))
                else:
                    go(v.tensor_scalar(upper_scratch, dst[:, :], base - SHIFT - 0.5, -16.0, ALU.subtract, ALU.mult))
                go(v.tensor_tensor(src[:, :], src[:, :], dst[:, :], ALU.bitwise_xor)); settle()
                go(v.tensor_scalar(word[:, :], dst[:, :], float(base), *edge_clamp, ALU.subtract, edge_op)); settle()
                go(v.tensor_scalar(dst[:, :], word[:, :], float(LEAST), -1.0, ALU.is_lt, ALU.mult)); settle()
                go(v.scalar_tensor_tensor(out=word[:, :], in0=dst[:, :], scalar=-float(FLIP), in1=word[:, :], op0=ALU.mult, op1=ALU.add)); settle()
                go(v.tensor_scalar(word[:, :], word[:, :], 16, None, ALU.logical_shift_left)); settle()
                go(v.tensor_tensor(word[:, :], word[:, :], src[:, :], ALU.bitwise_or)); settle()
                go(v.tensor_tensor(word[:, :], word[:, :], dst[:, :], ALU.bitwise_xor)); settle()
                go(v.tensor_tensor(word_f, word[:, :].bitcast(F32), upper_scratch, ALU.max)); settle()
            v.wait_ge(loaded, 32)
            if flag is not None:
                go(v.tensor_reduce(top[:, :], dst[:, :], AX.X, ALU.max))
            upper_scratch = upper[:, :]
            words(ping[:, :], True)
            v.wait_ge(tables, 1)
            for k in range(8):
                go(v.tensor_scalar(lane[:, k:k+1], lane[:, 0:1], k, 1, ALU.logical_shift_right, ALU.bitwise_and)) if k else None
            settle()
            go(v.tensor_scalar(lane[:, 0:1], lane[:, 0:1], 1, None, ALU.bitwise_and)); settle()
            go(v.tensor_scalar(sign[:, :], lane[:, :], -2.0, 1.0, ALU.mult, ALU.add)); settle()
            go(v.tensor_copy(turn_sign[:, 0:1], sign[:, 0:1]))
            go(v.tensor_tensor(turn_sign[:, 1:8], sign[:, 0:7], sign[:, 1:8], ALU.mult)); settle()
            a, b = ping, pong
            go(v.tensor_scalar(b[:, :], a[:, :], turn_sign[:, 0:1], None, ALU.mult)); settle()
            v.sem_inc(tables, 1)
            a, b = b, a

            def step(a, b, span, mirrored=False, n=None):
                lo, hi = halves(a[:, :], span, mirrored)
                olo, ohi = halves(b[:, :], span, mirrored)
                go(v.tensor_tensor(olo, lo, hi, ALU.min))
                go(v.tensor_tensor(ohi, lo, hi, ALU.max))
                settle()
                return b, a

            def cross(a, b):
                x = len(crossing_source)
                crossing_source.append(a)
                v.sem_inc(to_turn, 1)
                for c in range(TURN_CHUNKS):
                    lo, _ = chunk_of(turned_ps[:, :], x, spans[x], c)
                    olo, ohi = chunk_of(b[:, :], x, spans[x], c)
                    hi = copy_of(x, c)
                    v.wait_ge(copied, TURN_CHUNKS * x + c + 1)
                    go(v.tensor_tensor(olo, lo, hi, ALU.min))
                    go(v.tensor_tensor(ohi, lo, hi, ALU.max))
                settle()
                return b, a

            for level in range(1, COL_BITS + 1):
                for s in range(level, 0, -1):
                    a, b = step(a, b, 1 << (s - 1), mirrored=(s == level))
            for k in range(1, PART_BITS + 1):
                go(v.tensor_scalar(b[:, :], a[:, :], turn_sign[:, k:k+1] if k < PART_BITS else sign[:, PART_BITS-1:PART_BITS], None, ALU.mult)); settle()
                a, b = b, a
                a, b = cross(a, b)
                for s in range(k - 1, 0, -1):
                    a, b = step(a, b, 1 << (s - 1))
                a, b = cross(a, b)
                for s in range(COL_BITS - 1, 0, -1):
                    a, b = step(a, b, 1 << (s - 1))
            v.wait_ge(tables, 3)
            if half:
                go(v.tensor_scalar(b[:, :], dst[:, :], HALF - 0.5, 16.0, ALU.subtract, ALU.mult))
                go(v.tensor_scalar(src[:, :], dst[:, :], float(HALF), 2.0 * HALF - 1, ALU.add, ALU.min)); settle()
                go(v.tensor_copy(dst[:, :], src[:, :])); settle()
                words(upper[:, :], False)
                go(v.tensor_tensor(upper[:, :], upper[:, :], b[:, :], ALU.max)); settle()
            else:
                go(v.tensor_copy(src[:, :], dst[:, :])); settle()
                words(upper[:, :], False)
            go(v.tensor_tensor(b[:, :], a[:, :], upper[:, :], ALU.min))
            go(v.tensor_tensor(upper[:, :], a[:, :], upper[:, :], ALU.max)); settle()
            v.sem_inc(iota_free, 1)
            a, b = b, a
            a, b = cross(a, b)
            for s in range(PART_BITS - 1, 0, -1):
                a, b = step(a, b, 1 << (s - 1))
            a, b = cross(a, b)
            for s in range(COL_BITS - 1, 0, -1):
                a, b = step(a, b, 1 << (s - 1))
            assert a is final_low[0], "low"
            v.sem_inc(iota_free, 1)
            v.wait_ge(u_back, 16)
            ua, ub = u_a, u_b
            for x, (top_bit) in enumerate((PART_BITS, COL_BITS - 4)):
                v.sem_inc(to_turn, 1)
                v.wait_ge(copied, TURN_CHUNKS * CROSS + x + 1)
                lo, _ = halves(turned_ps[:, 0:HEAD_COLS], 1 << (top_bit - 1))
                olo, ohi = halves(ub[:, :], 1 << (top_bit - 1))
                hi = u_copy(x)
                go(v.tensor_tensor(olo, lo, hi, ALU.min))
                go(v.tensor_tensor(ohi, lo, hi, ALU.max)); settle()
                ua, ub = ub, ua
                for s in range(top_bit - 1, 0, -1):
                    ua, ub = step(ua, ub, 1 << (s - 1))
                if x == 0:
                    assert ua is u_source[1], "u"
            assert ua is final_high[0], "high"
            v.sem_inc(iota_free, 1)
            if flag is not None:
                v.sem_inc(flagged, 1)
                v.wait_ge(flagged, 2)
                go(v.tensor_reduce(topf[:, :], turned_ps[0:1, 0:P], AX.X, ALU.max)); settle()
                go(v.tensor_scalar(flag, topf[:, :], float(HALF), None, ALU.is_ge)); settle()

        @block.scalar
        def _(act):
            for x in range(CROSS):
                for c in range(TURN_CHUNKS):
                    act.wait_ge(turned, TURN_CHUNKS * x + c + 1)
                    _, hi = chunk_of(turned_ps[:, :], x, spans[x], c)
                    act.activation(copy_of(x, c), hi, ACT.Copy).then_inc(copied, 1)
            for x in range(2):
                act.wait_ge(turned, TURN_CHUNKS * CROSS + x + 1)
                _, hi = halves(turned_ps[:, 0:HEAD_COLS], (64, 128)[x])
                act.activation(u_copy(x), hi, ACT.Copy).then_inc(copied, 1)
        @block.tensor
        def _(pe):
            pe.wait_ge(ident_ok, 1)
            blocks = EDGE_COLS // P
            per = blocks // TURN_CHUNKS
            for x in range(CROSS):
                pe.wait_ge(to_turn, x + 1)
                source = crossing_source[x]
                for c in range(TURN_CHUNKS):
                    if x % 2 == 0:
                        which = range(c * per, (c + 1) * per)
                    else:
                        a = range(c * per // 2, (c + 1) * per // 2)
                        which = [*a, *(g + blocks // 2 for g in a)]
                    for g in which:
                        last = pe.transpose(turned_ps[:, g*P:(g+1)*P], source[:, g*P:(g+1)*P], ident[:, :])
                    last.then_inc(turned, 1)
            for x in range(2):
                pe.wait_ge(to_turn, CROSS + x + 1)
                source = (u_a, u_b)[x]
                for g in range(HEAD_COLS // P):
                    last = pe.transpose(turned_ps[:, g*P:(g+1)*P], source[:, g*P:(g+1)*P], ident[:, :])
                last.then_inc(turned, 1)
            if flag is not None:
                pe.wait_ge(flagged, 1)
                pe.transpose(turned_ps[0:1, 0:P], top[:, :], ident[:, :]).then_inc(flagged, 1)


def attention(nc, edges_d, keys_d, rows_d, res_d, agg, half, gathers, make_experts=None):
    with ExitStack() as ctx, ExitStack() as during:
        def keep(name, shape, dt=F32): return ctx.enter_context(nc.sbuf_tensor(f"e{half}_{name}", shape, dt))
        def sb(name, shape, dt=F32): return during.enter_context(nc.sbuf_tensor(f"e{half}_{name}", shape, dt))
        def sem(name): return during.enter_context(nc.semaphore(f"e{half}_{name}"))
        prev_seg, first_seg, last_seg = (keep(n, [P, 1]) for n in ("prev_seg", "first_seg", "last_seg"))
        iota_f, zlast, counts = keep("iota_f", [P, HIS]), keep("zlast", [P, ROW]), keep("counts", [P, HIS])
        x = make_experts(during) if make_experts else None
        key = sb("key", [P, 2, COLS + 1], I32)
        sgn = sb("sgn", [P, COLS + 1], I32); mag = sb("mag", [P, COLS + 1], I32); low = sb("low", [P, COLS + 1], I32)
        seg = sb("seg", [P, COLS + 1], I32); dfull = sb("dfull", [P, COLS + 1], I32)
        index = sb("index", [P, 2, COLS], I32); first = sb("first", [P, 1], I32)
        start = sb("start", [P, 2, COLS]); cont = sb("cont", [P, 2, COLS]); cut = sb("cut", [P, 2, COLS])
        got = sb("got", [P, 2, COLS, ROW]); head0 = sb("head0", [P, ROW])
        adv = sb("adv", [P, HEADS, COLS]); ad = sb("ad", [P, 2, HEADS, COLS]); e = sb("e", [P, HEADS, COLS])
        mx = sb("mx", [P, 2, HEADS, COLS + 1]); dif = sb("dif", [P, 2, HEADS, COLS]); rp = sb("rp", [P, 2, HEADS, COLS])
        wgt = sb("wgt", [P, HEADS, EXPERTS, COLS]); out = sb("out", [P, 2, COLS, ROW])
        tgt = sb("tgt", [P, 2, COUNT_TILES], I32); tlo_i = sb("tlo_i", [P, COUNT_TILES], I32); thi_i = sb("thi_i", [P, COUNT_TILES], I32)
        tlo = sb("tlo", [P, COUNT_TILES]); thi = sb("thi", [P, COUNT_TILES])
        iota_i = sb("iota_i", [P, HIS], I32); iota_b = sb("iota_b", [P, HIS], BF16)
        is_lo = sb("is_lo", [P, 2, RING, P], BF16); is_hi = sb("is_hi", [P, 2, RING, HIS], BF16)
        count_ps = during.enter_context(nc.psum_tensor(f"e{half}_count_ps", [P, 512], F32))
        S = dict(during.enter_context(semaphores(nc, f"e{half}", "key0 key1 dec idx init proc dif exp out st0 st1 tgt0 tgt1 cnt_d hot hit edge iot free")))
        S.update({n: gathers(f"e{half}_{n}") for n in ("gat0", "gat1", "gat2", "gat3", "head")})
        DEC, PROC, CNT = 12, 37, 4

        LAST = CHUNKS + 1
        def decodes(k): return not isinstance(k, int) or k < CHUNKS
        def attends(k): return not isinstance(k, int) or k >= 1

        key_rows = lambda k: keys_d[bass.ds(k * COLS, P * RUN)].rearrange("(q f) -> q f", f=RUN)[:, 0:COLS + 1]
        tgt_rows = lambda k: edges_d[1:2, bass.ds(k * (P * COUNT_TILES), P * COUNT_TILES)].rearrange("a (p f) -> (a p) f", p=P)
        res_rows = res_d.rearrange("(q f) r -> q (f r)", f=RUN)

        with nc.Block() as block:
            @block.sync
            def _(sp):
                if x: x.start_sync(sp)
                for u in range(2):
                    sp.dma_start(key[:, u, :].bitcast(F32), key_rows(u)).then_inc(S["key%d" % u], 16)
                    sp.dma_start(tgt[:, u, :], tgt_rows(u)).then_inc(S["tgt%d" % u], 16)
                def body(k, at, turn):
                    if attends(k):
                        q = (at - 1) % 2
                        need(sp, S["out"], k)
                        sp.dma_start(res_rows[:, bass.ds((k - 1) * (COLS * ROW), COLS * ROW)],
                                     out[:, q, :, :].rearrange("p f r -> p (f r)")).then_inc(S["st%d" % q], 16)
                    if not isinstance(k, int) or k + 2 < CHUNKS:
                        u = at % 2
                        need(sp, S["dec"], DEC * (k + 1))
                        sp.dma_start(key[:, u, :].bitcast(F32), key_rows(k + 2)).then_inc(S["key%d" % u], 16)
                        need(sp, S["cnt_d"], CNT * (k + 1))
                        sp.dma_start(tgt[:, u, :], tgt_rows(k + 2)).then_inc(S["tgt%d" % u], 16)
                    if x: x.sync(sp, k, at, turn, 4)
                rounds(sp, 6, LAST, 3, 4, body)
                for q in range(2):
                    sp.wait_ge(S["st%d" % q], 16 * CHUNKS // 2)
                if x: x.end_sync(sp)

            @block.gpsimd
            def _(pool):
                pool.iota(iota_i[:, :], [[1, HIS]], base=0, channel_multiplier=0).then_inc(S["iot"], 1)
                if x: x.start_gpsimd(pool)
                pool.wait_ge(S["edge"], 1)
                pool.indirect_dma_start(head0[:, :], None, rows_d, bass.IndirectOffsetOnAxis(ap=first[:, :], axis=0)).then_inc(S["head"], 16)
                def body(k, at, turn):
                    if decodes(k):
                        need(pool, S["idx"], k + 1)
                        need(pool, S["out"], k - 1)
                        pool.sem_inc(S["free"], 1)
                        for c in range(COLS):
                            pool.indirect_dma_start(got[:, at % 2, c, :], None, rows_d,
                                bass.IndirectOffsetOnAxis(ap=index[:, at % 2, c:c+1], axis=0)).then_inc(S["gat%d" % (at % 4)], 16)
                rounds(pool, 6, LAST, 3, 4, body)

            @block.tensor
            def _(pe):
                if x: x.start_tensor(pe)
                def body(k, at, turn):
                    if decodes(k):
                        for g in range(COUNT_TILES // RING):
                            need(pe, S["hot"], k * (COUNT_TILES // RING) + g + 1)
                            for t in range(RING):
                                last = pe.matmul(count_ps[:, 0:HIS], is_lo[:, g % 2, t, :], is_hi[:, g % 2, t, :],
                                                 start=(isinstance(k, int) and k == 0 and g == 0 and t == 0),
                                                 stop=(isinstance(k, int) and k == CHUNKS - 1 and g == COUNT_TILES // RING - 1 and t == RING - 1))
                            last.then_inc(S["hit"], 1)
                    if x: x.tensor(pe, k, at, turn, 4)
                rounds(pe, 6, LAST, 3, 4, body)

            @block.scalar
            def _(act):
                if x: act.wait_ge(x.S["w"], x.WEIGHTS)
                def body(k, at, turn):
                    if attends(k):
                        need(act, S["dif"], k)
                        act.activation(rp[:, :, :, :], dif[:, :, :, :], ACT.Exp).then_inc(S["exp"], 1)
                    if x: x.scalar(act, k, at, turn, 4)
                rounds(act, 6, LAST, 3, 4, body)

            @block.vector
            def _(v):
                if x: x.start_vector(v)
                v.wait_ge(S["iot"], 1)
                v.tensor_copy(iota_f[:, :], iota_i[:, :]).then_inc(S["iot"], 1)
                v.tensor_copy(iota_b[:, :], iota_i[:, :]).then_inc(S["iot"], 1)

                def body(k, at, turn):
                    if decodes(k):
                        u = at % 2
                        i = [0]
                        def go(ins):
                            i[0] += 1
                            ins.then_inc(S["dec"], 1)
                            v.wait_ge(S["dec"], DEC * k + i[0])
                        v.wait_ge(S["key%d" % u], 16 * (at // 2 + 1) + 32 * turn)
                        kk = key[:, u, :]
                        go(v.tensor_scalar(sgn[:, :], kk, 31, None, ALU.arith_shift_right))
                        go(v.tensor_tensor(mag[:, :], kk, sgn[:, :], ALU.bitwise_xor))
                        go(v.tensor_scalar(low[:, :], mag[:, :], 16, None, ALU.logical_shift_right))
                        go(v.scalar_tensor_tensor(out=seg[:, :], in0=sgn[:, :], scalar=float(FLIP), in1=low[:, :], op0=ALU.mult, op1=ALU.add))
                        go(v.tensor_scalar(dfull[:, :], seg[:, :], float(SHIFT + HALF * half), None, ALU.add))
                        go(v.tensor_tensor(mag[:, :], mag[:, :], dfull[:, :], ALU.bitwise_xor))
                        if not isinstance(k, int) or k >= 2:
                            v.wait_ge(S["gat%d" % ((at - 2) % 4)], 16 * COLS * ((at - 2) // 4 + 1) + 16 * COLS * turn)
                        go(v.tensor_scalar(index[:, u, :], mag[:, 1:COLS+1], 65535, None, ALU.bitwise_and))
                        v.sem_inc(S["idx"], 1)
                        go(v.tensor_tensor(start[:, u, :], seg[:, 1:COLS+1], seg[:, 0:COLS], ALU.not_equal))
                        go(v.tensor_scalar(cont[:, u, :], start[:, u, :], -1.0, 1.0, ALU.mult, ALU.add))
                        go(v.tensor_scalar(cut[:, u, :], start[:, u, :], -BIG, None, ALU.mult))
                        if isinstance(k, int) and k == 0:
                            go(v.tensor_copy(prev_seg[:, :], seg[:, 0:1]))
                            go(v.tensor_copy(first_seg[:, :], seg[:, 1:2]))
                            v.tensor_scalar(first[:, :], dfull[:, 1:2], 65535, None, ALU.bitwise_and).then_inc(S["edge"], 1)
                        else:
                            go(v.tensor_copy(last_seg[:, :], seg[:, COLS:COLS+1]))
                            go(v.tensor_copy(last_seg[:, :], seg[:, COLS:COLS+1]))
                        assert i[0] == DEC
                        v.wait_ge(S["tgt%d" % u], 16 * (at // 2 + 1) + 32 * turn)
                        need(v, S["hit"], k * (COUNT_TILES // RING))
                        c = S["cnt_d"]
                        v.tensor_scalar(tlo_i[:, :], tgt[:, u, :], P - 1, None, ALU.bitwise_and).then_inc(c, 1)
                        v.tensor_scalar(thi_i[:, :], tgt[:, u, :], 7, None, ALU.logical_shift_right).then_inc(c, 1)
                        v.wait_ge(c, CNT * k + 2)
                        v.tensor_copy(tlo[:, :], tlo_i[:, :]).then_inc(c, 1)
                        v.tensor_scalar(thi[:, :], thi_i[:, :], float(HIS * half), None, ALU.subtract).then_inc(c, 1)
                        v.wait_ge(c, CNT * k + 4)
                        v.wait_ge(S["iot"], 3)
                        for g in range(COUNT_TILES // RING):
                            if (isinstance(k, int) and k > 0) or not isinstance(k, int) or g >= 2:
                                v.wait_ge(S["hit"], k * (COUNT_TILES // RING) + g - 1)
                            for t in range(RING):
                                n = g * RING + t
                                v.tensor_scalar(is_lo[:, g % 2, t, :], iota_b[:, 0:P], tlo[:, n:n+1], None, ALU.is_equal)
                                last = v.tensor_scalar(is_hi[:, g % 2, t, :], iota_b[:, :], thi[:, n:n+1], None, ALU.is_equal)
                            last.then_inc(S["hot"], 1)
                    if attends(k):
                        q = (at - 1) % 2
                        j = k - 1
                        i = [0]
                        def go(ins):
                            i[0] += 1
                            ins.then_inc(S["proc"], 1)
                        def settle():
                            v.wait_ge(S["proc"], PROC * j + i[0])
                        if isinstance(k, int) and k == 1:
                            v.wait_ge(S["head"], 16)
                            v.tensor_copy(ad[:, 1, :, COLS-1], head0[:, 20:24]).then_inc(S["init"], 1)
                            v.memset(mx[:, 1, :, COLS], -BIG).then_inc(S["init"], 1)
                            v.memset(out[:, 1, :, :], 0.0).then_inc(S["init"], 1)
                            v.wait_ge(S["init"], 3)
                        v.wait_ge(S["gat%d" % ((at - 1) % 4)], 16 * COLS * ((at - 1) // 4 + 1) + 16 * COLS * turn)
                        if not isinstance(k, int) or k >= 3:
                            v.wait_ge(S["st%d" % q], 16 * ((at - 1) // 2) + 32 * turn)
                        g = got[:, q, :, :]
                        by_head = lambda ap: ap.unsqueeze(1).broadcast_to([P, HEADS, COLS])
                        go(v.tensor_tensor(adv[:, :, :], g[:, :, 20:24].rearrange("p c h -> p h c"), by_head(start[:, q, :]), ALU.mult)); settle()
                        for h in range(HEADS):
                            go(v.tensor_tensor_scan(ad[:, q, h, :], cont[:, q, :], adv[:, h, :], ad[:, 1 - q, h, COLS-1:COLS], ALU.mult, ALU.add))
                        settle()
                        go(v.tensor_tensor(e[:, :, :], ad[:, q, :, :], g[:, :, 16:20].rearrange("p c h -> p h c"), ALU.add)); settle()
                        go(v.scalar_tensor_tensor(out=e[:, :, :], in0=e[:, :, :], scalar=0.2, in1=e[:, :, :], op0=ALU.mult, op1=ALU.max))
                        go(v.tensor_copy(mx[:, q, :, 0], mx[:, 1 - q, :, COLS])); settle()
                        for h in range(HEADS):
                            go(v.tensor_tensor_scan(mx[:, q, h, 1:COLS+1], cut[:, q, :], e[:, h, :], mx[:, 1 - q, h, COLS:COLS+1], ALU.add, ALU.max))
                        settle()
                        go(v.tensor_tensor(dif[:, 0, :, :], mx[:, q, :, 0:COLS], by_head(cut[:, q, :]), ALU.add)); settle()
                        go(v.tensor_tensor(dif[:, 0, :, :], dif[:, 0, :, :], mx[:, q, :, 1:COLS+1], ALU.subtract))
                        go(v.tensor_tensor(dif[:, 1, :, :], e[:, :, :], mx[:, q, :, 1:COLS+1], ALU.subtract)); settle()
                        v.sem_inc(S["dif"], 1)
                        go(v.tensor_copy(out[:, q, :, 20:24].rearrange("p c h -> p h c"), mx[:, q, :, 1:COLS+1]))
                        v.wait_ge(S["exp"], k)
                        go(v.tensor_tensor(wgt[:, :, :, :], g[:, :, 0:16].rearrange("p c (h x) -> p h x c", x=EXPERTS),
                                           rp[:, 1, :, :].unsqueeze(2).broadcast_to([P, HEADS, EXPERTS, COLS]), ALU.mult)); settle()
                        for h in range(HEADS):
                            for w in range(EXPERTS + 1):
                                ch = h * EXPERTS + w if w < EXPERTS else HEADS * EXPERTS + h
                                data = wgt[:, h, w, :] if w < EXPERTS else rp[:, 1, h, :]
                                go(v.tensor_tensor_scan(out[:, q, :, ch], rp[:, 0, h, :], data, out[:, 1 - q, COLS-1, ch:ch+1], ALU.mult, ALU.add))
                        settle()
                        v.sem_inc(S["out"], 1)
                        assert i[0] == PROC, i[0]
                    if x: x.vector(v, k, at, turn, 4)
                rounds(v, 6, LAST, 3, 4, body)
                v.wait_ge(S["hit"], CHUNKS * COUNT_TILES // RING)
                v.tensor_scalar(counts[:, :], count_ps[:, 0:HIS], 1.0, None, ALU.add).then_inc(S["iot"], 1)
                v.tensor_copy(zlast[:, :], out[:, (CHUNKS - 1) % 2, COLS-1, :]).then_inc(S["iot"], 1)
                v.wait_ge(S["iot"], 5)

        during.close()
        gather_tokens(nc, ctx, res_d, agg, half, gathers, zlast, counts, prev_seg, first_seg, last_seg, iota_f)

def gather_tokens(nc, ctx, res_d, agg, half, gathers, zlast, counts, prev_seg, first_seg, last_seg, iota_f):
    def sb(name, shape, dt=F32): return ctx.enter_context(nc.sbuf_tensor(f"e{half}_{name}", shape, dt))
    def ps(name, shape, dt=F32): return ctx.enter_context(nc.psum_tensor(f"e{half}_{name}", shape, dt))
    def sem(name): return ctx.enter_context(nc.semaphore(f"g{half}_{name}"))
    CH = HEADS * (EXPERTS + 1)
    ident = sb("g_ident", [P, P]); ones = sb("g_ones", [P, P]); upto = sb("g_upto", [P, P])
    total = sb("g_total", [P, HIS]); before = sb("g_before", [P, HIS]); pos = sb("g_pos", [P, HIS]); pos_i = sb("g_pos_i", [P, HIS], I32)
    tok = sb("g_tok", [P, 1]); tok_i = sb("g_tok_i", [P, 1], I32); lo_i = sb("g_lo_i", [P, 1], I32); hi_i = sb("g_hi_i", [P, 1], I32)
    lo_f = sb("g_lo_f", [P, 1]); hi_f = sb("g_hi_f", [P, 1])
    one_lo = sb("g_one_lo", [P, P]); one_lo_t = sb("g_one_lo_t", [P, P]); one_hi = sb("g_one_hi", [P, HIS]); picked = sb("g_picked", [P, HIS])
    end = sb("g_end", [P, 1]); lane_end = sb("g_lane_end", [P, 1]); lane_i = sb("g_lane_i", [P, 1], I32)
    t1 = sb("g_t1", [P, 1]); t2 = sb("g_t2", [P, 1]); skip = sb("g_skip", [P, 1]); at_i = sb("g_at_i", [P, 1], I32); to_i = sb("g_to_i", [P, 1], I32)
    z = sb("g_z", [P, 3, CH]); zt = sb("g_zt", [CH, 3, P]); mm = sb("g_mm", [CH, P + 1]); ss = sb("g_ss", [CH, P + 1])
    dd = sb("g_dd", [CH, 2, P]); ee = sb("g_ee", [CH, 2, P]); ww = sb("g_ww", [CH, P])
    cin = sb("g_cin", [P, 2, CH]); row = sb("g_row", [P, ROW]); rm = sb("g_rm", [P, CH]); nm = sb("g_nm", [P, CH])
    d2 = sb("g_d2", [P, 2, CH]); e2 = sb("g_e2", [P, 2, CH]); new = sb("g_new", [P, ROW])
    PER = 8
    tidx = sb("g_tidx", [P, 2, PER], I32); trow = sb("g_trow", [P, 2, PER, ROW]); tsum = sb("g_tsum", [P, 2, PER, HEADS]); trec = sb("g_trec", [P, 2, PER, HEADS])
    a_ps = ps("g_a_ps", [P, 512]); b_ps = ps("g_b_ps", [P, 512]); c_ps = ps("g_c_ps", [P, 512])
    S = dict(ctx.enter_context(semaphores(nc, f"g{half}", "const c2 dv pe act got idx agg dn free")))
    S.update({n: gathers(f"g{half}_{n}") for n in ("put", "tg0", "tg1")})
    TURNS = HIS // PER
    with nc.Block() as block:
        dv, pe_s = S["dv"], S["pe"]
        @block.gpsimd
        def _(pool):
            pool.memset(ident[:, :], 0.0)
            pool.memset(ones[:, :], 1.0)
            pool.memset(upto[:, :], 1.0).then_inc(S["const"], 1)
            pool.wait_ge(S["const"], 1)
            pool.iota(lane_i[:, :], [[0, 1]], base=RUN - 1, channel_multiplier=RUN)
            pool.affine_select(out=ident[:, :], in_=ident[:, :], compare_op=ALU.not_equal, fill=1.0, base=0, pattern=[[-1, P]], channel_multiplier=1)
            pool.affine_select(out=upto[:, :], in_=upto[:, :], compare_op=ALU.is_ge, fill=0.0, base=0, pattern=[[1, P]], channel_multiplier=-1).then_inc(S["const"], 1)
            pool.wait_ge(S["got"], 1)
            pool.indirect_dma_start(row[:, :], None, res_d, bass.IndirectOffsetOnAxis(ap=at_i[:, :], axis=0)).then_inc(S["put"], 16)
            pool.wait_ge(S["got"], 2)
            pool.indirect_dma_start(res_d, bass.IndirectOffsetOnAxis(ap=to_i[:, :], axis=0), new[:, :], None,
                                    bounds_check=ENTRIES - 1, oob_is_err=False).then_inc(S["put"], 16)
            pool.wait_ge(S["put"], 32)
            def body(k, at, turn):
                if not isinstance(k, int) or k < TURNS:
                    need(pool, S["idx"], k + 1)
                    need(pool, S["agg"], k - 1)
                    pool.sem_inc(S["free"], 1)
                    for c in range(PER):
                        pool.indirect_dma_start(trow[:, at % 2, c, :], None, res_d,
                            bass.IndirectOffsetOnAxis(ap=tidx[:, at % 2, c:c+1], axis=0)).then_inc(S["tg%d" % (at % 2)], 16)
            rounds(pool, 2, TURNS + 1, 1, 2, body)

        @block.tensor
        def _(pe):
            pe.wait_ge(S["const"], 2)
            pe.matmul(a_ps[:, 0:HIS], ones[:, :], counts[:, :], start=True, stop=True)
            pe.matmul(a_ps[:, HIS:2*HIS], upto[:, :], counts[:, :], start=True, stop=True).then_inc(pe_s, 1)
            pe.wait_ge(S["c2"], 1)
            pe.transpose(b_ps[:, 0:P], one_lo[:, :], ident[:, :]).then_inc(pe_s, 1)
            pe.wait_ge(S["c2"], 2)
            pe.matmul(b_ps[:, P:P+HIS], one_lo_t[:, :], pos[:, :], start=True, stop=True).then_inc(pe_s, 1)
            pe.wait_ge(S["c2"], 3)
            for i in range(3):
                last = pe.transpose(c_ps[0:CH, i*P:(i+1)*P], z[:, i, :], ident[:, :])
            last.then_inc(pe_s, 1)
            pe.wait_ge(S["c2"], 4)
            pe.transpose(c_ps[:, 384:384+CH], mm[:, 0:P], ident[0:CH, 0:CH])
            pe.transpose(c_ps[:, 448:448+CH], ss[:, 0:P], ident[0:CH, 0:CH]).then_inc(pe_s, 1)

        @block.scalar
        def _(act):
            act.wait_ge(S["act"], 1)
            act.activation(ee[:, :, :], dd[:, :, :], ACT.Exp).then_inc(S["act"], 1)
            act.wait_ge(S["act"], 3)
            act.activation(e2[:, :, :], d2[:, :, :], ACT.Exp).then_inc(S["act"], 1)

        @block.vector
        def _(v):
            n = [0]
            def go(i):
                n[0] += 1
                i.then_inc(dv, 1)
                v.wait_ge(dv, n[0])
            v.wait_ge(S["const"], 2)
            v.wait_ge(pe_s, 1)
            go(v.tensor_copy(total[:, :], a_ps[:, 0:HIS]))
            go(v.memset(one_hi[:, :], 1.0))
            go(v.tensor_tensor_scan(before[:, :], one_hi[:, :], total[:, :], 0.0, ALU.mult, ALU.add))
            go(v.tensor_tensor(before[:, :], before[:, :], total[:, :], ALU.subtract))
            go(v.scalar_tensor_tensor(out=pos[:, :], in0=a_ps[:, HIS:2*HIS], scalar=-1.0, in1=before[:, :], op0=ALU.add, op1=ALU.add))
            go(v.tensor_copy(pos_i[:, :], pos[:, :]))
            go(v.tensor_scalar(tok[:, :], first_seg[:, :], float(SHIFT), None, ALU.add))
            go(v.tensor_copy(tok_i[:, :], tok[:, :]))
            go(v.tensor_scalar(lo_i[:, :], tok_i[:, :], P - 1, None, ALU.bitwise_and))
            go(v.tensor_scalar(hi_i[:, :], tok_i[:, :], 7, None, ALU.logical_shift_right))
            go(v.tensor_copy(lo_f[:, :], lo_i[:, :]))
            go(v.tensor_copy(hi_f[:, :], hi_i[:, :]))
            go(v.tensor_scalar(one_lo[:, :], iota_f[:, 0:P], lo_f[:, :], None, ALU.is_equal))
            go(v.tensor_scalar(one_hi[:, :], iota_f[:, :], hi_f[:, :], None, ALU.is_equal))
            v.sem_inc(S["c2"], 1)
            v.wait_ge(pe_s, 2)
            go(v.tensor_copy(one_lo_t[:, :], b_ps[:, 0:P]))
            v.sem_inc(S["c2"], 1)
            v.wait_ge(pe_s, 3)
            go(v.tensor_tensor(picked[:, :], b_ps[:, P:P+HIS], one_hi[:, :], ALU.mult))
            go(v.reduce_sum(end[:, :], picked[:, :], axis=AX.X))
            go(v.tensor_copy(lane_end[:, :], lane_i[:, :]))
            go(v.tensor_tensor(skip[:, :], first_seg[:, :], prev_seg[:, :], ALU.not_equal))
            go(v.tensor_tensor(t1[:, :], end[:, :], lane_end[:, :], ALU.is_gt))
            go(v.tensor_tensor(skip[:, :], skip[:, :], t1[:, :], ALU.add))
            go(v.tensor_scalar(t2[:, :], tok[:, :], float(HALF), None, ALU.is_ge))
            go(v.tensor_tensor(skip[:, :], skip[:, :], t2[:, :], ALU.add))
            go(v.tensor_copy(at_i[:, :], end[:, :]))
            v.sem_inc(S["got"], 1)
            go(v.scalar_tensor_tensor(out=t1[:, :], in0=skip[:, :], scalar=float(ENTRIES), in1=end[:, :], op0=ALU.mult, op1=ALU.add))
            go(v.tensor_copy(to_i[:, :], t1[:, :]))
            five = lambda ap: ap.unsqueeze(2).broadcast_to([P, HEADS, EXPERTS])
            go(v.tensor_copy(z[:, 0, 0:16].rearrange("p (h x) -> p h x", x=EXPERTS), five(zlast[:, 20:24])))
            go(v.tensor_copy(z[:, 0, 16:20], zlast[:, 20:24]))
            go(v.tensor_copy(z[:, 1, :], zlast[:, 0:20]))
            go(v.tensor_tensor(t2[:, :], last_seg[:, :], prev_seg[:, :], ALU.not_equal))
            go(v.tensor_scalar(z[:, 2, :], z[:, 0, :], 0.0, t2[:, :], ALU.mult, ALU.add))
            go(v.tensor_scalar(z[:, 2, :], z[:, 2, :], -BIG, None, ALU.mult))
            v.sem_inc(S["c2"], 1)
            v.wait_ge(pe_s, 4)
            go(v.tensor_copy(zt[:, :, :], c_ps[0:CH, 0:3*P].rearrange("c (i p) -> c i p", p=P)))
            go(v.memset(mm[:, 0:1], -BIG))
            go(v.memset(ss[:, 0:1], 0.0))
            go(v.tensor_tensor_scan(mm[:, 1:P+1], zt[:, 2, :], zt[:, 0, :], mm[:, 0:1], ALU.add, ALU.max))
            go(v.tensor_tensor(dd[:, 0, :], mm[:, 0:P], zt[:, 2, :], ALU.add))
            go(v.tensor_tensor(dd[:, 0, :], dd[:, 0, :], mm[:, 1:P+1], ALU.subtract))
            go(v.tensor_tensor(dd[:, 1, :], zt[:, 0, :], mm[:, 1:P+1], ALU.subtract))
            v.sem_inc(S["act"], 1)
            v.wait_ge(S["act"], 2)
            go(v.tensor_tensor(ww[:, :], ee[:, 1, :], zt[:, 1, :], ALU.mult))
            go(v.tensor_tensor_scan(ss[:, 1:P+1], ee[:, 0, :], ww[:, :], ss[:, 0:1], ALU.mult, ALU.add))
            v.sem_inc(S["c2"], 1)
            v.wait_ge(pe_s, 5)
            go(v.tensor_copy(cin[:, 0, :], c_ps[:, 384:384+CH]))
            go(v.tensor_copy(cin[:, 1, :], c_ps[:, 448:448+CH]))
            v.wait_ge(S["put"], 16)
            go(v.tensor_copy(rm[:, 0:16].rearrange("p (h x) -> p h x", x=EXPERTS), five(row[:, 20:24])))
            go(v.tensor_copy(rm[:, 16:20], row[:, 20:24]))
            go(v.tensor_tensor(nm[:, :], rm[:, :], cin[:, 0, :], ALU.max))
            go(v.tensor_tensor(d2[:, 0, :], rm[:, :], nm[:, :], ALU.subtract))
            go(v.tensor_tensor(d2[:, 1, :], cin[:, 0, :], nm[:, :], ALU.subtract))
            v.sem_inc(S["act"], 1)
            v.wait_ge(S["act"], 4)
            go(v.tensor_tensor(new[:, 0:20], row[:, 0:20], e2[:, 0, :], ALU.mult))
            go(v.tensor_tensor(cin[:, 1, :], cin[:, 1, :], e2[:, 1, :], ALU.mult))
            go(v.tensor_tensor(new[:, 0:20], new[:, 0:20], cin[:, 1, :], ALU.add))
            go(v.tensor_copy(new[:, 20:24], nm[:, 16:20]))
            v.sem_inc(S["got"], 1)

            def indices(k, at, turn):
                if not isinstance(k, int) or k >= 2:
                    v.wait_ge(S["tg%d" % (at % 2)], 16 * PER * (at // 2) + 16 * PER * turn)
                v.tensor_copy(tidx[:, at % 2, :], pos_i[:, bass.ds(k * PER, PER)]).then_inc(S["idx"], 1)
            def body(k, at, turn):
                if not isinstance(k, int) or k < TURNS:
                    indices(k, at, turn)
                if not isinstance(k, int) or k >= 1:
                    j, q = k - 1, (at - 1) % 2
                    v.wait_ge(S["tg%d" % q], 16 * PER * ((at - 1) // 2 + 1) + 16 * PER * turn)
                    need(v, S["agg"], j)
                    v.tensor_scalar(tsum[:, q, :, :], trow[:, q, :, 16:20], 1e-16, None, ALU.add).then_inc(S["dn"], 1)
                    v.wait_ge(S["dn"], 2 * j + 1)
                    v.reciprocal(trec[:, q, :, :], tsum[:, q, :, :]).then_inc(S["dn"], 1)
                    v.wait_ge(S["dn"], 2 * j + 2)
                    v.tensor_tensor(agg[:, bass.ds(half * HIS + j * PER, PER), :].rearrange("p b (h x) -> p b h x", x=EXPERTS), trow[:, q, :, 0:16].rearrange("p b (h x) -> p b h x", x=EXPERTS),
                                    trec[:, q, :, :].unsqueeze(3).broadcast_to([P, PER, HEADS, EXPERTS]), ALU.mult).then_inc(S["agg"], 1)
            rounds(v, 2, TURNS + 1, 1, 2, body)

def gates(nc, agg, io, parts, name):
    with ExitStack() as ctx:
        def sb(n, shape, dt=F32): return ctx.enter_context(nc.sbuf_tensor(f"{name}_{n}", shape, dt))
        def sem(n): return ctx.enter_context(nc.semaphore(f"{name}_{n}"))
        D = HEADS * EXPERTS
        con = sb("con", [P, 3, D]); eps = sb("eps", [P, 1])
        cen = sb("cen", [P, HIS, D]); sq = sb("sq", [P, HIS, D])
        mu = sb("mu", [P, HIS]); var = sb("var", [P, HIS]); sd = sb("sd", [P, HIS]); rs = sb("rs", [P, HIS])
        sc = sb("sc", [P, HIS, EXPERTS]); won = sb("won", [P, HIS, EXPERTS]); cmp_ = sb("cmp", [P, HIS, EXPERTS]); top = sb("top", [P, HIS])
        ex = sb("ex", [P, HIS, EXPERTS]); g = sb("g", [P, HIS, EXPERTS])
        ld, dv, act_s, cst = ctx.enter_context(semaphores(nc, name, "ld dv act cst")).values()
        over = lambda ap, d: ap.unsqueeze(2).broadcast_to([P, HIS, d])
        row = lambda i: con[:, i, :].unsqueeze(1).broadcast_to([P, HIS, D])
        with nc.Block() as block:
            @block.sync
            def _(sp):
                for i, n in enumerate(("b_gat", "ln_gamma", "ln_beta")):
                    sp.dma_start(con[:, i, :], io[n].rearrange("(a d) -> a d", a=1).broadcast_to([P, D])).then_inc(ld, 16)
            @block.gpsimd
            def _(pool):
                pool.memset(eps[:, :], 1e-5).then_inc(cst, 1)
            @block.scalar
            def _(act):
                act.wait_ge(cst, 1)
                act.wait_ge(act_s, 1)
                act.activation(sd[:, :], var[:, :], ACT.Sqrt, bias=eps[:, :], scale=1.0 / D).then_inc(act_s, 1)
                act.wait_ge(act_s, 3)
                act.activation(ex[:, :, :], ex[:, :, :], ACT.Exp).then_inc(act_s, 1)
            @block.vector
            def _(v):
                n = [0]
                def go(i):
                    n[0] += 1
                    i.then_inc(dv, 1)
                    v.wait_ge(dv, n[0])
                v.wait_ge(ld, 48)
                go(v.tensor_tensor(cen[:, :, :], agg, row(0), ALU.add))
                go(v.reduce_sum(mu[:, :], cen[:, :, :], axis=AX.X))
                go(v.tensor_scalar(mu[:, :], mu[:, :], 1.0 / D, None, ALU.mult))
                go(v.tensor_tensor(cen[:, :, :], cen[:, :, :], over(mu[:, :], D), ALU.subtract))
                go(v.tensor_tensor(sq[:, :, :], cen[:, :, :], cen[:, :, :], ALU.mult))
                go(v.reduce_sum(var[:, :], sq[:, :, :], axis=AX.X))
                v.sem_inc(act_s, 1)
                v.wait_ge(act_s, 2)
                go(v.reciprocal(rs[:, :], sd[:, :]))
                go(v.tensor_tensor(cen[:, :, :], cen[:, :, :], over(rs[:, :], D), ALU.mult))
                go(v.tensor_tensor(cen[:, :, :], cen[:, :, :], row(1), ALU.mult))
                go(v.tensor_tensor(cen[:, :, :], cen[:, :, :], row(2), ALU.add))
                go(v.reduce_sum(sc[:, :, :], cen[:, :, :].rearrange("p b (h e) -> p b e h", e=EXPERTS), axis=AX.X))
                go(v.tensor_scalar(sc[:, :, :], sc[:, :, :], 1.0 / HEADS, None, ALU.mult))
                go(v.memset(won[:, :, :], 0.0))
                for d in range(1, EXPERTS):
                    lo, hi = slice(0, EXPERTS - d), slice(d, EXPERTS)
                    for mine, other, op in ((lo, hi, ALU.is_ge), (hi, lo, ALU.is_gt)):
                        go(v.tensor_tensor(cmp_[:, :, mine], sc[:, :, mine], sc[:, :, other], op))
                        go(v.tensor_tensor(won[:, :, mine], won[:, :, mine], cmp_[:, :, mine], ALU.add))
                go(v.tensor_scalar(won[:, :, :], won[:, :, :], 2.0, None, ALU.is_ge))
                go(v.tensor_reduce(top[:, :], sc[:, :, :], AX.X, ALU.max))
                go(v.tensor_tensor(ex[:, :, :], sc[:, :, :], over(top[:, :], EXPERTS), ALU.subtract))
                v.sem_inc(act_s, 1)
                v.wait_ge(act_s, 4)
                go(v.tensor_tensor(ex[:, :, :], ex[:, :, :], won[:, :, :], ALU.mult))
                go(v.reduce_sum(mu[:, :], ex[:, :, :], axis=AX.X))
                go(v.reciprocal(rs[:, :], mu[:, :]))
                go(v.tensor_tensor(g[:, :, :], ex[:, :, :], over(rs[:, :], EXPERTS), ALU.mult))
                split = parts.rearrange("p b (i j e) -> p b i j e", j=PARTS, e=EXPERTS)
                for j in range(PARTS):
                    go(v.tensor_copy(split[:, :, 0, j, :], g[:, :, :]))
                    if j < PARTS - 1:
                        go(v.tensor_tensor(g[:, :, :], g[:, :, :], split[:, :, 0, j, :], ALU.subtract))
                for i in range(1, PARTS):
                    go(v.tensor_copy(split[:, :, i, :, :], split[:, :, 0, :, :]))

class Experts:
    AHEAD = 2
    GATED, STEPS = EXPERTS * HID, 2 * EXPERTS * HID
    PREPARED = 25
    WEIGHTS = 16 * (4 + PARTS * PARTS)
    def __init__(self, nc, ctx, io, norm_d, mid_d, out_d, kept_d, parts, name):
        self.nc, self.io, self.norm_d, self.mid_d, self.out_d, self.kept_d, self.parts = nc, io, norm_d, mid_d, out_d, kept_d, parts
        def sb(n, shape, dt=F32): return ctx.enter_context(nc.sbuf_tensor(f"{name}_{n}", shape, dt))
        def ps(n, shape, dt=F32): return ctx.enter_context(nc.psum_tensor(f"{name}_{n}", shape, dt))
        self.S = ctx.enter_context(semaphores(nc, name, "w prep lane ident ld0 ld1 ld2 ld3 gst gtp gt w1 gel sel mul w2 fin go ycp st0 st1 st2 st3 kept0 kept1"))
        self.w1 = sb("w1", [P, EXPERTS, HID * P]); self.w2 = sb("w2", [P, EXPERTS, HID, P]); self.b1 = sb("b1", [P, EXPERTS, HID])
        self.b2c = sb("b2c", [P, EXPERTS])
        self.b2f = sb("b2f", [G, P]); self.b2t = sb("b2t", [G, P]); self.b2p = sb("b2p", [G, PARTS, P], BF16); self.b2 = sb("b2", [G, P], BF16)
        self.mask = sb("mask", [G, 8])
        self.gates = GateRows(nc, sb, ps, self.S, parts)
        self.tn = sb("tn", [P, 4, TOK]); self.xm = sb("xm", [P, 4, TOK]); self.o = sb("o", [P, 4, TOK]); self.lower = sb("lower", [P, 4, TOK])
        self.kept = sb("kept", [P, 2, EXPERTS, TOK])
        self.hh = sb("hh", [P, 2, TOK]); self.hs = sb("hs", [P, 2, TOK])
        self.hid_ps = ps("hid_ps", [P, 2, TOK]); self.gate_ps = ps("gate_ps", [P, 2, TOK])
        self.out_ps = ps("out_ps", [P, TOK]); self.kept_ps = ps("kept_ps", [P, TOK])
    def ready(self, k, at, turn, unroll):
        return 48 * (at // 4 + 1) + 48 * (unroll // 4) * turn
    def start_sync(self, sp):
        S, io = self.S, self.io
        sp.dma_start(self.w1[:, :, :], io["W1"].rearrange("e c h -> c e h")).then_inc(S["w"], 16)
        sp.dma_start(self.w2[:, :, :, :], io["W2"].rearrange("e (f h) c -> h e f c", h=P)).then_inc(S["w"], 16)
        with self.nc.allow_non_contiguous_dma("the biases, once, one to a partition"):
            sp.dma_start(self.b1[:, :, :], io["b1"].rearrange("e (f h) -> h e f", h=P)).then_inc(S["w"], 16)
            sp.dma_start(self.b2c[:, :], io["b2"].rearrange("e c -> c e")).then_inc(S["w"], 16)
        for r in range(PARTS * PARTS):
            sp.dma_start(self.b2f[r*EXPERTS:(r+1)*EXPERTS, :], io["b2"]).then_inc(S["w"], 16)
        for k in range(self.AHEAD + 1):
            self.load(sp, k, 0, 4, 0)
    def load(self, sp, at, turn, unroll, ahead):
        u = (at + ahead) % 4
        S = self.S
        sp.dma_start(self.tn[:, u, :], tile_of(self.norm_d, 1, at, turn, unroll, ahead)).then_inc(S["ld%d" % u], 16)
        sp.dma_start(self.xm[:, u, :], tile_of(self.mid_d, 1, at, turn, unroll, ahead)).then_inc(S["ld%d" % u], 16)
        sp.dma_start(self.lower[:, u, :], tile_of(self.norm_d, 0, at, turn, unroll, ahead)).then_inc(S["ld%d" % u], 16)
    def start_gpsimd(self, pool):
        self.gates.start_gpsimd(pool)
    def start_vector(self, v):
        S = self.S
        n = [0]
        def go(i):
            n[0] += 1
            i.then_inc(S["prep"], 1)
            v.wait_ge(S["prep"], n[0])
        v.wait_ge(S["w"], self.WEIGHTS)
        m = self.mask
        self.gates.start_vector(v, go, m)
        for i in range(PARTS):
            go(v.tensor_copy(self.b2p[:, i, :], self.b2f[:, :]))
            go(v.tensor_tensor(self.b2f[:, :], self.b2f[:, :], self.b2p[:, i, :], ALU.subtract))
        go(v.tensor_scalar(self.b2t[:, :], self.b2p[:, 0, :], m[:, 0:1], None, ALU.mult))
        for i in (1, 2):
            go(v.scalar_tensor_tensor(out=self.b2t[:, :], in0=self.b2p[:, i, :], scalar=m[:, i:i+1], in1=self.b2t[:, :], op0=ALU.mult, op1=ALU.add))
        go(v.tensor_copy(self.b2[:, :], self.b2t[:, :]))
        assert n[0] == self.PREPARED
        self.stage(v, 0, 0)
        self.turned(v, 0, 0)
    def stage(self, v, k, at):
        need(v, self.S["gtp"], k - 1)
        v.tensor_copy(self.gates.staged[:, at % 2, :, :], self.parts[:, bass.ds(k * BLKS, BLKS), :]).then_inc(self.S["gst"], 1)
    def turned(self, v, k, at):
        v.wait_ge(self.S["gtp"], k + 1)
        need(v, self.S["w2"], self.STEPS * (k - 1))
        v.tensor_copy(self.gates.turned[:, at % 2, :], self.gates.turned_ps[0:G, 0:TOK]).then_inc(self.S["gt"], 1)
    def turn_gates(self, pe, k, at):
        need(pe, self.S["gst"], k + 1)
        need(pe, self.S["gt"], k)
        if not isinstance(k, int):
            pe.sem_inc(self.S["go"], 1)
        self.gates.turn(pe, self.gates.turned_ps, at).then_inc(self.S["gtp"], 1)
    def first_product(self, pe, k, at, s):
        S = self.S
        need(pe, S["gel"], self.STEPS * k + s - 1)
        e, f = s % self.GATED // HID, s % HID
        tokens = self.tn if s < self.GATED else self.lower
        pe.matmul(self.hid_ps[:, s % 2, :], self.w1[:, e, f*P:(f+1)*P], tokens[:, at % 4, :], start=True, stop=True).then_inc(S["w1"], 1)
    def choose_gate(self, pe, k, at, e):
        S = self.S
        need(pe, S["gt"], k + 1)
        need(pe, S["mul"], 8 * k + 2 * e - 2)
        pe.matmul(self.gate_ps[:, e % 2, :], self.gates.choose[:, e, :], self.gates.turned[:, at % 2, :], start=True, stop=True).then_inc(S["sel"], 1)
    def start_tensor(self, pe):
        S = self.S
        pe.wait_ge(S["ident"], 1)
        pe.wait_ge(S["w"], self.WEIGHTS)
        self.turn_gates(pe, 0, 0)
        pe.wait_ge(S["ld0"], 48)
        for s in range(2):
            self.first_product(pe, 0, 0, s)
        pe.wait_ge(S["prep"], self.PREPARED)
        self.choose_gate(pe, 0, 0, 0)
    def sync(self, sp, k, at, turn, unroll):
        S = self.S
        if not isinstance(k, int) or k >= 1:
            q = (at - 1) % 4
            need(sp, S["fin"], k)
            sp.dma_start(tile_of(self.out_d, 1, at, turn, unroll, -1), self.o[:, q, :]).then_inc(S["st%d" % q], 16)
            if not isinstance(k, int) or k + self.AHEAD < TOKEN_TILES:
                self.load(sp, at, turn, unroll, self.AHEAD)
            u = (at - 1) % 2
            need(sp, S["ycp"], EXPERTS * k)
            sp.dma_start(self.kept_d[k - 1], self.kept[:, u, :, :]).then_inc(S["kept%d" % u], 16)
    def end_sync(self, sp):
        for q in range(4):
            sp.wait_ge(self.S["st%d" % q], 16 * TOKEN_TILES // 4)
        for u in range(2):
            sp.wait_ge(self.S["kept%d" % u], 16 * TOKEN_TILES // 2)
    def tensor(self, pe, k, at, turn, unroll):
        S = self.S
        if isinstance(k, int) and k >= TOKEN_TILES:
            return
        more = not isinstance(k, int) or k + 1 < TOKEN_TILES
        need(pe, S["fin"], k)
        pe.matmul(self.out_ps[:, :], self.b2[:, :], self.gates.turned[:, at % 2, :], start=True, stop=False)
        for s in range(self.STEPS):
            e, f = s % self.GATED // HID, s % HID
            if s < self.GATED:
                need(pe, S["mul"], self.GATED * k + s + 1)
                pe.matmul(self.out_ps[:, :], self.w2[:, e, f, :], self.hs[:, s % 2, :], start=False, stop=(s == self.GATED - 1)).then_inc(S["w2"], 1)
            else:
                if f == 0:
                    need(pe, S["ycp"], EXPERTS * k + e)
                need(pe, S["gel"], self.STEPS * k + s + 1)
                pe.matmul(self.kept_ps[:, :], self.w2[:, e, f, :], self.hh[:, s % 2, :], start=(f == 0), stop=(f == HID - 1)).then_inc(S["w2"], 1)
            if s + 2 < self.STEPS:
                self.first_product(pe, k, at, s + 2)
            elif more:
                if s == self.STEPS - 2:
                    pe.wait_ge(S["ld%d" % ((at + 1) % 4)], self.ready(k + 1, at + 1, turn, unroll))
                self.first_product(pe, k + 1, at + 1, s + 2 - self.STEPS)
            if s % 2 == 0 and s < 6:
                self.choose_gate(pe, k, at, s // 2 + 1)
            if s == 3 and more:
                self.turn_gates(pe, k + 1, at + 1)
            if s == 7 and more:
                self.choose_gate(pe, k + 1, at + 1, 0)
    def scalar(self, act, k, at, turn, unroll):
        S = self.S
        if isinstance(k, int) and k >= TOKEN_TILES:
            return
        def keep_output(e):
            need(act, S["w2"], self.STEPS * k + self.GATED + HID * (e + 1))
            if e == 0:
                need(act, S["kept%d" % (at % 2)], 16 * (at // 2) + 16 * (unroll // 2) * turn)
            act.activation(self.kept[:, at % 2, e, :], self.kept_ps[:, :], ACT.Identity, bias=self.b2c[:, e:e+1]).then_inc(S["ycp"], 1)
        for s in range(self.STEPS):
            need(act, S["w1"], self.STEPS * k + s + 1)
            if 2 <= s < self.GATED + 2:
                need(act, S["mul"], self.GATED * k + s - 1)
            else:
                need(act, S["w2"], self.STEPS * k + s - 1)
            act.activation(self.hh[:, s % 2, :], self.hid_ps[:, s % 2, :], ACT.Gelu, bias=self.b1[:, s % self.GATED // HID, s % HID:s % HID + 1]).then_inc(S["gel"], 1)
            if s >= self.GATED + 3 and s % HID == 1:
                keep_output((s - self.GATED - 3) // HID)
        keep_output(EXPERTS - 1)
    def vector(self, v, k, at, turn, unroll):
        S = self.S
        tile = not isinstance(k, int) or k < TOKEN_TILES
        more = not isinstance(k, int) or k + 1 < TOKEN_TILES
        if not isinstance(k, int) or k >= 1:
            q = (at - 1) % 4
            need(v, S["w2"], self.STEPS * (k - 1) + self.GATED)
            need(v, S["ld%d" % q], self.ready(k - 1, at - 1, turn, unroll))
            need(v, S["st%d" % q], 16 * ((at - 1) // 4) + 16 * (unroll // 4) * turn)
            v.tensor_tensor(self.o[:, q, :], self.xm[:, q, :], self.out_ps[:, :], ALU.add).then_inc(S["fin"], 1)
        for s in range(self.GATED):
            if tile:
                need(v, S["gel"], self.STEPS * k + s + 1)
                need(v, S["sel"], EXPERTS * k + s // HID + 1)
                need(v, S["w2"], self.STEPS * k + s - 1 if s >= 2 else self.STEPS * (k - 1) + self.GATED - 1 + s)
                v.tensor_tensor(self.hs[:, s % 2, :], self.hh[:, s % 2, :], self.gate_ps[:, (s // HID) % 2, :], ALU.mult).then_inc(S["mul"], 1)
            if s == 2 and more:
                self.stage(v, k + 1, at + 1)
            if s == 5 and more:
                self.turned(v, k + 1, at + 1)

def tile_of(d, half, at, turn, unroll, ahead=0):
    n = at + ahead
    img = half * (TOKEN_TILES // 2) + n // 2 + turn * (unroll // 2)
    return d[img, :, (n % 2) * TOK:(n % 2 + 1) * TOK]

class GateRows:
    def __init__(self, nc, sb, ps, S, parts):
        self.S, self.parts = S, parts
        self.lane_i = sb("lane_i", [G, 1], I32); self.lane = sb("lane", [G, 2], I32); self.lf = sb("lf", [G, 2])
        self.choose = sb("choose", [G, EXPERTS, P], BF16); self.onesb = sb("onesb", [G, P], BF16); self.ident = sb("ident", [P, P], BF16)
        self.staged = sb("staged", [P, 2, BLKS, G], BF16); self.turned = sb("turned", [G, 2, TOK], BF16)
        self.turned_ps = ps("turned_ps", [P, 2 * TOK], BF16)
    def start_gpsimd(self, pool):
        S = self.S
        pool.iota(self.lane_i[:, :], [[0, 1]], base=0, channel_multiplier=1)
        pool.memset(self.onesb[:, :], 1.0)
        pool.memset(self.ident[:, :], 0.0).then_inc(S["lane"], 1)
        pool.wait_ge(S["lane"], 1)
        pool.affine_select(out=self.ident[:, :], in_=self.ident[:, :], compare_op=ALU.not_equal, fill=1.0, base=0, pattern=[[-1, P]], channel_multiplier=1).then_inc(S["ident"], 1)
    def start_vector(self, v, go, m):
        v.wait_ge(self.S["lane"], 1)
        GE = PARTS * EXPERTS
        go(v.tensor_copy(self.lf[:, 0:1], self.lane_i[:, :]))
        go(v.tensor_scalar(self.lane[:, 0:1], self.lane_i[:, :], EXPERTS - 1, None, ALU.bitwise_and))
        go(v.tensor_copy(self.lf[:, 1:2], self.lane[:, 0:1]))
        go(v.tensor_scalar(m[:, 0:1], self.lf[:, 0:1], float(GE), None, ALU.is_lt))
        go(v.tensor_scalar(m[:, 2:3], self.lf[:, 0:1], float(2 * GE), None, ALU.is_ge))
        go(v.tensor_scalar(m[:, 1:2], m[:, 0:1], -1.0, 1.0, ALU.mult, ALU.add))
        go(v.tensor_tensor(m[:, 1:2], m[:, 1:2], m[:, 2:3], ALU.subtract))
        for e in range(EXPERTS):
            go(v.tensor_scalar(m[:, 4+e:5+e], self.lf[:, 1:2], float(e), m[:, 0:1], ALU.is_equal, ALU.mult))
            go(v.tensor_scalar(self.choose[:, e, :], self.onesb[:, :], m[:, 4+e:5+e], None, ALU.mult))
    def turn(self, pe, out_ps, at):
        for b in range(BLKS):
            last = pe.transpose(out_ps[0:G, b*P:(b+1)*P], self.staged[:, at % 2, b, :], self.ident[:, :])
        return last

def combine(nc, io, mid_d, out_d, kept_d, parts):
    with ExitStack() as ctx:
        def sb(n, shape, dt=F32): return ctx.enter_context(nc.sbuf_tensor(f"c_{n}", shape, dt))
        def ps(n, shape, dt=F32): return ctx.enter_context(nc.psum_tensor(f"c_{n}", shape, dt))
        S = ctx.enter_context(semaphores(nc, "c", "prep lane ident ld0 ld1 ld2 ld3 gst gtp gt sel mul pair rest fin go st0 st1 st2 st3"))
        gates = GateRows(nc, sb, ps, S, parts)
        mask = sb("mask", [G, 8])
        kept = sb("kept", [P, 4, EXPERTS, TOK]); xm = sb("xm", [P, 4, TOK]); o = sb("o", [P, 4, TOK])
        weighed = sb("weighed", [P, 2, EXPERTS, TOK]); pair = sb("pair", [P, 2, TOK]); rest = sb("rest", [P, 2, TOK]); more_s = sb("more", [P, 2, TOK])
        gate_ps = ps("gate_ps", [P, EXPERTS, TOK])
        UNROLL, FIRST, LAST, END = 4, 6, TOKEN_TILES + 1, 3
        def tile(k): return not isinstance(k, int) or k < TOKEN_TILES
        def more(k): return not isinstance(k, int) or k + 1 < TOKEN_TILES
        def before(k): return not isinstance(k, int) or k >= 1
        with nc.Block() as block:
            @block.sync
            def _(sp):
                def load(k, at, turn, ahead):
                    u = (at + ahead) % 4
                    sp.dma_start(kept[:, u, :, :], kept_d[k + ahead]).then_inc(S["ld%d" % u], 16)
                    sp.dma_start(xm[:, u, :], tile_of(mid_d, 0, at, turn, UNROLL, ahead)).then_inc(S["ld%d" % u], 16)
                for k in range(3):
                    load(k, k, 0, 0)
                def body(k, at, turn):
                    if before(k):
                        q = (at - 1) % 4
                        need(sp, S["fin"], k)
                        sp.dma_start(tile_of(out_d, 0, at, turn, UNROLL, -1), o[:, q, :]).then_inc(S["st%d" % q], 16)
                        if not isinstance(k, int) or k + 2 < TOKEN_TILES:
                            load(k, at, turn, 2)
                rounds(sp, FIRST, LAST, END, UNROLL, body)
                for q in range(4):
                    sp.wait_ge(S["st%d" % q], 16 * TOKEN_TILES // 4)
            @block.gpsimd
            def _(pool):
                gates.start_gpsimd(pool)
                def body(k, at, turn):
                    if tile(k):
                        need(pool, S["mul"], EXPERTS * k + 2)
                        need(pool, S["fin"], k - 1)
                        pool.tensor_tensor(pair[:, at % 2, :], weighed[:, at % 2, 0, :], weighed[:, at % 2, 1, :], ALU.add).then_inc(S["pair"], 1)
                        need(pool, S["mul"], EXPERTS * k + 4)
                        pool.tensor_tensor(rest[:, at % 2, :], weighed[:, at % 2, 2, :], weighed[:, at % 2, 3, :], ALU.add).then_inc(S["pair"], 1)
                rounds(pool, FIRST, LAST, END, UNROLL, body)
            @block.tensor
            def _(pe):
                pe.wait_ge(S["ident"], 1)
                def turn_gates(k, at):
                    need(pe, S["gst"], k + 1)
                    need(pe, S["gt"], k)
                    if not isinstance(k, int):
                        pe.sem_inc(S["go"], 1)
                    gates.turn(pe, gates.turned_ps, at).then_inc(S["gtp"], 1)
                turn_gates(0, 0)
                pe.wait_ge(S["prep"], 15)
                def body(k, at, turn):
                    if more(k):
                        turn_gates(k + 1, at + 1)
                    if tile(k):
                        need(pe, S["gt"], k + 1)
                        for e in range(EXPERTS):
                            need(pe, S["mul"], EXPERTS * (k - 1) + e + 1)
                            pe.matmul(gate_ps[:, e, :], gates.choose[:, e, :], gates.turned[:, at % 2, :], start=True, stop=True).then_inc(S["sel"], 1)
                rounds(pe, FIRST, LAST, END, UNROLL, body)
            @block.scalar
            def _(act):
                def stage(k, at):
                    need(act, S["gtp"], k - 1)
                    act.activation(gates.staged[:, at % 2, :, :], parts[:, bass.ds(k * BLKS, BLKS), :], ACT.Identity).then_inc(S["gst"], 1)
                def turned(k, at):
                    need(act, S["gtp"], k + 1)
                    need(act, S["sel"], EXPERTS * (k - 1))
                    act.activation(gates.turned[:, at % 2, :], gates.turned_ps[0:G, 0:TOK], ACT.Identity).then_inc(S["gt"], 1)
                stage(0, 0)
                turned(0, 0)
                stage(1, 1)
                def body(k, at, turn):
                    if more(k):
                        turned(k + 1, at + 1)
                    if not isinstance(k, int) or k + 2 < TOKEN_TILES:
                        stage(k + 2, at + 2)
                rounds(act, FIRST, LAST, END, UNROLL, body)
            @block.vector
            def _(v):
                n = [0]
                def go(i):
                    n[0] += 1
                    i.then_inc(S["prep"], 1)
                    v.wait_ge(S["prep"], n[0])
                gates.start_vector(v, go, mask)
                def body(k, at, turn):
                    if tile(k):
                        v.wait_ge(S["ld%d" % (at % 4)], 32 * (at // 4 + 1) + 32 * (UNROLL // 4) * turn)
                        need(v, S["pair"], 2 * (k - 1))
                        for e in range(EXPERTS):
                            need(v, S["sel"], EXPERTS * k + e + 1)
                            v.tensor_tensor(weighed[:, at % 2, e, :], kept[:, at % 4, e, :], gate_ps[:, e, :], ALU.mult).then_inc(S["mul"], 1)
                    if before(k):
                        q, r = (at - 1) % 4, (at - 1) % 2
                        need(v, S["pair"], 2 * k - 1)
                        need(v, S["fin"], k - 1)
                        v.tensor_tensor(more_s[:, r, :], pair[:, r, :], xm[:, q, :], ALU.add).then_inc(S["rest"], 1)
                        need(v, S["pair"], 2 * k)
                        need(v, S["rest"], k)
                        need(v, S["st%d" % q], 16 * ((at - 1) // 4) + 16 * (UNROLL // 4) * turn)
                        v.tensor_tensor(o[:, q, :], more_s[:, r, :], rest[:, r, :], ALU.add).then_inc(S["fin"], 1)
                rounds(v, FIRST, LAST, END, UNROLL, body)
def program(nc, io, out):
    IMAGES, C, H, W = io["x"].shape
    M = IMAGES * H * W
    keys = [nc.dram_tensor(f"keys{h}", [1 + ENTRIES + TAIL], F32, kind="Internal").ap() for h in range(2)]
    rows = nc.dram_tensor("rows", [M, ROW], F32, kind="Internal").ap()
    res = [nc.dram_tensor(f"sums{h}", [ENTRIES, ROW], F32, kind="Internal").ap() for h in range(2)]
    mid = nc.dram_tensor("mid", [IMAGES, C, H * W], F32, kind="Internal").ap()
    norm = nc.dram_tensor("norm", [IMAGES, C, H * W], F32, kind="Internal").ap()
    kept = nc.dram_tensor("kept", [TOKEN_TILES, P, EXPERTS, TOK], F32, kind="Internal").ap()
    out_d = out.rearrange("b c h w -> b c (h w)")
    edges = io["edge_index"]
    with ExitStack() as ctx:
        agg = ctx.enter_context(nc.sbuf_tensor("agg", [P, M // P, 16], F32))
        gathers = lambda name: ctx.enter_context(nc.semaphore(name))
        flag = ctx.enter_context(nc.sbuf_tensor("flag", [1, 1], I32))
        sorter(nc, edges, keys[0], 0, flag[:, :])
        mixer(nc, io, dict(xmid=mid, norm=norm, rows=rows.rearrange("(b j p) r -> b p j r", j=H*W//P, p=P), agg=agg[:, :, :], ROW=ROW))
        high = nc.values_load(flag[0:1, 0:1], min_val=0, max_val=1)
        with nc.If(high):
            sorter(nc, edges, keys[1], 1, None)
            attention(nc, edges, keys[1], rows, res[1], agg[:, :, :], 1, gathers)
        with ExitStack() as c1:
            parts = c1.enter_context(nc.sbuf_tensor("parts1", [P, HIS, G], BF16))
            gates(nc, agg[:, HIS:2*HIS, :], io, parts[:, :, :], "gates1")
            attention(nc, edges, keys[0], rows, res[0], agg[:, :, :], 0, gathers,
                      lambda c: Experts(nc, c, io, norm, mid, out_d, kept, parts[:, :, :], "ex"))
        with ExitStack() as c1:
            parts = c1.enter_context(nc.sbuf_tensor("parts0", [P, HIS, G], BF16))
            gates(nc, agg[:, 0:HIS, :], io, parts[:, :, :], "gates0")
            combine(nc, io, mid, out_d, kept, parts[:, :, :])


_INS = ['x', 'L0_conv_w1', 'L0_conv_w2', 'L0_conv_b11', 'L0_conv_b12', 'L0_conv_b13', 'L0_conv_b21', 'L0_conv_b22', 'L0_conv_b23',
        'L0_conv_a1', 'L0_conv_a2', 'L0_conv_g1m', 'L0_conv_be1m', 'L0_conv_m1m', 'L0_conv_v1m', 'L0_conv_g2m', 'L0_conv_be2m',
        'L0_conv_m2m', 'L0_conv_v2m', 'L0_ffn_W_gat', 'L0_ffn_att_src', 'L0_ffn_att_dst', 'L0_ffn_b_gat', 'L0_ffn_ln_gamma',
        'L0_ffn_ln_beta', 'L0_ffn_W1', 'L0_ffn_b1', 'L0_ffn_W2', 'L0_ffn_b2', 'L0_ffn_edge_index']


def kernel(**inputs):
    import numpy as _np
    import concourse.bacc as _bacc
    from concourse import mybir as _mybir
    from concourse.bass_utils import run_bass_kernel_spmd as _run

    nc = _bacc.Bacc("TRN2", target_bir_lowering=False, num_devices=1)
    arrays, io = {}, {}
    for name in _INS:
        a = _np.ascontiguousarray(inputs[name])
        arrays[f"in_{name}_dram"] = a
        short = name.replace("L0_conv_", "").replace("L0_ffn_", "")
        io[short] = nc.dram_tensor(f"in_{name}_dram", a.shape, _mybir.dt.from_np(a.dtype), kind="ExternalInput").ap()
    shape = inputs["x"].shape
    out = nc.dram_tensor("out_0_dram", shape, _mybir.dt.float32, kind="ExternalOutput").ap()
    program(nc, io, out)
    r = _run(nc, [arrays], core_ids=[0])
    return r.results[0]["out_0_dram"]
```

```python
from contextlib import ExitStack, contextmanager

import concourse.bass as bass
from concourse import mybir

F32 = mybir.dt.float32
I32 = mybir.dt.int32
BF16 = mybir.dt.bfloat16
ALU = mybir.AluOpType
ACT = mybir.ActivationFunctionType
AX = mybir.AxisListType

P = 128
EDGES = 524288
HALF = 32768
HEADS, EXPERTS = 4, 4

EDGE_COLS = EDGES // P
PART_BITS, COL_BITS = 7, 12
TURN_CHUNKS = 4
HEAD_COLS = HALF // P
LEAST = 128
SHIFT = HALF // 2 - LEAST
FLIP = 2 * SHIFT

ENTRIES = EDGES + HALF
RUN = ENTRIES // P
TAIL = RUN
CHUNKS = 64
COLS = RUN // CHUNKS
ROW = 24
BIG = 1e30
HIS = HALF // P
COUNT_TILES = EDGE_COLS // CHUNKS
RING = 8

HID = 2
PARTS = 3
G = PARTS * PARTS * EXPERTS
TOK = 512
BLKS = TOK // P
TOKEN_TILES = HALF // TOK



def need(eng, sem, count):
    if isinstance(count, int) and count <= 0:
        return
    eng.wait_ge(sem, count)

def rounds(eng, first, last, tail, unroll, body):
    turns = (last - first - tail) // unroll
    for k in range(first):
        body(k, k, 0)
    with eng.Fori(0, turns) as turn:
        for at in range(first, first + unroll):
            body(turn * unroll + at, at, turn)
    for k in range(first + turns * unroll, last):
        body(k, k, 0)

@contextmanager
def semaphores(nc, prefix, names):
    with ExitStack() as stack:
        signals = {n: stack.enter_context(nc.semaphore(f"{prefix}_{n}")) for n in names.split()}
        yield signals
        with nc.Block() as block:
            @block.gpsimd
            def _(pool):
                for s in signals.values():
                    pool.sem_clear(s)

def mixer(nc, io, tables):
    x, w1, w2 = io["x"], io["w1"], io["w2"]
    IMAGES, C, H, W = x.shape
    PIX = H * W
    BLK = PIX // P
    HALVES = PIX // 512
    TAPS = 9
    PADW = W + 2
    LEAD, WIDE = 2, 6
    LAST = IMAGES + 5
    FIRST, TAIL_ROUNDS = 8, 7
    x_d = x.rearrange("b c h w -> b c (h w)")
    xmid_d, norm_d, rows_d, agg = tables["xmid"], tables["norm"], tables["rows"], tables["agg"]
    with ExitStack() as ctx:
        def sb(name, shape, dt=F32): return ctx.enter_context(nc.sbuf_tensor(f"m_{name}", shape, dt))
        def ps(name, shape, dt=F32): return ctx.enter_context(nc.psum_tensor(f"m_{name}", shape, dt))
        NAMES = ["b11", "b12", "b13", "b21", "b22", "b23", "a1", "a2", "g1m", "be1m", "m1m", "v1m", "g2m", "be2m", "m2m", "v2m"]
        par = sb("par", [P, len(NAMES)])
        col = {n: par[:, i:i+1] for i, n in enumerate(NAMES)}
        der = sb("der", [P, 16])
        weight_sum, deviation_v, gain, scale, shift, one_less_slope = (der[:, 2*i:2*i+2] for i in range(6))
        sign_shift2, relu_shift2, last_shift, excess_slope1 = (der[:, i:i+1] for i in (12, 13, 14, 15))
        eps = sb("eps", [P, 2])
        w1f = sb("w1f", [P, C*TAPS]); w2f = sb("w2f", [P, C])
        w1s = sb("w1s", [P, TAPS, C], BF16); w2s = sb("w2s", [P, C], BF16)
        w1T = sb("w1T", [P, TAPS, C], BF16); w2T = sb("w2T", [P, C], BF16)
        wabs = sb("wabs", [P, C*TAPS])
        identb = sb("identb", [P, P], BF16); ident = sb("ident", [P, P])
        wg = sb("wg", [P, ROW]); att = sb("att", [P, 32]); wtmp = sb("wtmp", [P, 32])
        xin = sb("xin", [P, WIDE, PIX])
        stats1 = sb("stats1", [P, BLK, 6]); mv1 = sb("mv1", [P, BLK, 2]); stats2 = sb("stats2", [P, BLK, 6]); mv2 = sb("mv2", [P, BLK, 2])
        sd1 = sb("sd1", [P, BLK]); rs1 = sb("rs1", [P, BLK]); nb1 = sb("nb1", [P, BLK])
        sd2 = sb("sd2", [P, BLK]); rs2 = sb("rs2", [P, BLK]); nb2 = sb("nb2", [P, BLK])
        xn = sb("xn", [P, 2, PIX]); xt1 = sb("xt1", [P, PIX]); xt2 = sb("xt2", [P, PIX])
        sg1 = sb("sg1", [P, 2, PADW, PADW], BF16); sg2 = sb("sg2", [P, PIX], BF16)
        z1 = sb("z1", [P, PIX]); neg1 = sb("neg1", [P, PIX]); out1 = sb("out1", [P, 2, PIX])
        z2 = sb("z2", [P, PIX]); neg2 = sb("neg2", [P, PIX]); out2 = sb("out2", [P, PIX])
        xm = sb("xm", [P, 2, PIX]); tn = sb("tn", [P, 2, PIX]); rw = sb("rw", [P, 2, BLK, ROW])
        ln1_ps = ps("ln1_ps", [P, 2, PIX]); conv_ps = ps("conv_ps", [P, PIX]); ln2_ps = ps("ln2_ps", [P, PIX])
        S = ctx.enter_context(semaphores(nc, "m", "par w params const ident dp sdv wsg wT x0 x1 x2 x3 x4 x5 xT1 st1 bn1 sd1 rc1 rs1 xt1 xnT1 xn sg1 conv z1 neg1 out1 sg2 "
             "conv2 z2 neg2 out2 xm xT2 st2 bn2 sd2 rc2 rs2 xt2 xnT2 tn rows rw stx0 stx1 stt0 stt1 str0 str1 xs hold still"))
        block = ctx.enter_context(nc.Block())
        def there(k, lag):
            return not isinstance(k, int) or 0 <= k - lag < IMAGES
        def after(eng, sem, images):
            need(eng, sem, min(images, IMAGES) if isinstance(images, int) else images)
        def stored(at, turn, lag):
            return 16 * ((at - lag) // 2) + 16 * (WIDE // 2) * turn

        @block.sync
        def _(sp):
            for i, n in enumerate(NAMES):
                sp.dma_start(col[n], io[n].rearrange("(p a) -> p a", a=1)).then_inc(S["par"], 16)
            sp.dma_start(w1f[:, :], w1.rearrange("o i a b -> o (i a b)")).then_inc(S["w"], 16)
            sp.dma_start(w2f[:, :], w2.rearrange("o i a b -> o (i a b)")).then_inc(S["w"], 16)
            sp.dma_start(wg[:, 0:16], io["W_gat"]).then_inc(S["w"], 16)
            sp.dma_start(att[:, 0:16], io["att_src"].rearrange("(a h) e -> a (h e)", a=1).broadcast_to([P, 16])).then_inc(S["w"], 16)
            sp.dma_start(att[:, 16:32], io["att_dst"].rearrange("(a h) e -> a (h e)", a=1).broadcast_to([P, 16])).then_inc(S["w"], 16)
            for k in range(LEAD):
                sp.dma_start(xin[:, k, :], x_d[k, :, :]).then_inc(S["x%d" % k], 16)

            def body(k, at, turn):
                if not isinstance(k, int) or k + LEAD < IMAGES:
                    after(sp, S["xm"], k - 3)
                    u = (at + LEAD) % WIDE
                    sp.dma_start(xin[:, u, :], x_d[k + LEAD, :, :]).then_inc(S["x%d" % u], 16)
                if there(k, 5):
                    q = (at - 5) % 2
                    after(sp, S["tn"], k - 4)
                    sp.dma_start(norm_d[k - 5, :, :], tn[:, q, :]).then_inc(S["stt%d" % q], 16)
                    after(sp, S["rw"], k - 4)
                    sp.dma_start(rows_d[k - 5], rw[:, q, :, :]).then_inc(S["str%d" % q], 16)
                if there(k, 3):
                    q = (at - 3) % 2
                    after(sp, S["xm"], k - 2)
                    sp.dma_start(xmid_d[k - 3, :, :], xm[:, q, :]).then_inc(S["stx%d" % q], 16)
            rounds(sp, FIRST, LAST, TAIL_ROUNDS, WIDE, body)
            for n in ("stx", "stt", "str"):
                for q in range(2):
                    sp.wait_ge(S[n + str(q)], 16 * IMAGES // 2)

        @block.gpsimd
        def _(pool):
            pool.memset(identb[:, :], 0.0)
            pool.memset(ident[:, :], 0.0)
            pool.memset(sg1[:, :, :, :], 0.0)
            pool.memset(eps[:, 0:1], 1e-6)
            pool.memset(eps[:, 1:2], 1e-5).then_inc(S["const"], 1)
            pool.wait_ge(S["const"], 1)
            for m in (identb, ident):
                last = pool.affine_select(out=m[:, :], in_=m[:, :], compare_op=ALU.not_equal, fill=1.0, base=0,
                                          pattern=[[-1, P]], channel_multiplier=1)
            last.then_inc(S["ident"], 1)
            pool.wait_ge(S["params"], 1)

            def body(k, at, turn):
                if there(k, 2):
                    after(pool, S["neg1"], k - 1)
                    after(pool, S["sg2"], k - 3)
                    after(pool, S["z2"], k - 3)
                    pool.tensor_tensor(out1[:, at % 2, :], neg1[:, :], z1[:, :], ALU.add).then_inc(S["out1"], 1)
                if there(k, 3):
                    q, u = (at - 3) % 2, (at - 3) % WIDE
                    after(pool, S["xT1"], k - 2)
                    pool.sem_inc(S["still"], 1)
                    pool.tensor_scalar(xin[:, u, :], xin[:, u, :], last_shift, None, ALU.add).then_inc(S["xs"], 1)
                    after(pool, S["xs"], k - 2)
                    after(pool, S["out2"], k - 2)
                    after(pool, S["xT2"], k - 4)
                    need(pool, S["stx%d" % q], stored(at, turn, 3))
                    pool.tensor_tensor(xm[:, q, :], out2[:, :], xin[:, u, :], ALU.add).then_inc(S["xm"], 1)
            rounds(pool, FIRST, LAST, TAIL_ROUNDS, WIDE, body)

        @block.tensor
        def _(pe):
            pe.wait_ge(S["ident"], 1)
            pe.wait_ge(S["wsg"], 2)
            wps = conv_ps[:, :].bitcast(BF16)
            for t in range(TAPS + 1):
                src = w1s[:, t, :] if t < TAPS else w2s[:, :]
                last = pe.transpose(wps[:, t*P:(t+1)*P], src, identb[:, :])
            last.then_inc(S["wT"], 1)
            pe.wait_ge(S["wT"], 3)
            pe.wait_ge(S["params"], 1)

            def turned(out, src, signal):
                for j in range(BLK):
                    last = pe.transpose(out[:, j*P:(j+1)*P], src[:, j*P:(j+1)*P], ident[:, :])
                last.then_inc(signal, 1)
            def body(k, at, turn):
                if there(k, 2):
                    after(pe, S["sg1"], k - 1)
                    after(pe, S["z1"], k - 2)
                    after(pe, S["z2"], k - 3)
                    rows_of = H // HALVES
                    for hf in range(HALVES):
                        for t in range(TAPS):
                            dy, dx = t // 3, t % 3
                            last = pe.matmul(conv_ps[:, hf*512:(hf+1)*512], w1T[:, t, :],
                                             sg1[:, at % 2, hf*rows_of+dy:hf*rows_of+dy+rows_of, dx:dx+W],
                                             start=(t == 0), stop=(t == TAPS - 1))
                    last.then_inc(S["conv"], 1)
                if there(k, 1):
                    after(pe, S["xt1"], k)
                    turned(ln1_ps[:, (at - 1) % 2, :], xt1[:, :], S["xnT1"])
                if there(k, 5):
                    after(pe, S["xt2"], k - 4)
                    turned(ln2_ps[:, :], xt2[:, :], S["xnT2"])
                if there(k, 0):
                    pe.wait_ge(S["x%d" % (at % WIDE)], 16 * (at // WIDE + 1) + 16 * turn)
                    after(pe, S["xn"], k - 1)
                    turned(ln1_ps[:, at % 2, :], xin[:, at % WIDE, :], S["xT1"])
                if there(k, 3):
                    after(pe, S["sg2"], k - 2)
                    after(pe, S["z1"], k - 1)
                    after(pe, S["z2"], k - 3)
                    for hf in range(HALVES):
                        last = pe.matmul(conv_ps[:, hf*512:(hf+1)*512], w2T[:, :], sg2[:, hf*512:(hf+1)*512], start=True, stop=True)
                    last.then_inc(S["conv2"], 1)
                if there(k, 5):
                    after(pe, S["tn"], k - 4)
                    for j in range(BLK):
                        last = pe.matmul(ln2_ps[:, j*ROW:(j+1)*ROW], tn[:, (at - 5) % 2, j*P:(j+1)*P], wg[:, :], start=True, stop=True)
                    last.then_inc(S["rows"], 1)
                if there(k, 4):
                    after(pe, S["xm"], k - 3)
                    after(pe, S["rw"], k - 4)
                    turned(ln2_ps[:, :], xm[:, at % 2, :], S["xT2"])
            rounds(pe, FIRST, LAST, TAIL_ROUNDS, WIDE, body)

        @block.vector
        def _(v):
            n = [0]
            def go(i):
                n[0] += 1
                i.then_inc(S["dp"], 1)
                v.wait_ge(S["dp"], n[0])
            v.wait_ge(S["par"], 16 * len(NAMES))
            v.wait_ge(S["w"], 80)
            go(v.scalar_tensor_tensor(out=wabs[:, :], in0=w1f[:, :], scalar=-1.0, in1=w1f[:, :], op0=ALU.mult, op1=ALU.max))
            go(v.reduce_sum(weight_sum[:, 0:1], wabs[:, :], axis=AX.X))
            go(v.scalar_tensor_tensor(out=wabs[:, 0:C], in0=w2f[:, :], scalar=-1.0, in1=w2f[:, :], op0=ALU.mult, op1=ALU.max))
            go(v.reduce_sum(weight_sum[:, 1:2], wabs[:, 0:C], axis=AX.X))
            v.wait_ge(S["sdv"], 2)
            go(v.reciprocal(gain, deviation_v))
            for s, (g, m, be, b2, a) in enumerate((("g1m", "m1m", "be1m", "b12", "a1"), ("g2m", "m2m", "be2m", "b22", "a2"))):
                inv, sc, sh, less = (t[:, s:s+1] for t in (gain, scale, shift, one_less_slope))
                go(v.tensor_tensor(inv, inv, col[g], ALU.mult))
                go(v.tensor_scalar(sc, weight_sum[:, s:s+1], 1.0 / (C * (TAPS if s == 0 else 1)), inv, ALU.mult, ALU.mult))
                go(v.tensor_tensor(sh, col[m], inv, ALU.mult))
                go(v.tensor_tensor(sh, col[be], sh, ALU.subtract))
                go(v.tensor_tensor(sh, sh, col[b2], ALU.add))
                go(v.tensor_scalar(less, col[a], -1.0, 1.0, ALU.mult, ALU.add))
            go(v.tensor_scalar(excess_slope1, one_less_slope[:, 0:1], -1.0, None, ALU.mult))
            go(v.tensor_tensor(sign_shift2, col["b13"], col["b21"], ALU.add))
            go(v.tensor_tensor(last_shift, col["b13"], shift[:, 1:2], ALU.add))
            go(v.tensor_scalar(relu_shift2, last_shift, -1.0, None, ALU.mult))
            go(v.tensor_tensor(last_shift, last_shift, col["b23"], ALU.add))
            for s in range(2):
                go(v.tensor_tensor(wtmp[:, 0:16], wg[:, 0:16], att[:, 16*s:16*s+16], ALU.mult))
                go(v.reduce_sum(wg[:, 16+4*s:20+4*s], wtmp[:, 0:16].rearrange("p (h e) -> p h e", e=4), axis=AX.X))
            v.wait_ge(S["wT"], 1)
            wps = conv_ps[:, :].bitcast(BF16)
            v.tensor_copy(w1T[:, :, :], wps[:, 0:TAPS*P].rearrange("p (t o) -> p t o", o=P)).then_inc(S["wT"], 1)
            v.tensor_copy(w2T[:, :], wps[:, TAPS*P:(TAPS+1)*P]).then_inc(S["wT"], 1)
            v.wait_ge(S["wT"], 3)
            v.sem_inc(S["params"], 1)

            def moments(src, st, mv, s_st, s_bn, s_sd, s_rs, j):
                after(v, s_bn, j)
                for b in range(BLK):
                    last = v.bn_stats(st[:, b, :], src[:, b*P:(b+1)*P])
                last.then_inc(s_st, 1)
                after(v, s_st, j + 1)
                after(v, s_sd, j)
                after(v, s_rs, j)
                v.sem_inc(S["hold"], 1)
                for b in range(BLK):
                    last = v.bn_aggr(mv[:, b, :], st[:, b, :])
                last.then_inc(s_bn, 1)

            def scale_shift(sd, rs, nb, mv, s_sd, s_rc, s_rs, s_xt, j):
                after(v, s_sd, j + 1)
                after(v, s_xt, j)
                v.reciprocal(rs[:, :], sd[:, :]).then_inc(s_rc, 1)
                after(v, s_rc, j + 1)
                v.scalar_tensor_tensor(out=nb[:, :], in0=mv[:, :, 0], scalar=-1.0, in1=rs[:, :], op0=ALU.mult, op1=ALU.mult).then_inc(s_rs, 1)

            def body(k, at, turn):
                if there(k, 2):
                    after(v, S["conv"], k - 1)
                    after(v, S["xn"], k - 1)
                    after(v, S["out1"], k - 2)
                    v.scalar_tensor_tensor(out=z1[:, :], in0=conv_ps[:, :], scalar=scale[:, 0:1], in1=xn[:, at % 2, :],
                                           op0=ALU.mult, op1=ALU.add).then_inc(S["z1"], 1)
                    after(v, S["z1"], k - 1)
                    v.tensor_scalar(neg1[:, :], z1[:, :], 0.0, excess_slope1, ALU.min, ALU.mult).then_inc(S["neg1"], 1)
                if there(k, 5):
                    q = (at - 5) % 2
                    after(v, S["xnT2"], k - 4)
                    need(v, S["stt%d" % q], stored(at, turn, 5))
                    v.tensor_copy(tn[:, q, :], ln2_ps[:, :]).then_inc(S["tn"], 1)
                if there(k, 0):
                    after(v, S["xT1"], k + 1)
                    moments(ln1_ps[:, at % 2, :], stats1, mv1, S["st1"], S["bn1"], S["sd1"], S["rs1"], k)
                if there(k, 3):
                    after(v, S["conv2"], k - 2)
                    after(v, S["out2"], k - 3)
                    v.scalar_tensor_tensor(out=z2[:, :], in0=conv_ps[:, :], scalar=scale[:, 1:2], in1=out1[:, (at - 3) % 2, :],
                                           op0=ALU.mult, op1=ALU.add).then_inc(S["z2"], 1)
                if there(k, 0):
                    scale_shift(sd1, rs1, nb1, mv1, S["sd1"], S["rc1"], S["rs1"], S["xt1"], k)
                if there(k, 4):
                    after(v, S["xT2"], k - 3)
                    moments(ln2_ps[:, :], stats2, mv2, S["st2"], S["bn2"], S["sd2"], S["rs2"], k - 4)
                if there(k, 4):
                    scale_shift(sd2, rs2, nb2, mv2, S["sd2"], S["rc2"], S["rs2"], S["xt2"], k - 4)
                if there(k, 3):
                    after(v, S["neg2"], k - 2)
                    after(v, S["xm"], k - 3)
                    v.scalar_tensor_tensor(out=out2[:, :], in0=neg2[:, :], scalar=one_less_slope[:, 1:2], in1=z2[:, :],
                                           op0=ALU.mult, op1=ALU.add).then_inc(S["out2"], 1)
            rounds(v, FIRST, LAST, TAIL_ROUNDS, WIDE, body)

        @block.scalar
        def _(act):
            act.wait_ge(S["const"], 1)
            act.wait_ge(S["par"], 16 * len(NAMES))
            act.wait_ge(S["w"], 80)
            act.activation(deviation_v[:, 0:1], col["v1m"], ACT.Sqrt, bias=eps[:, 1:2]).then_inc(S["sdv"], 1)
            act.activation(deviation_v[:, 1:2], col["v2m"], ACT.Sqrt, bias=eps[:, 1:2]).then_inc(S["sdv"], 1)
            act.activation(w1s[:, :, :], w1f[:, :].rearrange("o (i t) -> o t i", t=TAPS), ACT.Sign).then_inc(S["wsg"], 1)
            act.activation(w2s[:, :], w2f[:, :], ACT.Sign).then_inc(S["wsg"], 1)
            act.wait_ge(S["params"], 1)

            def normal(xt, src, sd, mv, rs, nb, e, s_rc, s_bn, s_sd, s_rs, s_turned, s_xt, j):
                after(act, s_bn, j + 1)
                after(act, s_rc, j)
                act.activation(sd[:, :], mv[:, :, 1], ACT.Sqrt, bias=eps[:, e:e+1]).then_inc(s_sd, 1)
                yield
                after(act, s_rs, j + 1)
                after(act, s_turned, j)
                for b in range(BLK):
                    last = act.activation(xt[:, b*P:(b+1)*P], src[:, b*P:(b+1)*P], ACT.Identity, bias=nb[:, b:b+1], scale=rs[:, b:b+1])
                last.then_inc(s_xt, 1)

            def body(k, at, turn):
                if there(k, 3):
                    after(act, S["out1"], k - 2)
                    after(act, S["conv2"], k - 3)
                    act.activation(sg2[:, :], out1[:, (at - 3) % 2, :], ACT.Sign, bias=sign_shift2).then_inc(S["sg2"], 1)
                if there(k, 1):
                    p = (at - 1) % 2
                    after(act, S["xnT1"], k)
                    after(act, S["conv"], k - 2)
                    act.activation(sg1[:, p, 1:H+1, 1:W+1], ln1_ps[:, p, :].rearrange("p (h w) -> p h w", w=W),
                                   ACT.Sign, bias=col["b11"]).then_inc(S["sg1"], 1)
                if there(k, 1):
                    after(act, S["z1"], k - 2)
                    act.activation(xn[:, p, :], ln1_ps[:, p, :], ACT.Identity, bias=shift[:, 0:1]).then_inc(S["xn"], 1)
                if there(k, 5):
                    q = (at - 5) % 2
                    after(act, S["rows"], k - 4)
                    need(act, S["str%d" % q], stored(at, turn, 5))
                    act.activation(agg[:, bass.ds((k - 5) * BLK, BLK), :], ln2_ps[:, 0:BLK*ROW].rearrange("p (b r) -> p b r", r=ROW)[:, :, 0:16], ACT.Identity)
                    act.activation(rw[:, q, :, :], ln2_ps[:, 0:BLK*ROW].rearrange("p (b r) -> p b r", r=ROW), ACT.Identity).then_inc(S["rw"], 1)
                if there(k, 0):
                    one = normal(xt1, ln1_ps[:, at % 2, :], sd1, mv1, rs1, nb1, 0, S["rc1"], S["bn1"], S["sd1"], S["rs1"], S["xnT1"], S["xt1"], k)
                    next(one)
                if there(k, 3):
                    after(act, S["z2"], k - 2)
                    after(act, S["out2"], k - 3)
                    act.activation(neg2[:, :], z2[:, :], ACT.Relu, bias=relu_shift2, scale=-1.0).then_inc(S["neg2"], 1)
                if there(k, 0):
                    next(one, None)
                if there(k, 4):
                    two = normal(xt2, ln2_ps[:, :], sd2, mv2, rs2, nb2, 1, S["rc2"], S["bn2"], S["sd2"], S["rs2"], S["xnT2"], S["xt2"], k - 4)
                    next(two)
                    next(two, None)
            rounds(act, FIRST, LAST, TAIL_ROUNDS, WIDE, body)


def sorter(nc, edges_d, keys_d, half, flag):
    with ExitStack() as ctx:
        def sb(name, shape, dt=F32): return ctx.enter_context(nc.sbuf_tensor(f"s{half}_{name}", shape, dt))
        ping = sb("ping", [P, EDGE_COLS]); pong = sb("pong", [P, EDGE_COLS]); upper = sb("upper", [P, EDGE_COLS])
        src = sb("src", [P, EDGE_COLS], I32); dst = sb("dst", [P, EDGE_COLS], I32); word = sb("word", [P, EDGE_COLS], I32)
        hi_half = sb("hi_half", [P, EDGE_COLS // 2])
        lane = sb("lane", [P, 8], I32); sign = sb("sign", [P, 8]); turn_sign = sb("turn_sign", [P, 8])
        ident = sb("ident", [P, P]); pad = sb("pad", [P, TAIL // P]); top = sb("top", [P, 1]); topf = sb("topf", [1, 1])
        u_a = sb("u_a", [P, HEAD_COLS]); u_b = sb("u_b", [P, HEAD_COLS])
        turned_ps = ctx.enter_context(nc.psum_tensor(f"s{half}_turned", [P, EDGE_COLS], F32))
        loaded, const, ident_ok, done, to_turn, turned, copied, tables, storable, stored, u_back, flagged = (
            ctx.enter_context(semaphores(nc, f"s{half}", "loaded const ident done to_turn turned copied tables storable stored u_back flagged")).values())
        block = ctx.enter_context(nc.Block())
        edge_rows = [edges_d[r:r+1, :].rearrange("a (p f) -> (a p) f", p=P) for r in range(2)]
        low_rows = keys_d[1:1 + EDGES].rearrange("(p f) -> p f", p=P)
        high_flat = keys_d[1 + EDGES:1 + EDGES + HALF]
        CROSS = 2 * PART_BITS + 2

        final_low, final_high = [ping], [u_b]

        @block.sync
        def _(sp):
            sp.dma_start(src[:, :], edge_rows[0]).then_inc(loaded, 16)
            sp.dma_start(dst[:, :], edge_rows[1]).then_inc(loaded, 16)
            sp.wait_ge(const, 1)
            sp.dma_start(keys_d[0:1].rearrange("(a b) -> a b", a=1), pad[0:1, 0:1]).then_inc(stored, 16)
            sp.dma_start(keys_d[1 + EDGES + HALF:1 + EDGES + HALF + TAIL].rearrange("(a b) -> a b", a=P), pad[:, :]).then_inc(stored, 16)
            sp.wait_ge(storable, 1)
            sp.dma_start(high_flat.rearrange("(p f) -> p f", f=EDGE_COLS), upper[P - HALF // EDGE_COLS:P, :]).then_inc(stored, 16)
            sp.wait_ge(stored, 48)
            sp.dma_start(u_a[:, :], high_flat.rearrange("(p f) -> p f", p=P)).then_inc(u_back, 16)
            sp.wait_ge(storable, 2)
            sp.dma_start(low_rows, final_low[0][:, :]).then_inc(stored, 16)
            sp.wait_ge(storable, 3)
            sp.dma_start(high_flat.rearrange("(p f) -> p f", p=P), final_high[0][:, :]).then_inc(stored, 16)
            sp.wait_ge(stored, 80)

        crossing_source = []

        def halves(ap, span, mirrored=False):
            v = ap.rearrange("p (g two h) -> p g two h", two=2, h=span)
            return v[:, :, 0, :], (v[:, :, 1, ::-1] if mirrored else v[:, :, 1, :])

        def chunk_of(ap, x, span, c):
            lo, hi = halves(ap, span)
            if x % 2 == 0:
                n = lo.shape[1] // TURN_CHUNKS
                return lo[:, c*n:(c+1)*n, :], hi[:, c*n:(c+1)*n, :]
            n = span // TURN_CHUNKS
            return lo[:, :, c*n:(c+1)*n], hi[:, :, c*n:(c+1)*n]

        spans = []
        for k in [*range(1, PART_BITS + 1), PART_BITS]:
            spans += [1 << (k - 1), 1 << (COL_BITS - 1)]

        def copy_of(x, c):
            n = EDGE_COLS // 2 // TURN_CHUNKS
            _, hi = chunk_of(turned_ps[:, :], x, spans[x], c)
            return hi_half[:, c*n:(c+1)*n].rearrange("p (g h) -> p g h", h=hi.shape[2])
        def u_copy(x):
            return hi_half[:, 0:HEAD_COLS//2].rearrange("p (g h) -> p g h", h=(64, 128)[x])
        u_source = (u_a, u_b)
        @block.vector
        def _(v):
            count = [0]
            def go(i):
                count[0] += 1
                i.then_inc(done, 1)
            def settle():
                v.wait_ge(done, count[0])
            edge_clamp, edge_op = ([float(HALF - SHIFT - 1)], ALU.min) if half == 0 else ([-float(SHIFT)], ALU.max)
            def words(word_f):
                base = HALF * half + SHIFT
                settle()
                if half == 0:
                    go(v.tensor_scalar(upper_scratch, dst[:, :], base + (HALF - SHIFT) - 0.5, 16.0, ALU.subtract, ALU.mult))
                else:
                    go(v.tensor_scalar(upper_scratch, dst[:, :], base - SHIFT - 0.5, -16.0, ALU.subtract, ALU.mult))
                go(v.tensor_tensor(src[:, :], src[:, :], dst[:, :], ALU.bitwise_xor)); settle()
                go(v.tensor_scalar(word[:, :], dst[:, :], float(base), *edge_clamp, ALU.subtract, edge_op)); settle()
                go(v.tensor_scalar(dst[:, :], word[:, :], float(LEAST), -1.0, ALU.is_lt, ALU.mult)); settle()
                go(v.scalar_tensor_tensor(out=word[:, :], in0=dst[:, :], scalar=-float(FLIP), in1=word[:, :], op0=ALU.mult, op1=ALU.add)); settle()
                go(v.tensor_scalar(word[:, :], word[:, :], 16, None, ALU.logical_shift_left)); settle()
                go(v.tensor_tensor(word[:, :], word[:, :], src[:, :], ALU.bitwise_or)); settle()
                go(v.tensor_tensor(word[:, :], word[:, :], dst[:, :], ALU.bitwise_xor)); settle()
                go(v.tensor_tensor(word_f, word[:, :].bitcast(F32), upper_scratch, ALU.max)); settle()
            v.wait_ge(loaded, 32)
            if flag is not None:
                go(v.tensor_reduce(top[:, :], dst[:, :], AX.X, ALU.max))
            upper_scratch = upper[:, :]
            words(ping[:, :])
            v.wait_ge(tables, 1)
            for k in range(8):
                go(v.tensor_scalar(lane[:, k:k+1], lane[:, 0:1], k, 1, ALU.logical_shift_right, ALU.bitwise_and)) if k else None
            settle()
            go(v.tensor_scalar(lane[:, 0:1], lane[:, 0:1], 1, None, ALU.bitwise_and)); settle()
            go(v.tensor_scalar(sign[:, :], lane[:, :], -2.0, 1.0, ALU.mult, ALU.add)); settle()
            go(v.tensor_copy(turn_sign[:, 0:1], sign[:, 0:1]))
            go(v.tensor_tensor(turn_sign[:, 1:8], sign[:, 0:7], sign[:, 1:8], ALU.mult)); settle()
            a, b = ping, pong
            go(v.tensor_scalar(b[:, :], a[:, :], turn_sign[:, 0:1], None, ALU.mult)); settle()
            v.sem_inc(tables, 1)
            a, b = b, a

            def step(a, b, span, mirrored=False):
                lo, hi = halves(a[:, :], span, mirrored)
                olo, ohi = halves(b[:, :], span, mirrored)
                go(v.tensor_tensor(olo, lo, hi, ALU.min))
                go(v.tensor_tensor(ohi, lo, hi, ALU.max))
                settle()
                return b, a

            def cross(a, b):
                x = len(crossing_source)
                crossing_source.append(a)
                v.sem_inc(to_turn, 1)
                for c in range(TURN_CHUNKS):
                    lo, _ = chunk_of(turned_ps[:, :], x, spans[x], c)
                    olo, ohi = chunk_of(b[:, :], x, spans[x], c)
                    hi = copy_of(x, c)
                    v.wait_ge(copied, TURN_CHUNKS * x + c + 1)
                    go(v.tensor_tensor(olo, lo, hi, ALU.min))
                    go(v.tensor_tensor(ohi, lo, hi, ALU.max))
                settle()
                return b, a

            for level in range(1, COL_BITS + 1):
                for s in range(level, 0, -1):
                    a, b = step(a, b, 1 << (s - 1), mirrored=(s == level))
            for k in range(1, PART_BITS + 1):
                go(v.tensor_scalar(b[:, :], a[:, :], turn_sign[:, k:k+1] if k < PART_BITS else sign[:, PART_BITS-1:PART_BITS], None, ALU.mult)); settle()
                a, b = b, a
                a, b = cross(a, b)
                for s in range(k - 1, 0, -1):
                    a, b = step(a, b, 1 << (s - 1))
                a, b = cross(a, b)
                for s in range(COL_BITS - 1, 0, -1):
                    a, b = step(a, b, 1 << (s - 1))
            v.wait_ge(tables, 3)
            if half:
                go(v.tensor_scalar(b[:, :], dst[:, :], HALF - 0.5, 16.0, ALU.subtract, ALU.mult))
                go(v.tensor_scalar(src[:, :], dst[:, :], float(HALF), 2.0 * HALF - 1, ALU.add, ALU.min)); settle()
                go(v.tensor_copy(dst[:, :], src[:, :])); settle()
                words(upper[:, :])
                go(v.tensor_tensor(upper[:, :], upper[:, :], b[:, :], ALU.max)); settle()
            else:
                go(v.tensor_copy(src[:, :], dst[:, :])); settle()
                words(upper[:, :])
            go(v.tensor_tensor(b[:, :], a[:, :], upper[:, :], ALU.min))
            go(v.tensor_tensor(upper[:, :], a[:, :], upper[:, :], ALU.max)); settle()
            v.sem_inc(storable, 1)
            a, b = b, a
            a, b = cross(a, b)
            for s in range(PART_BITS - 1, 0, -1):
                a, b = step(a, b, 1 << (s - 1))
            a, b = cross(a, b)
            for s in range(COL_BITS - 1, 0, -1):
                a, b = step(a, b, 1 << (s - 1))
            assert a is final_low[0], "low"
            v.sem_inc(storable, 1)
            v.wait_ge(u_back, 16)
            ua, ub = u_a, u_b
            for x, (top_bit) in enumerate((PART_BITS, COL_BITS - 4)):
                v.sem_inc(to_turn, 1)
                v.wait_ge(copied, TURN_CHUNKS * CROSS + x + 1)
                lo, _ = halves(turned_ps[:, 0:HEAD_COLS], 1 << (top_bit - 1))
                olo, ohi = halves(ub[:, :], 1 << (top_bit - 1))
                hi = u_copy(x)
                go(v.tensor_tensor(olo, lo, hi, ALU.min))
                go(v.tensor_tensor(ohi, lo, hi, ALU.max)); settle()
                ua, ub = ub, ua
                for s in range(top_bit - 1, 0, -1):
                    ua, ub = step(ua, ub, 1 << (s - 1))
                if x == 0:
                    assert ua is u_source[1], "u"
            assert ua is final_high[0], "high"
            v.sem_inc(storable, 1)
            if flag is not None:
                v.sem_inc(flagged, 1)
                v.wait_ge(flagged, 2)
                go(v.tensor_reduce(topf[:, :], turned_ps[0:1, 0:P], AX.X, ALU.max)); settle()
                go(v.tensor_scalar(flag, topf[:, :], float(HALF), None, ALU.is_ge)); settle()

        @block.gpsimd
        def _(pool):
            pool.memset(ident[:, :], 0.0)
            pool.memset(pad[:, :], 1e4).then_inc(const, 1)
            pool.iota(lane[:, 0:1], [[0, 1]], base=0, channel_multiplier=1).then_inc(tables, 1)
            pool.wait_ge(const, 1)
            pool.affine_select(out=ident[:, :], in_=ident[:, :], compare_op=ALU.not_equal, fill=1.0, base=0,
                               pattern=[[-1, P]], channel_multiplier=1).then_inc(ident_ok, 1)
            pool.wait_ge(tables, 2)
            pool.iota(dst[:, :], [[-1, EDGE_COLS]], base=EDGES - 1, channel_multiplier=-EDGE_COLS).then_inc(tables, 1)

        @block.scalar
        def _(act):
            for x in range(CROSS):
                for c in range(TURN_CHUNKS):
                    act.wait_ge(turned, TURN_CHUNKS * x + c + 1)
                    _, hi = chunk_of(turned_ps[:, :], x, spans[x], c)
                    act.activation(copy_of(x, c), hi, ACT.Copy).then_inc(copied, 1)
            for x in range(2):
                act.wait_ge(turned, TURN_CHUNKS * CROSS + x + 1)
                _, hi = halves(turned_ps[:, 0:HEAD_COLS], (64, 128)[x])
                act.activation(u_copy(x), hi, ACT.Copy).then_inc(copied, 1)
        @block.tensor
        def _(pe):
            pe.wait_ge(ident_ok, 1)
            blocks = EDGE_COLS // P
            per = blocks // TURN_CHUNKS
            for x in range(CROSS):
                pe.wait_ge(to_turn, x + 1)
                source = crossing_source[x]
                for c in range(TURN_CHUNKS):
                    if x % 2 == 0:
                        which = range(c * per, (c + 1) * per)
                    else:
                        a = range(c * per // 2, (c + 1) * per // 2)
                        which = [*a, *(g + blocks // 2 for g in a)]
                    for g in which:
                        last = pe.transpose(turned_ps[:, g*P:(g+1)*P], source[:, g*P:(g+1)*P], ident[:, :])
                    last.then_inc(turned, 1)
            for x in range(2):
                pe.wait_ge(to_turn, CROSS + x + 1)
                source = (u_a, u_b)[x]
                for g in range(HEAD_COLS // P):
                    last = pe.transpose(turned_ps[:, g*P:(g+1)*P], source[:, g*P:(g+1)*P], ident[:, :])
                last.then_inc(turned, 1)
            if flag is not None:
                pe.wait_ge(flagged, 1)
                pe.transpose(turned_ps[0:1, 0:P], top[:, :], ident[:, :]).then_inc(flagged, 1)



def attention(nc, edges_d, keys_d, rows_d, res_d, agg, half, gathers, make_experts=None, finish=None):
    with ExitStack() as ctx, ExitStack() as during:
        def keep(name, shape, dt=F32): return ctx.enter_context(nc.sbuf_tensor(f"e{half}_{name}", shape, dt))
        def sb(name, shape, dt=F32): return during.enter_context(nc.sbuf_tensor(f"e{half}_{name}", shape, dt))
        prev_seg, first_seg, last_seg = (keep(n, [P, 1]) for n in ("prev_seg", "first_seg", "last_seg"))
        iota_f, zlast, counts = keep("iota_f", [P, HIS]), keep("zlast", [P, ROW]), keep("counts", [P, HIS])
        x = make_experts(during) if make_experts else None
        key = sb("key", [P, 2, COLS + 1], I32)
        sgn = sb("sgn", [P, COLS + 1], I32); mag = sb("mag", [P, COLS + 1], I32); low = sb("low", [P, COLS + 1], I32)
        seg = sb("seg", [P, COLS + 1], I32); dfull = sb("dfull", [P, COLS + 1], I32)
        index = sb("index", [P, 2, COLS], I32); first = sb("first", [P, 1], I32)
        start = sb("start", [P, 2, COLS]); cont = sb("cont", [P, 2, COLS]); cut = sb("cut", [P, 2, COLS])
        got = sb("got", [P, 2, COLS, ROW]); head0 = sb("head0", [P, ROW])
        adv = sb("adv", [P, HEADS, COLS]); ad = sb("ad", [P, 2, HEADS, COLS]); e = sb("e", [P, HEADS, COLS])
        mx = sb("mx", [P, 2, HEADS, COLS + 1]); dif = sb("dif", [P, 2, HEADS, COLS]); rp = sb("rp", [P, 2, HEADS, COLS])
        wgt = sb("wgt", [P, HEADS, EXPERTS, COLS]); out = sb("out", [P, 2, COLS, ROW])
        tgt = sb("tgt", [P, 2, COUNT_TILES], I32); tlo_i = sb("tlo_i", [P, COUNT_TILES], I32); thi_i = sb("thi_i", [P, COUNT_TILES], I32)
        tlo = sb("tlo", [P, COUNT_TILES]); thi = sb("thi", [P, COUNT_TILES])
        iota_i = sb("iota_i", [P, HIS], I32); iota_b = sb("iota_b", [P, HIS], BF16)
        is_lo = sb("is_lo", [P, 2, RING, P], BF16); is_hi = sb("is_hi", [P, 2, RING, HIS], BF16)
        count_ps = during.enter_context(nc.psum_tensor(f"e{half}_count_ps", [P, 512], F32))
        S = dict(during.enter_context(semaphores(nc, f"e{half}", "key0 key1 dec idx init proc dif exp out st0 st1 tgt0 tgt1 cnt_d hot hit edge iot free")))
        S.update({n: gathers(f"e{half}_{n}") for n in ("gat0", "gat1", "gat2", "gat3", "head")})
        DEC, PROC, CNT = 12, 37, 4

        LAST = CHUNKS + 1
        def decodes(k): return not isinstance(k, int) or k < CHUNKS
        def attends(k): return not isinstance(k, int) or k >= 1

        key_rows = lambda k: keys_d[bass.ds(k * COLS, P * RUN)].rearrange("(q f) -> q f", f=RUN)[:, 0:COLS + 1]
        tgt_rows = lambda k: edges_d[1:2, bass.ds(k * (P * COUNT_TILES), P * COUNT_TILES)].rearrange("a (p f) -> (a p) f", p=P)
        res_rows = res_d.rearrange("(q f) r -> q (f r)", f=RUN)

        with nc.Block() as block:
            @block.sync
            def _(sp):
                if x: x.start_sync(sp)
                for u in range(2):
                    sp.dma_start(key[:, u, :].bitcast(F32), key_rows(u)).then_inc(S["key%d" % u], 16)
                    sp.dma_start(tgt[:, u, :], tgt_rows(u)).then_inc(S["tgt%d" % u], 16)
                def body(k, at, turn):
                    if attends(k):
                        q = (at - 1) % 2
                        need(sp, S["out"], k)
                        sp.dma_start(res_rows[:, bass.ds((k - 1) * (COLS * ROW), COLS * ROW)],
                                     out[:, q, :, :].rearrange("p f r -> p (f r)")).then_inc(S["st%d" % q], 16)
                    if not isinstance(k, int) or k + 2 < CHUNKS:
                        u = at % 2
                        need(sp, S["dec"], DEC * (k + 1))
                        sp.dma_start(key[:, u, :].bitcast(F32), key_rows(k + 2)).then_inc(S["key%d" % u], 16)
                        need(sp, S["cnt_d"], CNT * (k + 1))
                        sp.dma_start(tgt[:, u, :], tgt_rows(k + 2)).then_inc(S["tgt%d" % u], 16)
                    if x: x.sync(sp, k, at, turn, 4)
                rounds(sp, 6, LAST, 3, 4, body)
                for q in range(2):
                    sp.wait_ge(S["st%d" % q], 16 * CHUNKS // 2)
                if x: x.end_sync(sp)

            @block.gpsimd
            def _(pool):
                pool.iota(iota_i[:, :], [[1, HIS]], base=0, channel_multiplier=0).then_inc(S["iot"], 1)
                if x: x.start_gpsimd(pool)
                pool.wait_ge(S["edge"], 1)
                pool.indirect_dma_start(head0[:, :], None, rows_d, bass.IndirectOffsetOnAxis(ap=first[:, :], axis=0)).then_inc(S["head"], 16)
                def body(k, at, turn):
                    if decodes(k):
                        need(pool, S["idx"], k + 1)
                        need(pool, S["out"], k - 1)
                        pool.sem_inc(S["free"], 1)
                        for c in range(COLS):
                            pool.indirect_dma_start(got[:, at % 2, c, :], None, rows_d,
                                bass.IndirectOffsetOnAxis(ap=index[:, at % 2, c:c+1], axis=0)).then_inc(S["gat%d" % (at % 4)], 16)
                rounds(pool, 6, LAST, 3, 4, body)

            @block.tensor
            def _(pe):
                if x: x.start_tensor(pe)
                def body(k, at, turn):
                    if decodes(k):
                        def count(g):
                            need(pe, S["hot"], k * (COUNT_TILES // RING) + g + 1)
                            for t in range(RING):
                                last = pe.matmul(count_ps[:, 0:HIS], is_lo[:, g % 2, t, :], is_hi[:, g % 2, t, :],
                                                 start=(isinstance(k, int) and k == 0 and g == 0 and t == 0),
                                                 stop=(isinstance(k, int) and k == CHUNKS - 1 and g == COUNT_TILES // RING - 1 and t == RING - 1))
                            last.then_inc(S["hit"], 1)
                        if x:
                            x.tensor(pe, k, at, turn, 4, count)
                        else:
                            for g in range(COUNT_TILES // RING):
                                count(g)
                rounds(pe, 6, LAST, 3, 4, body)

            @block.scalar
            def _(act):
                if x: act.wait_ge(x.S["w"], x.WEIGHTS)
                def body(k, at, turn):
                    if x and isinstance(k, int) and k < x.WEIGHINGS:
                        x.weigh_scalar(act, k)
                    if attends(k):
                        need(act, S["dif"], k)
                        act.activation(rp[:, :, :, :], dif[:, :, :, :], ACT.Exp).then_inc(S["exp"], 1)
                    if x: x.scalar(act, k, at, turn, 4)
                rounds(act, 6, LAST, 3, 4, body)

            @block.vector
            def _(v):
                v.wait_ge(S["iot"], 1)
                v.tensor_copy(iota_f[:, :], iota_i[:, :]).then_inc(S["iot"], 1)
                v.tensor_copy(iota_b[:, :], iota_i[:, :]).then_inc(S["iot"], 1)

                def body(k, at, turn):
                    if decodes(k):
                        u = at % 2
                        i = [0]
                        def go(ins):
                            i[0] += 1
                            ins.then_inc(S["dec"], 1)
                            v.wait_ge(S["dec"], DEC * k + i[0])
                        v.wait_ge(S["key%d" % u], 16 * (at // 2 + 1) + 32 * turn)
                        kk = key[:, u, :]
                        go(v.tensor_scalar(sgn[:, :], kk, 31, None, ALU.arith_shift_right))
                        go(v.tensor_tensor(mag[:, :], kk, sgn[:, :], ALU.bitwise_xor))
                        go(v.tensor_scalar(low[:, :], mag[:, :], 16, None, ALU.logical_shift_right))
                        go(v.scalar_tensor_tensor(out=seg[:, :], in0=sgn[:, :], scalar=float(FLIP), in1=low[:, :], op0=ALU.mult, op1=ALU.add))
                        go(v.tensor_scalar(dfull[:, :], seg[:, :], float(SHIFT + HALF * half), None, ALU.add))
                        go(v.tensor_tensor(mag[:, :], mag[:, :], dfull[:, :], ALU.bitwise_xor))
                        if not isinstance(k, int) or k >= 2:
                            v.wait_ge(S["gat%d" % ((at - 2) % 4)], 16 * COLS * ((at - 2) // 4 + 1) + 16 * COLS * turn)
                        go(v.tensor_scalar(index[:, u, :], mag[:, 1:COLS+1], 65535, None, ALU.bitwise_and))
                        v.sem_inc(S["idx"], 1)
                        go(v.tensor_tensor(start[:, u, :], seg[:, 1:COLS+1], seg[:, 0:COLS], ALU.not_equal))
                        go(v.tensor_scalar(cont[:, u, :], start[:, u, :], -1.0, 1.0, ALU.mult, ALU.add))
                        go(v.tensor_scalar(cut[:, u, :], start[:, u, :], -BIG, None, ALU.mult))
                        if isinstance(k, int) and k == 0:
                            go(v.tensor_copy(prev_seg[:, :], seg[:, 0:1]))
                            go(v.tensor_copy(first_seg[:, :], seg[:, 1:2]))
                            v.tensor_scalar(first[:, :], dfull[:, 1:2], 65535, None, ALU.bitwise_and).then_inc(S["edge"], 1)
                        else:
                            for _ in range(2):
                                go(v.tensor_copy(last_seg[:, :], seg[:, COLS:COLS+1]))
                        assert i[0] == DEC
                        if x and isinstance(k, int) and k < x.WEIGHINGS:
                            x.weigh_vector(v, k)
                            if k == 0:
                                x.start_vector(v)
                        v.wait_ge(S["tgt%d" % u], 16 * (at // 2 + 1) + 32 * turn)
                        need(v, S["hit"], k * (COUNT_TILES // RING))
                        c = S["cnt_d"]
                        v.tensor_scalar(tlo_i[:, :], tgt[:, u, :], P - 1, None, ALU.bitwise_and).then_inc(c, 1)
                        v.tensor_scalar(thi_i[:, :], tgt[:, u, :], 7, None, ALU.logical_shift_right).then_inc(c, 1)
                        v.wait_ge(c, CNT * k + 2)
                        v.tensor_copy(tlo[:, :], tlo_i[:, :]).then_inc(c, 1)
                        v.tensor_scalar(thi[:, :], thi_i[:, :], float(HIS * half), None, ALU.subtract).then_inc(c, 1)
                        v.wait_ge(c, CNT * k + 4)
                        v.wait_ge(S["iot"], 3)
                    if attends(k):
                        q = (at - 1) % 2
                        j = k - 1
                        i = [0]
                        def go(ins):
                            i[0] += 1
                            ins.then_inc(S["proc"], 1)
                        def settle():
                            v.wait_ge(S["proc"], PROC * j + i[0])
                        if isinstance(k, int) and k == 1:
                            v.wait_ge(S["head"], 16)
                            v.tensor_copy(ad[:, 1, :, COLS-1], head0[:, 20:24]).then_inc(S["init"], 1)
                            v.memset(mx[:, 1, :, COLS], -BIG).then_inc(S["init"], 1)
                            v.memset(out[:, 1, :, :], 0.0).then_inc(S["init"], 1)
                            v.wait_ge(S["init"], 3)
                        v.wait_ge(S["gat%d" % ((at - 1) % 4)], 16 * COLS * ((at - 1) // 4 + 1) + 16 * COLS * turn)
                        if not isinstance(k, int) or k >= 3:
                            v.wait_ge(S["st%d" % q], 16 * ((at - 1) // 2) + 32 * turn)
                        g = got[:, q, :, :]
                        by_head = lambda ap: ap.unsqueeze(1).broadcast_to([P, HEADS, COLS])
                        go(v.tensor_tensor(adv[:, :, :], g[:, :, 20:24].rearrange("p c h -> p h c"), by_head(start[:, q, :]), ALU.mult)); settle()
                        for h in range(HEADS):
                            go(v.tensor_tensor_scan(ad[:, q, h, :], cont[:, q, :], adv[:, h, :], ad[:, 1 - q, h, COLS-1:COLS], ALU.mult, ALU.add))
                        settle()
                        go(v.tensor_tensor(e[:, :, :], ad[:, q, :, :], g[:, :, 16:20].rearrange("p c h -> p h c"), ALU.add)); settle()
                        go(v.scalar_tensor_tensor(out=e[:, :, :], in0=e[:, :, :], scalar=0.2, in1=e[:, :, :], op0=ALU.mult, op1=ALU.max))
                        go(v.tensor_copy(mx[:, q, :, 0], mx[:, 1 - q, :, COLS])); settle()
                        for h in range(HEADS):
                            go(v.tensor_tensor_scan(mx[:, q, h, 1:COLS+1], cut[:, q, :], e[:, h, :], mx[:, 1 - q, h, COLS:COLS+1], ALU.add, ALU.max))
                        settle()
                        go(v.tensor_tensor(dif[:, 0, :, :], mx[:, q, :, 0:COLS], by_head(cut[:, q, :]), ALU.add)); settle()
                        go(v.tensor_tensor(dif[:, 0, :, :], dif[:, 0, :, :], mx[:, q, :, 1:COLS+1], ALU.subtract))
                        go(v.tensor_tensor(dif[:, 1, :, :], e[:, :, :], mx[:, q, :, 1:COLS+1], ALU.subtract)); settle()
                        v.sem_inc(S["dif"], 1)
                        go(v.tensor_copy(out[:, q, :, 20:24].rearrange("p c h -> p h c"), mx[:, q, :, 1:COLS+1]))
                        v.wait_ge(S["exp"], k)
                        go(v.tensor_tensor(wgt[:, :, :, :], g[:, :, 0:16].rearrange("p c (h x) -> p h x c", x=EXPERTS),
                                           rp[:, 1, :, :].unsqueeze(2).broadcast_to([P, HEADS, EXPERTS, COLS]), ALU.mult)); settle()
                        for h in range(HEADS):
                            for w in range(EXPERTS + 1):
                                ch = h * EXPERTS + w if w < EXPERTS else HEADS * EXPERTS + h
                                data = wgt[:, h, w, :] if w < EXPERTS else rp[:, 1, h, :]
                                go(v.tensor_tensor_scan(out[:, q, :, ch], rp[:, 0, h, :], data, out[:, 1 - q, COLS-1, ch:ch+1], ALU.mult, ALU.add))
                        settle()
                        v.sem_inc(S["out"], 1)
                        assert i[0] == PROC, i[0]
                    def one_hot(g):
                        if (isinstance(k, int) and k > 0) or not isinstance(k, int) or g >= 2:
                            v.wait_ge(S["hit"], k * (COUNT_TILES // RING) + g - 1)
                        for t in range(RING):
                            n = g * RING + t
                            v.tensor_scalar(is_lo[:, g % 2, t, :], iota_b[:, 0:P], tlo[:, n:n+1], None, ALU.is_equal)
                            last = v.tensor_scalar(is_hi[:, g % 2, t, :], iota_b[:, :], thi[:, n:n+1], None, ALU.is_equal)
                        last.then_inc(S["hot"], 1)
                    if x:
                        x.vector(v, k, at, turn, 4, one_hot)
                    elif decodes(k):
                        for g in range(COUNT_TILES // RING):
                            one_hot(g)
                rounds(v, 6, LAST, 3, 4, body)
                v.wait_ge(S["hit"], CHUNKS * COUNT_TILES // RING)
                v.tensor_scalar(counts[:, :], count_ps[:, 0:HIS], 1.0, None, ALU.add).then_inc(S["iot"], 1)
                v.tensor_copy(zlast[:, :], out[:, (CHUNKS - 1) % 2, COLS-1, :]).then_inc(S["iot"], 1)
                v.wait_ge(S["iot"], 5)

        during.close()
        gather_tokens(nc, ctx, res_d, agg, half, gathers, zlast, counts, prev_seg, first_seg, last_seg, iota_f, finish)

def gather_tokens(nc, ctx, res_d, agg, half, gathers, zlast, counts, prev_seg, first_seg, last_seg, iota_f, finish):
    def sb(name, shape, dt=F32): return ctx.enter_context(nc.sbuf_tensor(f"e{half}_{name}", shape, dt))
    def ps(name, shape, dt=F32): return ctx.enter_context(nc.psum_tensor(f"e{half}_{name}", shape, dt))
    CH = HEADS * (EXPERTS + 1)
    ident = sb("g_ident", [P, P]); ones = sb("g_ones", [P, P]); upto = sb("g_upto", [P, P])
    total = sb("g_total", [P, HIS]); before = sb("g_before", [P, HIS]); pos = sb("g_pos", [P, HIS]); pos_i = sb("g_pos_i", [P, HIS], I32)
    tok = sb("g_tok", [P, 1]); tok_i = sb("g_tok_i", [P, 1], I32); lo_i = sb("g_lo_i", [P, 1], I32); hi_i = sb("g_hi_i", [P, 1], I32)
    lo_f = sb("g_lo_f", [P, 1]); hi_f = sb("g_hi_f", [P, 1])
    one_lo = sb("g_one_lo", [P, P]); one_lo_t = sb("g_one_lo_t", [P, P]); one_hi = sb("g_one_hi", [P, HIS]); picked = sb("g_picked", [P, HIS])
    end = sb("g_end", [P, 1]); lane_end = sb("g_lane_end", [P, 1]); lane_i = sb("g_lane_i", [P, 1], I32)
    t1 = sb("g_t1", [P, 1]); t2 = sb("g_t2", [P, 1]); skip = sb("g_skip", [P, 1]); at_i = sb("g_at_i", [P, 1], I32); to_i = sb("g_to_i", [P, 1], I32)
    z = sb("g_z", [P, 3, CH]); zt = sb("g_zt", [CH, 3, P]); mm = sb("g_mm", [CH, P + 1]); ss = sb("g_ss", [CH, P + 1])
    dd = sb("g_dd", [CH, 2, P]); ee = sb("g_ee", [CH, 2, P]); ww = sb("g_ww", [CH, P])
    cin = sb("g_cin", [P, 2, CH]); row = sb("g_row", [P, ROW]); rm = sb("g_rm", [P, CH]); nm = sb("g_nm", [P, CH])
    d2 = sb("g_d2", [P, 2, CH]); e2 = sb("g_e2", [P, 2, CH]); new = sb("g_new", [P, ROW])
    PER = 8
    tidx = sb("g_tidx", [P, 2, PER], I32); trow = sb("g_trow", [P, 2, PER, ROW]); tsum = sb("g_tsum", [P, 2, PER, HEADS]); trec = sb("g_trec", [P, 2, PER, HEADS])
    a_ps = ps("g_a_ps", [P, 512]); b_ps = ps("g_b_ps", [P, 512]); c_ps = ps("g_c_ps", [P, 512])
    S = dict(ctx.enter_context(semaphores(nc, f"g{half}", "const c2 dv pe act got idx agg dn free")))
    S.update({n: gathers(f"g{half}_{n}") for n in ("put", "tg0", "tg1")})
    TURNS = HIS // PER
    with nc.Block() as block:
        dv, pe_s = S["dv"], S["pe"]
        @block.gpsimd
        def _(pool):
            pool.memset(ident[:, :], 0.0)
            pool.memset(ones[:, :], 1.0)
            pool.memset(upto[:, :], 1.0).then_inc(S["const"], 1)
            pool.wait_ge(S["const"], 1)
            pool.iota(lane_i[:, :], [[0, 1]], base=RUN - 1, channel_multiplier=RUN)
            pool.affine_select(out=ident[:, :], in_=ident[:, :], compare_op=ALU.not_equal, fill=1.0, base=0, pattern=[[-1, P]], channel_multiplier=1)
            pool.affine_select(out=upto[:, :], in_=upto[:, :], compare_op=ALU.is_ge, fill=0.0, base=0, pattern=[[1, P]], channel_multiplier=-1).then_inc(S["const"], 1)
            pool.wait_ge(S["got"], 1)
            pool.indirect_dma_start(row[:, :], None, res_d, bass.IndirectOffsetOnAxis(ap=at_i[:, :], axis=0)).then_inc(S["put"], 16)
            pool.wait_ge(S["got"], 2)
            pool.indirect_dma_start(res_d, bass.IndirectOffsetOnAxis(ap=to_i[:, :], axis=0), new[:, :], None,
                                    bounds_check=ENTRIES - 1, oob_is_err=False).then_inc(S["put"], 16)
            pool.wait_ge(S["put"], 32)
            def body(k, at, turn):
                if not isinstance(k, int) or k < TURNS:
                    need(pool, S["idx"], k + 1)
                    need(pool, S["agg"], k - 1)
                    pool.sem_inc(S["free"], 1)
                    for c in range(PER):
                        pool.indirect_dma_start(trow[:, at % 2, c, :], None, res_d,
                            bass.IndirectOffsetOnAxis(ap=tidx[:, at % 2, c:c+1], axis=0)).then_inc(S["tg%d" % (at % 2)], 16)
            if not finish:
                rounds(pool, 2, TURNS + 1, 1, 2, body)

        @block.tensor
        def _(pe):
            pe.wait_ge(S["const"], 2)
            pe.matmul(a_ps[:, 0:HIS], ones[:, :], counts[:, :], start=True, stop=True)
            pe.matmul(a_ps[:, HIS:2*HIS], upto[:, :], counts[:, :], start=True, stop=True).then_inc(pe_s, 1)
            pe.wait_ge(S["c2"], 1)
            pe.transpose(b_ps[:, 0:P], one_lo[:, :], ident[:, :]).then_inc(pe_s, 1)
            pe.wait_ge(S["c2"], 2)
            pe.matmul(b_ps[:, P:P+HIS], one_lo_t[:, :], pos[:, :], start=True, stop=True).then_inc(pe_s, 1)
            pe.wait_ge(S["c2"], 3)
            for i in range(3):
                last = pe.transpose(c_ps[0:CH, i*P:(i+1)*P], z[:, i, :], ident[:, :])
            last.then_inc(pe_s, 1)
            pe.wait_ge(S["c2"], 4)
            pe.transpose(c_ps[:, 384:384+CH], mm[:, 0:P], ident[0:CH, 0:CH])
            pe.transpose(c_ps[:, 448:448+CH], ss[:, 0:P], ident[0:CH, 0:CH]).then_inc(pe_s, 1)

        @block.scalar
        def _(act):
            act.wait_ge(S["act"], 1)
            act.activation(ee[:, :, :], dd[:, :, :], ACT.Exp).then_inc(S["act"], 1)
            act.wait_ge(S["act"], 3)
            act.activation(e2[:, :, :], d2[:, :, :], ACT.Exp).then_inc(S["act"], 1)

        @block.vector
        def _(v):
            n = [0]
            def go(i):
                n[0] += 1
                i.then_inc(dv, 1)
                v.wait_ge(dv, n[0])
            v.wait_ge(S["const"], 2)
            v.wait_ge(pe_s, 1)
            go(v.tensor_copy(total[:, :], a_ps[:, 0:HIS]))
            go(v.memset(one_hi[:, :], 1.0))
            go(v.tensor_tensor_scan(before[:, :], one_hi[:, :], total[:, :], 0.0, ALU.mult, ALU.add))
            go(v.tensor_tensor(before[:, :], before[:, :], total[:, :], ALU.subtract))
            go(v.scalar_tensor_tensor(out=pos[:, :], in0=a_ps[:, HIS:2*HIS], scalar=-1.0, in1=before[:, :], op0=ALU.add, op1=ALU.add))
            go(v.tensor_copy(pos_i[:, :], pos[:, :]))
            go(v.tensor_scalar(tok[:, :], first_seg[:, :], float(SHIFT), None, ALU.add))
            go(v.tensor_copy(tok_i[:, :], tok[:, :]))
            go(v.tensor_scalar(lo_i[:, :], tok_i[:, :], P - 1, None, ALU.bitwise_and))
            go(v.tensor_scalar(hi_i[:, :], tok_i[:, :], 7, None, ALU.logical_shift_right))
            go(v.tensor_copy(lo_f[:, :], lo_i[:, :]))
            go(v.tensor_copy(hi_f[:, :], hi_i[:, :]))
            go(v.tensor_scalar(one_lo[:, :], iota_f[:, 0:P], lo_f[:, :], None, ALU.is_equal))
            go(v.tensor_scalar(one_hi[:, :], iota_f[:, :], hi_f[:, :], None, ALU.is_equal))
            v.sem_inc(S["c2"], 1)
            v.wait_ge(pe_s, 2)
            go(v.tensor_copy(one_lo_t[:, :], b_ps[:, 0:P]))
            v.sem_inc(S["c2"], 1)
            v.wait_ge(pe_s, 3)
            go(v.tensor_tensor(picked[:, :], b_ps[:, P:P+HIS], one_hi[:, :], ALU.mult))
            go(v.reduce_sum(end[:, :], picked[:, :], axis=AX.X))
            go(v.tensor_copy(lane_end[:, :], lane_i[:, :]))
            go(v.tensor_tensor(skip[:, :], first_seg[:, :], prev_seg[:, :], ALU.not_equal))
            go(v.tensor_tensor(t1[:, :], end[:, :], lane_end[:, :], ALU.is_gt))
            go(v.tensor_tensor(skip[:, :], skip[:, :], t1[:, :], ALU.add))
            go(v.tensor_scalar(t2[:, :], tok[:, :], float(HALF), None, ALU.is_ge))
            go(v.tensor_tensor(skip[:, :], skip[:, :], t2[:, :], ALU.add))
            go(v.tensor_copy(at_i[:, :], end[:, :]))
            v.sem_inc(S["got"], 1)
            go(v.scalar_tensor_tensor(out=t1[:, :], in0=skip[:, :], scalar=float(ENTRIES), in1=end[:, :], op0=ALU.mult, op1=ALU.add))
            go(v.tensor_copy(to_i[:, :], t1[:, :]))
            five = lambda ap: ap.unsqueeze(2).broadcast_to([P, HEADS, EXPERTS])
            go(v.tensor_copy(z[:, 0, 0:16].rearrange("p (h x) -> p h x", x=EXPERTS), five(zlast[:, 20:24])))
            go(v.tensor_copy(z[:, 0, 16:20], zlast[:, 20:24]))
            go(v.tensor_copy(z[:, 1, :], zlast[:, 0:20]))
            go(v.tensor_tensor(t2[:, :], last_seg[:, :], prev_seg[:, :], ALU.not_equal))
            go(v.tensor_scalar(z[:, 2, :], z[:, 0, :], 0.0, t2[:, :], ALU.mult, ALU.add))
            go(v.tensor_scalar(z[:, 2, :], z[:, 2, :], -BIG, None, ALU.mult))
            v.sem_inc(S["c2"], 1)
            v.wait_ge(pe_s, 4)
            go(v.tensor_copy(zt[:, :, :], c_ps[0:CH, 0:3*P].rearrange("c (i p) -> c i p", p=P)))
            go(v.memset(mm[:, 0:1], -BIG))
            go(v.memset(ss[:, 0:1], 0.0))
            go(v.tensor_tensor_scan(mm[:, 1:P+1], zt[:, 2, :], zt[:, 0, :], mm[:, 0:1], ALU.add, ALU.max))
            go(v.tensor_tensor(dd[:, 0, :], mm[:, 0:P], zt[:, 2, :], ALU.add))
            go(v.tensor_tensor(dd[:, 0, :], dd[:, 0, :], mm[:, 1:P+1], ALU.subtract))
            go(v.tensor_tensor(dd[:, 1, :], zt[:, 0, :], mm[:, 1:P+1], ALU.subtract))
            v.sem_inc(S["act"], 1)
            v.wait_ge(S["act"], 2)
            go(v.tensor_tensor(ww[:, :], ee[:, 1, :], zt[:, 1, :], ALU.mult))
            go(v.tensor_tensor_scan(ss[:, 1:P+1], ee[:, 0, :], ww[:, :], ss[:, 0:1], ALU.mult, ALU.add))
            v.sem_inc(S["c2"], 1)
            v.wait_ge(pe_s, 5)
            go(v.tensor_copy(cin[:, 0, :], c_ps[:, 384:384+CH]))
            go(v.tensor_copy(cin[:, 1, :], c_ps[:, 448:448+CH]))
            v.wait_ge(S["put"], 16)
            go(v.tensor_copy(rm[:, 0:16].rearrange("p (h x) -> p h x", x=EXPERTS), five(row[:, 20:24])))
            go(v.tensor_copy(rm[:, 16:20], row[:, 20:24]))
            go(v.tensor_tensor(nm[:, :], rm[:, :], cin[:, 0, :], ALU.max))
            go(v.tensor_tensor(d2[:, 0, :], rm[:, :], nm[:, :], ALU.subtract))
            go(v.tensor_tensor(d2[:, 1, :], cin[:, 0, :], nm[:, :], ALU.subtract))
            v.sem_inc(S["act"], 1)
            v.wait_ge(S["act"], 4)
            go(v.tensor_tensor(new[:, 0:20], row[:, 0:20], e2[:, 0, :], ALU.mult))
            go(v.tensor_tensor(cin[:, 1, :], cin[:, 1, :], e2[:, 1, :], ALU.mult))
            go(v.tensor_tensor(new[:, 0:20], new[:, 0:20], cin[:, 1, :], ALU.add))
            go(v.tensor_copy(new[:, 20:24], nm[:, 16:20]))
            v.sem_inc(S["got"], 1)

            def indices(k, at, turn):
                if not isinstance(k, int) or k >= 2:
                    v.wait_ge(S["tg%d" % (at % 2)], 16 * PER * (at // 2) + 16 * PER * turn)
                v.tensor_copy(tidx[:, at % 2, :], pos_i[:, bass.ds(k * PER, PER)]).then_inc(S["idx"], 1)
            def body(k, at, turn):
                if not isinstance(k, int) or k < TURNS:
                    indices(k, at, turn)
                if not isinstance(k, int) or k >= 1:
                    j, q = k - 1, (at - 1) % 2
                    v.wait_ge(S["tg%d" % q], 16 * PER * ((at - 1) // 2 + 1) + 16 * PER * turn)
                    need(v, S["agg"], j)
                    v.tensor_scalar(tsum[:, q, :, :], trow[:, q, :, 16:20], 1e-16, None, ALU.add).then_inc(S["dn"], 1)
                    v.wait_ge(S["dn"], 2 * j + 1)
                    v.reciprocal(trec[:, q, :, :], tsum[:, q, :, :]).then_inc(S["dn"], 1)
                    v.wait_ge(S["dn"], 2 * j + 2)
                    v.tensor_tensor(agg[:, bass.ds(half * HIS + j * PER, PER), :].rearrange("p b (h x) -> p b h x", x=EXPERTS), trow[:, q, :, 0:16].rearrange("p b (h x) -> p b h x", x=EXPERTS),
                                    trec[:, q, :, :].unsqueeze(3).broadcast_to([P, PER, HEADS, EXPERTS]), ALU.mult).then_inc(S["agg"], 1)
            if not finish:
                rounds(v, 2, TURNS + 1, 1, 2, body)
    if finish:
        finish(pos_i)


class Gates:
    NAMES = "con dv moments eps"
    STEPS = 20 + 4 * (EXPERTS - 1) + 2 * PARTS - 1 + PARTS - 1
    def __init__(self, nc, ctx, io, S, name, width):
        def sb(n, shape, dt=F32): return ctx.enter_context(nc.sbuf_tensor(f"{name}_{n}", shape, dt))
        D = HEADS * EXPERTS
        self.D, self.width, self.S, self.io = D, width, S, io
        self.con = sb("con", [P, 3, D]); self.eps = sb("eps", [P, 1]); self.cen = sb("cen", [P, width, D]); self.sq = sb("sq", [P, width, D])
        self.mu, self.var, self.sd, self.rs, self.top = (sb(n, [P, width]) for n in ("mu", "var", "sd", "rs", "top"))
        self.sc, self.won, self.beats, self.ex, self.g = (sb(n, [P, width, EXPERTS]) for n in ("sc", "won", "beats", "ex", "g"))
    def sync(self, sp):
        for i, n in enumerate(("b_gat", "ln_gamma", "ln_beta")):
            sp.dma_start(self.con[:, i, :], self.io[n].rearrange("(a d) -> a d", a=1).broadcast_to([P, self.D])).then_inc(self.S["con"], 16)
    def gpsimd(self, pool):
        pool.memset(self.eps[:, :], 1e-5).then_inc(self.S["eps"], 1)
    def scalar(self, act, g):
        m = self.S["moments"]
        act.wait_ge(self.S["eps"], 1)
        act.wait_ge(m, 4 * g + 1)
        act.activation(self.sd[:, :], self.var[:, :], ACT.Sqrt, bias=self.eps[:, :], scale=1.0 / self.D).then_inc(m, 1)
        act.wait_ge(m, 4 * g + 3)
        act.activation(self.ex[:, :, :], self.ex[:, :, :], ACT.Exp).then_inc(m, 1)
    def vector(self, v, g, agg, parts):
        dv, m, width, D = self.S["dv"], self.S["moments"], self.width, self.D
        cen, sq, mu, var, sd, rs, top = (t[:, :] if len(t.shape) == 2 else t[:, :, :] for t in (self.cen, self.sq, self.mu, self.var, self.sd, self.rs, self.top))
        sc, won, beats, ex, gate = self.sc, self.won, self.beats, self.ex, self.g
        over = lambda ap, d: ap.unsqueeze(2).broadcast_to([P, width, d])
        row = lambda i: self.con[:, i, :].unsqueeze(1).broadcast_to([P, width, D])
        n = [0]
        def go(i):
            n[0] += 1
            i.then_inc(dv, 1)
            v.wait_ge(dv, self.STEPS * g + n[0])
        v.wait_ge(self.S["con"], 48)
        go(v.tensor_tensor(cen, agg, row(0), ALU.add))
        go(v.reduce_sum(mu, cen, axis=AX.X))
        go(v.tensor_scalar(mu, mu, 1.0 / D, None, ALU.mult))
        go(v.tensor_tensor(cen, cen, over(mu, D), ALU.subtract))
        go(v.tensor_tensor(sq, cen, cen, ALU.mult))
        go(v.reduce_sum(var, sq, axis=AX.X))
        v.sem_inc(m, 1)
        v.wait_ge(m, 4 * g + 2)
        go(v.reciprocal(rs, sd))
        go(v.tensor_tensor(cen, cen, over(rs, D), ALU.mult))
        go(v.tensor_tensor(cen, cen, row(1), ALU.mult))
        go(v.tensor_tensor(cen, cen, row(2), ALU.add))
        go(v.reduce_sum(sc[:, :, :], cen.rearrange("p b (h e) -> p b e h", e=EXPERTS), axis=AX.X))
        go(v.tensor_scalar(sc[:, :, :], sc[:, :, :], 1.0 / HEADS, None, ALU.mult))
        go(v.memset(won[:, :, :], 0.0))
        for d in range(1, EXPERTS):
            lo, hi = slice(0, EXPERTS - d), slice(d, EXPERTS)
            for mine, other, op in ((lo, hi, ALU.is_ge), (hi, lo, ALU.is_gt)):
                go(v.tensor_tensor(beats[:, :, mine], sc[:, :, mine], sc[:, :, other], op))
                go(v.tensor_tensor(won[:, :, mine], won[:, :, mine], beats[:, :, mine], ALU.add))
        go(v.tensor_scalar(won[:, :, :], won[:, :, :], 2.0, None, ALU.is_ge))
        go(v.tensor_reduce(top, sc[:, :, :], AX.X, ALU.max))
        go(v.tensor_tensor(ex[:, :, :], sc[:, :, :], over(top, EXPERTS), ALU.subtract))
        v.sem_inc(m, 1)
        v.wait_ge(m, 4 * g + 4)
        go(v.tensor_tensor(ex[:, :, :], ex[:, :, :], won[:, :, :], ALU.mult))
        go(v.reduce_sum(mu, ex[:, :, :], axis=AX.X))
        go(v.reciprocal(rs, mu))
        go(v.tensor_tensor(gate[:, :, :], ex[:, :, :], over(rs, EXPERTS), ALU.mult))
        split = parts.rearrange("p b (i j e) -> p b i j e", j=PARTS, e=EXPERTS)
        for j in range(PARTS):
            go(v.tensor_copy(split[:, :, 0, j, :], gate[:, :, :]))
            if j < PARTS - 1:
                go(v.tensor_tensor(gate[:, :, :], gate[:, :, :], split[:, :, 0, j, :], ALU.subtract))
        for i in range(1, PARTS):
            go(v.tensor_copy(split[:, :, i, :, :], split[:, :, 0, :, :]))
        assert n[0] == self.STEPS, n[0]

class Experts:
    WEIGHINGS = 4
    AHEAD = 2
    GATED, STEPS = EXPERTS * HID, 2 * EXPERTS * HID
    PREPARED = 25
    WEIGHTS = 16 * (4 + PARTS * PARTS)
    def __init__(self, nc, ctx, io, norm_d, mid_d, out_d, kept_d, agg, parts, name):
        self.agg = agg
        self.nc, self.io, self.norm_d, self.mid_d, self.out_d, self.kept_d, self.parts = nc, io, norm_d, mid_d, out_d, kept_d, parts
        def sb(n, shape, dt=F32): return ctx.enter_context(nc.sbuf_tensor(f"{name}_{n}", shape, dt))
        def ps(n, shape, dt=F32): return ctx.enter_context(nc.psum_tensor(f"{name}_{n}", shape, dt))
        self.S = ctx.enter_context(semaphores(nc, name, "w prep lane ident ld0 ld1 ld2 ld3 gst gtp gt w1 gel sel mul w2 fin go ycp st0 st1 st2 st3 kept0 kept1 " + Gates.NAMES))
        self.weights = Gates(nc, ctx, io, self.S, name, HIS // self.WEIGHINGS)
        self.w1 = sb("w1", [P, EXPERTS, HID * P]); self.w2 = sb("w2", [P, EXPERTS, HID, P]); self.b1 = sb("b1", [P, EXPERTS, HID])
        self.b2c = sb("b2c", [P, EXPERTS])
        self.b2f = sb("b2f", [G, P]); self.b2t = sb("b2t", [G, P]); self.b2p = sb("b2p", [G, PARTS, P], BF16); self.b2 = sb("b2", [G, P], BF16)
        self.mask = sb("mask", [G, 8])
        self.gates = GateRows(nc, sb, ps, self.S, parts)
        self.tn = sb("tn", [P, 4, TOK]); self.xm = sb("xm", [P, 4, TOK]); self.o = sb("o", [P, 4, TOK]); self.lower = sb("lower", [P, 4, TOK])
        self.kept = sb("kept", [P, 2, EXPERTS, TOK])
        self.hh = sb("hh", [P, 2, TOK]); self.hs = sb("hs", [P, 2, TOK])
        self.hid_ps = ps("hid_ps", [P, 2, TOK]); self.gate_ps = ps("gate_ps", [P, 2, TOK])
        self.out_ps = ps("out_ps", [P, TOK]); self.kept_ps = ps("kept_ps", [P, TOK])
    def ready(self, k, at, turn, unroll):
        return 48 * (at // 4 + 1) + 48 * (unroll // 4) * turn
    def start_sync(self, sp):
        S, io = self.S, self.io
        self.weights.sync(sp)
        sp.dma_start(self.w1[:, :, :], io["W1"].rearrange("e c h -> c e h")).then_inc(S["w"], 16)
        sp.dma_start(self.w2[:, :, :, :], io["W2"].rearrange("e (f h) c -> h e f c", h=P)).then_inc(S["w"], 16)
        with self.nc.allow_non_contiguous_dma("the biases, once, one to a partition"):
            sp.dma_start(self.b1[:, :, :], io["b1"].rearrange("e (f h) -> h e f", h=P)).then_inc(S["w"], 16)
            sp.dma_start(self.b2c[:, :], io["b2"].rearrange("e c -> c e")).then_inc(S["w"], 16)
        for r in range(PARTS * PARTS):
            sp.dma_start(self.b2f[r*EXPERTS:(r+1)*EXPERTS, :], io["b2"]).then_inc(S["w"], 16)
        for k in range(self.AHEAD + 1):
            self.load(sp, k, 0, 4, 0)
    def load(self, sp, at, turn, unroll, ahead):
        u = (at + ahead) % 4
        S = self.S
        sp.dma_start(self.tn[:, u, :], tile_of(self.norm_d, 1, at, turn, unroll, ahead)).then_inc(S["ld%d" % u], 16)
        sp.dma_start(self.xm[:, u, :], tile_of(self.mid_d, 1, at, turn, unroll, ahead)).then_inc(S["ld%d" % u], 16)
        sp.dma_start(self.lower[:, u, :], tile_of(self.norm_d, 0, at, turn, unroll, ahead)).then_inc(S["ld%d" % u], 16)
    def start_gpsimd(self, pool):
        self.weights.gpsimd(pool)
        self.gates.start_gpsimd(pool)
    def weigh_vector(self, v, part):
        cols = slice(part * HIS // self.WEIGHINGS, (part + 1) * HIS // self.WEIGHINGS)
        self.weights.vector(v, part, self.agg[:, cols, :], self.parts[:, cols, :])
    def weigh_scalar(self, act, part):
        self.weights.scalar(act, part)
    def start_vector(self, v):
        S = self.S
        n = [0]
        def go(i):
            n[0] += 1
            i.then_inc(S["prep"], 1)
            v.wait_ge(S["prep"], n[0])
        v.wait_ge(S["w"], self.WEIGHTS)
        m = self.mask
        self.gates.start_vector(v, go, m)
        for i in range(PARTS):
            go(v.tensor_copy(self.b2p[:, i, :], self.b2f[:, :]))
            go(v.tensor_tensor(self.b2f[:, :], self.b2f[:, :], self.b2p[:, i, :], ALU.subtract))
        go(v.tensor_scalar(self.b2t[:, :], self.b2p[:, 0, :], m[:, 0:1], None, ALU.mult))
        for i in (1, 2):
            go(v.scalar_tensor_tensor(out=self.b2t[:, :], in0=self.b2p[:, i, :], scalar=m[:, i:i+1], in1=self.b2t[:, :], op0=ALU.mult, op1=ALU.add))
        go(v.tensor_copy(self.b2[:, :], self.b2t[:, :]))
        assert n[0] == self.PREPARED
        self.stage(v, 0, 0)
        self.turned(v, 0, 0)
    def stage(self, v, k, at):
        need(v, self.S["gtp"], k - 1)
        v.tensor_copy(self.gates.staged[:, at % 2, :, :], self.parts[:, bass.ds(k * BLKS, BLKS), :]).then_inc(self.S["gst"], 1)
    def turned(self, v, k, at):
        v.wait_ge(self.S["gtp"], k + 1)
        need(v, self.S["w2"], self.STEPS * (k - 1))
        v.tensor_copy(self.gates.turned[:, at % 2, :], self.gates.turned_ps[0:G, 0:TOK]).then_inc(self.S["gt"], 1)
    def turn_gates(self, pe, k, at):
        need(pe, self.S["gst"], k + 1)
        need(pe, self.S["gt"], k)
        if not isinstance(k, int):
            pe.sem_inc(self.S["go"], 1)
        self.gates.turn(pe, self.gates.turned_ps, at).then_inc(self.S["gtp"], 1)
    def first_product(self, pe, k, at, s):
        S = self.S
        need(pe, S["gel"], self.STEPS * k + s - 1)
        e, f = s % self.GATED // HID, s % HID
        tokens = self.tn if s < self.GATED else self.lower
        pe.matmul(self.hid_ps[:, s % 2, :], self.w1[:, e, f*P:(f+1)*P], tokens[:, at % 4, :], start=True, stop=True).then_inc(S["w1"], 1)
    def choose_gate(self, pe, k, at, e):
        S = self.S
        need(pe, S["gt"], k + 1)
        need(pe, S["mul"], 8 * k + 2 * e - 2)
        pe.matmul(self.gate_ps[:, e % 2, :], self.gates.choose[:, e, :], self.gates.turned[:, at % 2, :], start=True, stop=True).then_inc(S["sel"], 1)
    def start_tensor(self, pe):
        S = self.S
        pe.wait_ge(S["ident"], 1)
        pe.wait_ge(S["w"], self.WEIGHTS)
        self.turn_gates(pe, 0, 0)
        pe.wait_ge(S["ld0"], 48)
        for s in range(2):
            self.first_product(pe, 0, 0, s)
        pe.wait_ge(S["prep"], self.PREPARED)
        self.choose_gate(pe, 0, 0, 0)
    def sync(self, sp, k, at, turn, unroll):
        S = self.S
        if not isinstance(k, int) or k >= 1:
            q = (at - 1) % 4
            need(sp, S["fin"], k)
            sp.dma_start(tile_of(self.out_d, 1, at, turn, unroll, -1), self.o[:, q, :]).then_inc(S["st%d" % q], 16)
            if not isinstance(k, int) or k + self.AHEAD < TOKEN_TILES:
                self.load(sp, at, turn, unroll, self.AHEAD)
            u = (at - 1) % 2
            need(sp, S["ycp"], EXPERTS * k)
            sp.dma_start(self.kept_d[k - 1], self.kept[:, u, :, :]).then_inc(S["kept%d" % u], 16)
    def end_sync(self, sp):
        for q in range(4):
            sp.wait_ge(self.S["st%d" % q], 16 * TOKEN_TILES // 4)
        for u in range(2):
            sp.wait_ge(self.S["kept%d" % u], 16 * TOKEN_TILES // 2)
    def tensor(self, pe, k, at, turn, unroll, beside):
        S = self.S
        if isinstance(k, int) and k >= TOKEN_TILES:
            return
        more = not isinstance(k, int) or k + 1 < TOKEN_TILES
        need(pe, S["fin"], k)
        pe.matmul(self.out_ps[:, :], self.b2[:, :], self.gates.turned[:, at % 2, :], start=True, stop=False)
        for s in range(self.STEPS):
            e, f = s % self.GATED // HID, s % HID
            if s < self.GATED:
                need(pe, S["mul"], self.GATED * k + s + 1)
                pe.matmul(self.out_ps[:, :], self.w2[:, e, f, :], self.hs[:, s % 2, :], start=False, stop=(s == self.GATED - 1)).then_inc(S["w2"], 1)
            else:
                if f == 0:
                    need(pe, S["ycp"], EXPERTS * k + e)
                need(pe, S["gel"], self.STEPS * k + s + 1)
                pe.matmul(self.kept_ps[:, :], self.w2[:, e, f, :], self.hh[:, s % 2, :], start=(f == 0), stop=(f == HID - 1)).then_inc(S["w2"], 1)
            if s + 2 < self.STEPS:
                self.first_product(pe, k, at, s + 2)
            elif more:
                if s == self.STEPS - 2:
                    pe.wait_ge(S["ld%d" % ((at + 1) % 4)], self.ready(k + 1, at + 1, turn, unroll))
                self.first_product(pe, k + 1, at + 1, s + 2 - self.STEPS)
            if s % 2 == 0 and s < 6:
                self.choose_gate(pe, k, at, s // 2 + 1)
            if s == 3 and more:
                self.turn_gates(pe, k + 1, at + 1)
            if s == 7 and more:
                self.choose_gate(pe, k + 1, at + 1, 0)
            if s < self.GATED:
                beside(s)
    def scalar(self, act, k, at, turn, unroll):
        S = self.S
        if isinstance(k, int) and k >= TOKEN_TILES:
            return
        def keep_output(e):
            need(act, S["w2"], self.STEPS * k + self.GATED + HID * (e + 1))
            if e == 0:
                need(act, S["kept%d" % (at % 2)], 16 * (at // 2) + 16 * (unroll // 2) * turn)
            act.activation(self.kept[:, at % 2, e, :], self.kept_ps[:, :], ACT.Identity, bias=self.b2c[:, e:e+1]).then_inc(S["ycp"], 1)
        for s in range(self.STEPS):
            need(act, S["w1"], self.STEPS * k + s + 1)
            if 2 <= s < self.GATED + 2:
                need(act, S["mul"], self.GATED * k + s - 1)
            else:
                need(act, S["w2"], self.STEPS * k + s - 1)
            act.activation(self.hh[:, s % 2, :], self.hid_ps[:, s % 2, :], ACT.Gelu, bias=self.b1[:, s % self.GATED // HID, s % HID:s % HID + 1]).then_inc(S["gel"], 1)
            if s >= self.GATED + 3 and s % HID == 1:
                keep_output((s - self.GATED - 3) // HID)
        keep_output(EXPERTS - 1)
    def vector(self, v, k, at, turn, unroll, beside):
        S = self.S
        tile = not isinstance(k, int) or k < TOKEN_TILES
        more = not isinstance(k, int) or k + 1 < TOKEN_TILES
        if not isinstance(k, int) or k >= 1:
            q = (at - 1) % 4
            need(v, S["w2"], self.STEPS * (k - 1) + self.GATED)
            need(v, S["ld%d" % q], self.ready(k - 1, at - 1, turn, unroll))
            need(v, S["st%d" % q], 16 * ((at - 1) // 4) + 16 * (unroll // 4) * turn)
            v.tensor_tensor(self.o[:, q, :], self.xm[:, q, :], self.out_ps[:, :], ALU.add).then_inc(S["fin"], 1)
        for s in range(self.GATED):
            if tile:
                need(v, S["gel"], self.STEPS * k + s + 1)
                need(v, S["sel"], EXPERTS * k + s // HID + 1)
                need(v, S["w2"], self.STEPS * k + s - 1 if s >= 2 else self.STEPS * (k - 1) + self.GATED - 1 + s)
                v.tensor_tensor(self.hs[:, s % 2, :], self.hh[:, s % 2, :], self.gate_ps[:, (s // HID) % 2, :], ALU.mult).then_inc(S["mul"], 1)
            if s == 2 and more:
                self.stage(v, k + 1, at + 1)
            if s == 5 and more:
                self.turned(v, k + 1, at + 1)
            if tile:
                beside(s)

def tile_of(d, half, at, turn, unroll, ahead=0):
    n = at + ahead
    img = half * (TOKEN_TILES // 2) + n // 2 + turn * (unroll // 2)
    return d[img, :, (n % 2) * TOK:(n % 2 + 1) * TOK]

class GateRows:
    def __init__(self, nc, sb, ps, S, parts):
        self.S, self.parts = S, parts
        self.lane_i = sb("lane_i", [G, 1], I32); self.lane = sb("lane", [G, 2], I32); self.lf = sb("lf", [G, 2])
        self.choose = sb("choose", [G, EXPERTS, P], BF16); self.onesb = sb("onesb", [G, P], BF16); self.ident = sb("ident", [P, P], BF16)
        self.staged = sb("staged", [P, 2, BLKS, G], BF16); self.turned = sb("turned", [G, 2, TOK], BF16)
        self.turned_ps = ps("turned_ps", [P, 2 * TOK], BF16)
    def start_gpsimd(self, pool):
        S = self.S
        pool.iota(self.lane_i[:, :], [[0, 1]], base=0, channel_multiplier=1)
        pool.memset(self.onesb[:, :], 1.0)
        pool.memset(self.ident[:, :], 0.0).then_inc(S["lane"], 1)
        pool.wait_ge(S["lane"], 1)
        pool.affine_select(out=self.ident[:, :], in_=self.ident[:, :], compare_op=ALU.not_equal, fill=1.0, base=0, pattern=[[-1, P]], channel_multiplier=1).then_inc(S["ident"], 1)
    def start_vector(self, v, go, m):
        v.wait_ge(self.S["lane"], 1)
        GE = PARTS * EXPERTS
        go(v.tensor_copy(self.lf[:, 0:1], self.lane_i[:, :]))
        go(v.tensor_scalar(self.lane[:, 0:1], self.lane_i[:, :], EXPERTS - 1, None, ALU.bitwise_and))
        go(v.tensor_copy(self.lf[:, 1:2], self.lane[:, 0:1]))
        go(v.tensor_scalar(m[:, 0:1], self.lf[:, 0:1], float(GE), None, ALU.is_lt))
        go(v.tensor_scalar(m[:, 2:3], self.lf[:, 0:1], float(2 * GE), None, ALU.is_ge))
        go(v.tensor_scalar(m[:, 1:2], m[:, 0:1], -1.0, 1.0, ALU.mult, ALU.add))
        go(v.tensor_tensor(m[:, 1:2], m[:, 1:2], m[:, 2:3], ALU.subtract))
        for e in range(EXPERTS):
            go(v.tensor_scalar(m[:, 4+e:5+e], self.lf[:, 1:2], float(e), m[:, 0:1], ALU.is_equal, ALU.mult))
            go(v.tensor_scalar(self.choose[:, e, :], self.onesb[:, :], m[:, 4+e:5+e], None, ALU.mult))
    def turn(self, pe, out_ps, at):
        for b in range(BLKS):
            last = pe.transpose(out_ps[0:G, b*P:(b+1)*P], self.staged[:, at % 2, b, :], self.ident[:, :])
        return last

def finish_lower(nc, io, mid_d, out_d, kept_d, res_d, agg, parts, pos_i, gathers):
    PER, TURNS, GROUP = 2 * BLKS, HIS // (2 * BLKS), 8
    with ExitStack() as ctx:
        def sb(n, shape, dt=F32): return ctx.enter_context(nc.sbuf_tensor(f"c_{n}", shape, dt))
        def ps(n, shape, dt=F32): return ctx.enter_context(nc.psum_tensor(f"c_{n}", shape, dt))
        S = dict(ctx.enter_context(semaphores(nc, "c", "prep lane ident ld0 ld1 ld2 ld3 gst gtp gt sel mul sum fin go st0 st1 st2 st3 idx agg dn free gated " + Gates.NAMES)))
        S.update({n: gathers(f"c_{n}") for n in ("tg0", "tg1")})
        weights = Gates(nc, ctx, io, S, "c", PER * GROUP)
        rows = GateRows(nc, sb, ps, S, parts)
        mask = sb("mask", [G, 8])
        tidx = sb("tidx", [P, 2, PER], I32); trow = sb("trow", [P, 2, PER, ROW]); tsum = sb("tsum", [P, PER, HEADS]); trec = sb("trec", [P, PER, HEADS])
        kept = sb("kept", [P, 4, EXPERTS, TOK]); xm = sb("xm", [P, 4, TOK]); o = sb("o", [P, 4, TOK])
        weighed = sb("weighed", [P, 2, EXPERTS, TOK]); pairs = sb("pairs", [P, 2, TOK]); total = sb("total", [P, TOK])
        gate_ps = ps("gate_ps", [P, EXPERTS, TOK])
        def gathered(k): return not isinstance(k, int) or k < TURNS
        def turns(eng, group, body):
            first = GROUP * group
            peeled = (GROUP, 2, 0, 0, 0)[group] if group < 4 else 0
            for k in range(first, first + peeled):
                body(k, k % 2, k // 2)
            if peeled < GROUP:
                with eng.Fori(0, (GROUP - peeled) // 2) as turn:
                    for at in range(2):
                        body(first + peeled + at + turn * 2, at, (first + peeled) // 2 + turn)
        def tiles(k, at):
            return [(k * 2 - 2 * GROUP + j, 2 * at + j, j) for j in range(2)]
        GROUPS = TURNS // GROUP
        with nc.Block() as block:
            @block.sync
            def _(sp):
                weights.sync(sp)
                def load(tile, image, u, j):
                    sp.dma_start(kept[:, u, :, :], kept_d[tile]).then_inc(S["ld%d" % u], 16)
                    sp.dma_start(xm[:, u, :], mid_d[image, :, j*TOK:(j+1)*TOK]).then_inc(S["ld%d" % u], 16)
                for n in range(4):
                    load(n, n // 2, n, n % 2)
                def body(k, at, pair):
                    for t, u, j in tiles(k, at):
                        need(sp, S["fin"], t + 1)
                        sp.dma_start(out_d[k - GROUP, :, j*TOK:(j+1)*TOK], o[:, u, :]).then_inc(S["st%d" % u], 16)
                        load(t + 4, k - GROUP + 2, u, j)
                def last(k, at, pair):
                    for t, u, j in tiles(k, at):
                        need(sp, S["fin"], t + 1)
                        sp.dma_start(out_d[k - GROUP, :, j*TOK:(j+1)*TOK], o[:, u, :]).then_inc(S["st%d" % u], 16)
                for group in range(1, GROUPS + 1):
                    if group < GROUPS:
                        turns(sp, group, body)
                    else:
                        first = GROUP * group
                        with sp.Fori(0, GROUP // 2 - 1) as turn:
                            for at in range(2):
                                body(first + at + turn * 2, at, first // 2 + turn)
                        for at in range(2):
                            last(first + GROUP - 2 + at, at, 0)
                for u in range(4):
                    sp.wait_ge(S["st%d" % u], 16 * TOKEN_TILES // 4)
            @block.gpsimd
            def _(pool):
                weights.gpsimd(pool)
                rows.start_gpsimd(pool)
                def body(k, at, pair):
                    need(pool, S["idx"], k + 1)
                    need(pool, S["agg"], k - 1)
                    pool.sem_inc(S["free"], 1)
                    for c in range(PER):
                        pool.indirect_dma_start(trow[:, at, c, :], None, res_d,
                            bass.IndirectOffsetOnAxis(ap=tidx[:, at, c:c+1], axis=0)).then_inc(S["tg%d" % at], 16)
                for group in range(GROUPS):
                    turns(pool, group, body)
            @block.tensor
            def _(pe):
                pe.wait_ge(S["ident"], 1)
                pe.wait_ge(S["prep"], 15)
                def body(k, at, pair):
                    for t, u, j in tiles(k, at):
                        need(pe, S["gst"], t + 1)
                        need(pe, S["gt"], t)
                        pe.sem_inc(S["go"], 1)
                        rows.turn(pe, rows.turned_ps, j).then_inc(S["gtp"], 1)
                        need(pe, S["gt"], t + 1)
                        for e in range(EXPERTS):
                            need(pe, S["mul"], (t - 1) * EXPERTS + e + 1)
                            pe.matmul(gate_ps[:, e, :], rows.choose[:, e, :], rows.turned[:, j, :], start=True, stop=True).then_inc(S["sel"], 1)
                for group in range(1, GROUPS + 1):
                    turns(pe, group, body)
            @block.scalar
            def _(act):
                def body(k, at, pair):
                    for t, u, j in tiles(k, at):
                        need(act, S["gtp"], t - 1)
                        act.activation(rows.staged[:, j, :, :], parts[:, bass.ds(t * BLKS, BLKS), :], ACT.Identity).then_inc(S["gst"], 1)
                        need(act, S["gtp"], t + 1)
                        need(act, S["sel"], (t - 1) * EXPERTS)
                        act.activation(rows.turned[:, j, :], rows.turned_ps[0:G, 0:TOK], ACT.Identity).then_inc(S["gt"], 1)
                for group in range(GROUPS + 1):
                    if group:
                        act.wait_ge(S["gated"], group)
                        turns(act, group, body)
                    if group < GROUPS:
                        weights.scalar(act, group)
            @block.vector
            def _(v):
                n = [0]
                def go(i):
                    n[0] += 1
                    i.then_inc(S["prep"], 1)
                    v.wait_ge(S["prep"], n[0])
                rows.start_vector(v, go, mask)
                assert n[0] == 15
                v.tensor_copy(tidx[:, 0, :], pos_i[:, 0:PER]).then_inc(S["idx"], 1)
                def body(k, at, pair):
                    if not isinstance(k, int) or k + 1 < TURNS:
                        if not isinstance(k, int) or k >= 1:
                            v.wait_ge(S["tg%d" % (1 - at)], 16 * PER * (pair + at))
                        v.tensor_copy(tidx[:, 1 - at, :], pos_i[:, bass.ds((k + 1) * PER, PER)]).then_inc(S["idx"], 1)
                    if not isinstance(k, int) or k >= GROUP:
                        weigh(k, at, pair)
                    v.wait_ge(S["tg%d" % at], 16 * PER * (pair + 1))
                    need(v, S["agg"], k)
                    v.tensor_scalar(tsum[:, :, :], trow[:, at, :, 16:20], 1e-16, None, ALU.add).then_inc(S["dn"], 1)
                    v.wait_ge(S["dn"], 2 * k + 1)
                    v.reciprocal(trec[:, :, :], tsum[:, :, :]).then_inc(S["dn"], 1)
                    v.wait_ge(S["dn"], 2 * k + 2)
                    v.tensor_tensor(agg[:, bass.ds(k * PER, PER), :].rearrange("p b (h x) -> p b h x", x=EXPERTS),
                                    trow[:, at, :, 0:16].rearrange("p b (h x) -> p b h x", x=EXPERTS),
                                    trec[:, :, :].unsqueeze(3).broadcast_to([P, PER, HEADS, EXPERTS]), ALU.mult).then_inc(S["agg"], 1)
                def weigh(k, at, pair):
                    for t, u, j in tiles(k, at):
                        v.wait_ge(S["ld%d" % u], 32 * (pair - GROUP // 2 + 1))
                        need(v, S["sum"], 3 * (t - 1))
                        for e in range(EXPERTS):
                            need(v, S["sel"], t * EXPERTS + e + 1)
                            v.tensor_tensor(weighed[:, j, e, :], kept[:, u, e, :], gate_ps[:, e, :], ALU.mult).then_inc(S["mul"], 1)
                        need(v, S["mul"], t * EXPERTS + EXPERTS)
                        need(v, S["fin"], t)
                        v.tensor_tensor(pairs[:, 0:2, :], weighed[:, j, 0:2, :], weighed[:, j, 2:4, :], ALU.add).then_inc(S["sum"], 1)
                        need(v, S["sum"], 3 * t + 1)
                        v.tensor_tensor(total[:, :], pairs[:, 0, :], pairs[:, 1, :], ALU.add).then_inc(S["sum"], 2)
                        need(v, S["sum"], 3 * t + 3)
                        need(v, S["st%d" % u], 16 * (pair - GROUP // 2))
                        v.tensor_tensor(o[:, u, :], total[:, :], xm[:, u, :], ALU.add).then_inc(S["fin"], 1)
                for group in range(GROUPS + 1):
                    if group < GROUPS:
                        if group < GROUPS - 1:
                            turns(v, group, body)
                        else:
                            first = GROUP * group
                            with v.Fori(0, GROUP // 2 - 1) as turn:
                                for at in range(2):
                                    body(first + at + turn * 2, at, first // 2 + turn)
                            for k in (first + GROUP - 2, first + GROUP - 1):
                                body(k, k % 2, k // 2)
                        v.wait_ge(S["agg"], GROUP * (group + 1))
                        cols = slice(PER * GROUP * group, PER * GROUP * (group + 1))
                        weights.vector(v, group, agg[:, cols, :], parts[:, cols, :])
                        v.sem_inc(S["gated"], 1)
                    else:
                        turns(v, group, weigh)


def program(nc, io, out):
    IMAGES, C, H, W = io["x"].shape
    M = IMAGES * H * W
    keys = [nc.dram_tensor(f"keys{h}", [1 + ENTRIES + TAIL], F32, kind="Internal").ap() for h in range(2)]
    rows = nc.dram_tensor("rows", [M, ROW], F32, kind="Internal").ap()
    res = [nc.dram_tensor(f"sums{h}", [ENTRIES, ROW], F32, kind="Internal").ap() for h in range(2)]
    mid = nc.dram_tensor("mid", [IMAGES, C, H * W], F32, kind="Internal").ap()
    norm = nc.dram_tensor("norm", [IMAGES, C, H * W], F32, kind="Internal").ap()
    kept = nc.dram_tensor("kept", [TOKEN_TILES, P, EXPERTS, TOK], F32, kind="Internal").ap()
    out_d = out.rearrange("b c h w -> b c (h w)")
    edges = io["edge_index"]
    with ExitStack() as ctx:
        agg = ctx.enter_context(nc.sbuf_tensor("agg", [P, M // P, 16], F32))
        gathers = lambda name: ctx.enter_context(nc.semaphore(name))
        flag = ctx.enter_context(nc.sbuf_tensor("flag", [1, 1], I32))
        sorter(nc, edges, keys[0], 0, flag[:, :])
        mixer(nc, io, dict(xmid=mid, norm=norm, rows=rows.rearrange("(b j p) r -> b p j r", j=H*W//P, p=P), agg=agg[:, :, :], ROW=ROW))
        high = nc.values_load(flag[0:1, 0:1], min_val=0, max_val=1)
        with nc.If(high):
            sorter(nc, edges, keys[1], 1, None)
            attention(nc, edges, keys[1], rows, res[1], agg[:, :, :], 1, gathers)
        with ExitStack() as c1:
            parts = c1.enter_context(nc.sbuf_tensor("parts", [P, HIS, G], BF16))
            attention(nc, edges, keys[0], rows, res[0], agg[:, :, :], 0, gathers,
                      lambda c: Experts(nc, c, io, norm, mid, out_d, kept, agg[:, HIS:2*HIS, :], parts[:, :, :], "ex"),
                      lambda places: finish_lower(nc, io, mid, out_d, kept, res[0], agg[:, :, :], parts[:, :, :], places, gathers))


_INS = ['x', 'L0_conv_w1', 'L0_conv_w2', 'L0_conv_b11', 'L0_conv_b12', 'L0_conv_b13', 'L0_conv_b21', 'L0_conv_b22', 'L0_conv_b23',
        'L0_conv_a1', 'L0_conv_a2', 'L0_conv_g1m', 'L0_conv_be1m', 'L0_conv_m1m', 'L0_conv_v1m', 'L0_conv_g2m', 'L0_conv_be2m',
        'L0_conv_m2m', 'L0_conv_v2m', 'L0_ffn_W_gat', 'L0_ffn_att_src', 'L0_ffn_att_dst', 'L0_ffn_b_gat', 'L0_ffn_ln_gamma',
        'L0_ffn_ln_beta', 'L0_ffn_W1', 'L0_ffn_b1', 'L0_ffn_W2', 'L0_ffn_b2', 'L0_ffn_edge_index']


def kernel(**inputs):
    import numpy as _np
    import concourse.bacc as _bacc
    from concourse import mybir as _mybir
    from concourse.bass_utils import run_bass_kernel_spmd as _run

    nc = _bacc.Bacc("TRN2", target_bir_lowering=False, num_devices=1)
    arrays, io = {}, {}
    for name in _INS:
        a = _np.ascontiguousarray(inputs[name])
        arrays[f"in_{name}_dram"] = a
        short = name.replace("L0_conv_", "").replace("L0_ffn_", "")
        io[short] = nc.dram_tensor(f"in_{name}_dram", a.shape, _mybir.dt.from_np(a.dtype), kind="ExternalInput").ap()
    shape = inputs["x"].shape
    out = nc.dram_tensor("out_0_dram", shape, _mybir.dt.float32, kind="ExternalOutput").ap()
    program(nc, io, out)
    r = _run(nc, [arrays], core_ids=[0])
    return r.results[0]["out_0_dram"]
```
